# Optimizing a Trainium2 kernel written in Bass

```python
import numpy as np
import jax
import jax.numpy as jnp

def _softmax(x, axis=-1):
    return jax.nn.softmax(x, axis=axis)

def _gelu(x):
    return jax.nn.gelu(x, approximate=True)

def _silu(x):
    return jax.nn.silu(x)

def _sigmoid(x):
    return jax.nn.sigmoid(x)

def _layernorm(x, axis=-1, eps=1e-05):
    m = jnp.mean(x, axis=axis, keepdims=True)
    v = jnp.var(x, axis=axis, keepdims=True)
    return (x - m) / jnp.sqrt(v + eps)

def _scatter_add(tgt, idx, src, axis=0):
    return tgt.at[idx].add(src)

def _segment_sum(src, seg, n):
    return jax.ops.segment_sum(src, seg, n)
kernel_name = 'mk_lm_tower_d2_tok_ids768_r4_ebcade'

def setup_inputs(seed: int=0):
    np.random.seed(seed)
    _w = jnp.asarray

    def _rec_inputs():
        import jax
        import jax.numpy as jnp
        _rk = jax.random.key(seed)
        x = jax.random.randint(jax.random.fold_in(_rk, 1), (8, 512), 0, 31983, jnp.int32)
        return x
    x = _rec_inputs()

    def _L0_tok_setup():
        import jax, jax.numpy as jnp
        import numpy as np
        NUM_EMBEDDINGS = 8000
        EMBED_DIM = 192
        BATCH, POS = (2, 512)
        INIT_RANGE = 0.02
        key = jax.random.key(seed)
        kx, kw = jax.random.split(key)
        x = jax.random.randint(kx, (BATCH, POS), 0, NUM_EMBEDDINGS, dtype=jnp.int64 if jax.config.jax_enable_x64 else jnp.int32)
        W = jax.random.normal(kw, (NUM_EMBEDDINGS, EMBED_DIM), dtype=jnp.float32) * INIT_RANGE
        return {'x': x, 'W': W}
    _L0_tok_all = _L0_tok_setup()
    _L0_tok_in = {k: v for k, v in _L0_tok_all.items() if k in ('W',)}
    del _L0_tok_all

    def _L0_attn_setup():
        import jax, jax.numpy as jnp
        import numpy as np
        import math
        N_LAYER, N_EMBD, LAYER_ID = (12, 192, 0)
        B, T, C = (32, 256, N_EMBD)

        def _init_params():
            r01 = LAYER_ID / (N_LAYER - 1)
            r1a0 = 1.0 - LAYER_ID / N_LAYER
            h = np.arange(C, dtype=np.float32)
            time_decay = (-5.0 + 8.0 * (h / (C - 1)) ** (0.7 + 1.3 * r01)).astype(np.float32)
            zigzag = np.array([(i + 1) % 3 - 1 for i in range(C)], dtype=np.float32) * 0.5
            time_first = (np.ones(C, dtype=np.float32) * math.log(0.3) + zigzag).astype(np.float32)
            xlin = (np.arange(C, dtype=np.float32) / C).reshape(1, 1, C)
            time_mix_k = np.power(xlin, r1a0).astype(np.float32)
            time_mix_v = (np.power(xlin, r1a0) + 0.3 * r01).astype(np.float32)
            time_mix_r = np.power(xlin, 0.5 * r1a0).astype(np.float32)
            return (time_decay, time_first, time_mix_k, time_mix_v, time_mix_r)

        def _wkv(w, u, k, v):

            def step(carry, kv):
                p, q, o = carry
                kt, vt = kv
                no = jnp.maximum(o, u + kt)
                A = jnp.exp(o - no)
                Bc = jnp.exp(u + kt - no)
                y = (A * p + Bc * vt) / (A * q + Bc)
                no2 = jnp.maximum(w + o, kt)
                A2 = jnp.exp(w + o - no2)
                B2 = jnp.exp(kt - no2)
                return ((A2 * p + B2 * vt, A2 * q + B2, no2), y)
            b = k.shape[0]
            init = (jnp.zeros((b, C), jnp.float32), jnp.zeros((b, C), jnp.float32), jnp.full((b, C), -1e+38, jnp.float32))
            kT = jnp.swapaxes(k, 0, 1)
            vT = jnp.swapaxes(v, 0, 1)
            _, ys = jax.lax.scan(step, init, (kT, vT))
            return jnp.swapaxes(ys, 0, 1)
        key = jax.random.key(seed)
        ks = jax.random.split(key, 5)
        td, tf, tmk, tmv, tmr = _init_params()
        scale = 0.02
        return {'x': jax.random.normal(ks[0], (B, T, C), dtype=jnp.float32), 'time_decay': jnp.asarray(td), 'time_first': jnp.asarray(tf), 'time_mix_k': jnp.asarray(tmk), 'time_mix_v': jnp.asarray(tmv), 'time_mix_r': jnp.asarray(tmr), 'Wk': jax.random.normal(ks[1], (C, C), dtype=jnp.float32) * scale, 'Wv': jax.random.normal(ks[2], (C, C), dtype=jnp.float32) * scale, 'Wr': jax.random.normal(ks[3], (C, C), dtype=jnp.float32) * scale, 'Wo': jax.random.normal(ks[4], (C, C), dtype=jnp.float32) * scale}
    _L0_attn_all = _L0_attn_setup()
    _L0_attn_in = {k: v for k, v in _L0_attn_all.items() if k in ('time_decay', 'time_first', 'time_mix_k', 'time_mix_v', 'time_mix_r', 'Wk', 'Wv', 'Wr', 'Wo')}
    del _L0_attn_all

    def _L0_ffn_setup():
        import jax, jax.numpy as jnp
        import numpy as np
        DIM = 192
        NUM_EXPERTS = 4
        NUM_HEADS = 12
        HEAD_DIM = DIM // NUM_HEADS
        MLP_HID = 4 * DIM
        FC1_OUT = MLP_HID + 3 * DIM
        FC2_IN = MLP_HID + DIM
        FC2_OUT = 2 * DIM
        CAP_FACTOR = 0.5
        LN_EPS = 1e-06
        key = jax.random.key(seed)
        ks = jax.random.split(key, 4)
        B, N = (8, 256)
        return {'x': jax.random.normal(ks[0], (B, N, DIM), jnp.float32), 'w_router': jax.random.normal(ks[1], (NUM_EXPERTS, DIM), jnp.float32) * 0.02, 'gamma1': jnp.ones((DIM,), jnp.float32), 'beta1': jnp.zeros((DIM,), jnp.float32), 'w1': jax.random.normal(ks[2], (FC1_OUT, DIM), jnp.float32) * 0.02, 'b1': jnp.zeros((FC1_OUT,), jnp.float32), 'w2': jax.random.normal(ks[3], (FC2_OUT, FC2_IN), jnp.float32) * 0.02, 'b2': jnp.zeros((FC2_OUT,), jnp.float32)}
    _L0_ffn_all = _L0_ffn_setup()
    _L0_ffn_in = {k: v for k, v in _L0_ffn_all.items() if k in ('w_router', 'gamma1', 'beta1', 'w1', 'b1', 'w2', 'b2')}
    del _L0_ffn_all

    def _L1_attn_setup():
        import jax, jax.numpy as jnp
        import numpy as np
        B_SZ, SEQ = (1, 512)
        D_MODEL, D_STATE, D_CONV, EXPAND = (192, 64, 4, 2)
        D_INNER = EXPAND * D_MODEL
        HEADDIM = 64
        NHEADS = D_INNER // HEADDIM
        CONV_DIM = D_INNER + 2 * D_STATE
        D_IN_PROJ = 2 * D_INNER + 2 * D_STATE + NHEADS
        HIDDEN = (D_MODEL * EXPAND + 127) // 128 * 128
        EPS = 1e-05

        def _ln(x, w, b):
            m = x.mean(-1, keepdims=True)
            v = ((x - m) ** 2).mean(-1, keepdims=True)
            return (x - m) * jax.lax.rsqrt(v + EPS) * w + b

        def _block(x, ln1_w, ln1_b, ln2_w, ln2_b, in_proj_w, conv_w, conv_b, dt_bias, A_log, D_skip, ssm_norm_w, out_proj_w, fc1_w, fc2_w):
            Bb, L, _ = x.shape
            h = _ln(x, ln1_w, ln1_b)
            zxbcdt = jnp.einsum('bld,pd->blp', h, in_proj_w)
            z = zxbcdt[..., :D_INNER]
            xBC = zxbcdt[..., D_INNER:D_INNER + CONV_DIM]
            dt = zxbcdt[..., D_INNER + CONV_DIM:]
            xp = jnp.pad(xBC, ((0, 0), (D_CONV - 1, 0), (0, 0)))
            xBC = sum((xp[:, k:k + L, :] * conv_w[:, k] for k in range(D_CONV))) + conv_b
            xBC = jax.nn.silu(xBC)
            xs = xBC[..., :D_INNER].reshape(Bb, L, NHEADS, HEADDIM)
            Bm = xBC[..., D_INNER:D_INNER + D_STATE]
            Cm = xBC[..., D_INNER + D_STATE:]
            dt = jax.nn.softplus(dt + dt_bias)
            dA = jnp.exp(dt * -jnp.exp(A_log))
            dtx = dt[..., None] * xs

            def step(hprev, inp):
                dA_t, dtx_t, B_t, C_t = inp
                hn = hprev * dA_t[:, :, None, None] + dtx_t[..., None] * B_t[:, None, None, :]
                return (hn, jnp.einsum('bhps,bs->bhp', hn, C_t))
            h0 = jnp.zeros((Bb, NHEADS, HEADDIM, D_STATE), x.dtype)
            _, ys = jax.lax.scan(step, h0, (dA.swapaxes(0, 1), dtx.swapaxes(0, 1), Bm.swapaxes(0, 1), Cm.swapaxes(0, 1)))
            y = ys.swapaxes(0, 1) + D_skip[None, None, :, None] * xs
            y = y.reshape(Bb, L, D_INNER) * jax.nn.silu(z)
            y = y * jax.lax.rsqrt((y * y).mean(-1, keepdims=True) + EPS) * ssm_norm_w
            x = x + jnp.einsum('bli,di->bld', y, out_proj_w)
            h2 = _ln(x, ln2_w, ln2_b)
            f = jnp.einsum('bld,hd->blh', h2, fc1_w)
            f = f[..., :HIDDEN] * jax.nn.silu(f[..., HIDDEN:])
            return x + jnp.einsum('blh,dh->bld', f, fc2_w)
        key = jax.random.key(seed)
        ks = jax.random.split(key, 8)
        s = 0.02
        return {'x': jax.random.normal(ks[0], (B_SZ, SEQ, D_MODEL), jnp.float32), 'ln1_w': jnp.ones((D_MODEL,), jnp.float32), 'ln1_b': jnp.zeros((D_MODEL,), jnp.float32), 'ln2_w': jnp.ones((D_MODEL,), jnp.float32), 'ln2_b': jnp.zeros((D_MODEL,), jnp.float32), 'in_proj_w': jax.random.normal(ks[1], (D_IN_PROJ, D_MODEL), jnp.float32) * s, 'conv_w': jax.random.normal(ks[2], (CONV_DIM, D_CONV), jnp.float32) * s, 'conv_b': jnp.zeros((CONV_DIM,), jnp.float32), 'dt_bias': jax.random.normal(ks[3], (NHEADS,), jnp.float32) * 0.1, 'A_log': jnp.log(jax.random.uniform(ks[4], (NHEADS,), jnp.float32, 1.0, 16.0)), 'D_skip': jnp.ones((NHEADS,), jnp.float32), 'ssm_norm_w': jnp.ones((D_INNER,), jnp.float32), 'out_proj_w': jax.random.normal(ks[5], (D_MODEL, D_INNER), jnp.float32) * s, 'fc1_w': jax.random.normal(ks[6], (2 * HIDDEN, D_MODEL), jnp.float32) * s, 'fc2_w': jax.random.normal(ks[7], (D_MODEL, HIDDEN), jnp.float32) * s}
    _L1_attn_all = _L1_attn_setup()
    _L1_attn_in = {k: v for k, v in _L1_attn_all.items() if k in ('ln1_w', 'ln1_b', 'ln2_w', 'ln2_b', 'in_proj_w', 'conv_w', 'conv_b', 'dt_bias', 'A_log', 'D_skip', 'ssm_norm_w', 'out_proj_w', 'fc1_w', 'fc2_w')}
    del _L1_attn_all

    def _L1_ffn_setup():
        import math
        import jax, jax.numpy as jnp
        import numpy as np
        NUM_EXPERTS = 8
        TOP_K = 2
        CAPACITY_FACTOR = 1.25
        H = 192
        INNER = 768
        B, S = (2, 512)
        key = jax.random.key(seed)
        ks = jax.random.split(key, 9)
        scale = 0.02
        x = jax.random.normal(ks[0], (B, S, H), dtype=jnp.float32)
        Wr = jax.random.normal(ks[1], (H, NUM_EXPERTS), dtype=jnp.float32) * scale
        w1 = jax.random.normal(ks[2], (NUM_EXPERTS, H, INNER), dtype=jnp.float32) * scale
        w3 = jax.random.normal(ks[3], (NUM_EXPERTS, H, INNER), dtype=jnp.float32) * scale
        w2 = jax.random.normal(ks[4], (NUM_EXPERTS, INNER, H), dtype=jnp.float32) * scale
        s1 = jax.random.normal(ks[5], (H, INNER), dtype=jnp.float32) * scale
        s3 = jax.random.normal(ks[6], (H, INNER), dtype=jnp.float32) * scale
        s2 = jax.random.normal(ks[7], (INNER, H), dtype=jnp.float32) * scale
        return {'x': x, 'Wr': Wr, 'w1': w1, 'w3': w3, 'w2': w2, 's1': s1, 's3': s3, 's2': s2}
    _L1_ffn_all = _L1_ffn_setup()
    _L1_ffn_in = {k: v for k, v in _L1_ffn_all.items() if k in ('Wr', 'w1', 'w3', 'w2', 's1', 's3', 's2')}
    del _L1_ffn_all
    return {'x': x, 'L0_tok_W': _L0_tok_in['W'], 'L0_attn_time_decay': _L0_attn_in['time_decay'], 'L0_attn_time_first': _L0_attn_in['time_first'], 'L0_attn_time_mix_k': _L0_attn_in['time_mix_k'], 'L0_attn_time_mix_v': _L0_attn_in['time_mix_v'], 'L0_attn_time_mix_r': _L0_attn_in['time_mix_r'], 'L0_attn_Wk': _L0_attn_in['Wk'], 'L0_attn_Wv': _L0_attn_in['Wv'], 'L0_attn_Wr': _L0_attn_in['Wr'], 'L0_attn_Wo': _L0_attn_in['Wo'], 'L0_ffn_w_router': _L0_ffn_in['w_router'], 'L0_ffn_gamma1': _L0_ffn_in['gamma1'], 'L0_ffn_beta1': _L0_ffn_in['beta1'], 'L0_ffn_w1': _L0_ffn_in['w1'], 'L0_ffn_b1': _L0_ffn_in['b1'], 'L0_ffn_w2': _L0_ffn_in['w2'], 'L0_ffn_b2': _L0_ffn_in['b2'], 'L1_attn_ln1_w': _L1_attn_in['ln1_w'], 'L1_attn_ln1_b': _L1_attn_in['ln1_b'], 'L1_attn_ln2_w': _L1_attn_in['ln2_w'], 'L1_attn_ln2_b': _L1_attn_in['ln2_b'], 'L1_attn_in_proj_w': _L1_attn_in['in_proj_w'], 'L1_attn_conv_w': _L1_attn_in['conv_w'], 'L1_attn_conv_b': _L1_attn_in['conv_b'], 'L1_attn_dt_bias': _L1_attn_in['dt_bias'], 'L1_attn_A_log': _L1_attn_in['A_log'], 'L1_attn_D_skip': _L1_attn_in['D_skip'], 'L1_attn_ssm_norm_w': _L1_attn_in['ssm_norm_w'], 'L1_attn_out_proj_w': _L1_attn_in['out_proj_w'], 'L1_attn_fc1_w': _L1_attn_in['fc1_w'], 'L1_attn_fc2_w': _L1_attn_in['fc2_w'], 'L1_ffn_Wr': _L1_ffn_in['Wr'], 'L1_ffn_w1': _L1_ffn_in['w1'], 'L1_ffn_w3': _L1_ffn_in['w3'], 'L1_ffn_w2': _L1_ffn_in['w2'], 'L1_ffn_s1': _L1_ffn_in['s1'], 'L1_ffn_s3': _L1_ffn_in['s3'], 'L1_ffn_s2': _L1_ffn_in['s2']}

def reference(x, L0_tok_W, L0_attn_time_decay, L0_attn_time_first, L0_attn_time_mix_k, L0_attn_time_mix_v, L0_attn_time_mix_r, L0_attn_Wk, L0_attn_Wv, L0_attn_Wr, L0_attn_Wo, L0_ffn_w_router, L0_ffn_gamma1, L0_ffn_beta1, L0_ffn_w1, L0_ffn_b1, L0_ffn_w2, L0_ffn_b2, L1_attn_ln1_w, L1_attn_ln1_b, L1_attn_ln2_w, L1_attn_ln2_b, L1_attn_in_proj_w, L1_attn_conv_w, L1_attn_conv_b, L1_attn_dt_bias, L1_attn_A_log, L1_attn_D_skip, L1_attn_ssm_norm_w, L1_attn_out_proj_w, L1_attn_fc1_w, L1_attn_fc2_w, L1_ffn_Wr, L1_ffn_w1, L1_ffn_w3, L1_ffn_w2, L1_ffn_s1, L1_ffn_s3, L1_ffn_s2):
    import jax
    import jax.numpy as jnp

    def _L0_tok_ref(x, W):
        import jax, jax.numpy as jnp
        import numpy as np
        NUM_EMBEDDINGS = 8000
        EMBED_DIM = 192
        BATCH, POS = (2, 512)
        INIT_RANGE = 0.02
        onehot = jax.nn.one_hot(x, NUM_EMBEDDINGS, dtype=W.dtype)
        return jnp.einsum('bpn,nd->bpd', onehot, W)

    def _L0_attn_ref(x, time_decay, time_first, time_mix_k, time_mix_v, time_mix_r, Wk, Wv, Wr, Wo):
        import jax, jax.numpy as jnp
        import numpy as np
        import math
        N_LAYER, N_EMBD, LAYER_ID = (12, 192, 0)
        B, T, C = (32, 256, N_EMBD)

        def _init_params():
            r01 = LAYER_ID / (N_LAYER - 1)
            r1a0 = 1.0 - LAYER_ID / N_LAYER
            h = np.arange(C, dtype=np.float32)
            time_decay = (-5.0 + 8.0 * (h / (C - 1)) ** (0.7 + 1.3 * r01)).astype(np.float32)
            zigzag = np.array([(i + 1) % 3 - 1 for i in range(C)], dtype=np.float32) * 0.5
            time_first = (np.ones(C, dtype=np.float32) * math.log(0.3) + zigzag).astype(np.float32)
            xlin = (np.arange(C, dtype=np.float32) / C).reshape(1, 1, C)
            time_mix_k = np.power(xlin, r1a0).astype(np.float32)
            time_mix_v = (np.power(xlin, r1a0) + 0.3 * r01).astype(np.float32)
            time_mix_r = np.power(xlin, 0.5 * r1a0).astype(np.float32)
            return (time_decay, time_first, time_mix_k, time_mix_v, time_mix_r)

        def _wkv(w, u, k, v):

            def step(carry, kv):
                p, q, o = carry
                kt, vt = kv
                no = jnp.maximum(o, u + kt)
                A = jnp.exp(o - no)
                Bc = jnp.exp(u + kt - no)
                y = (A * p + Bc * vt) / (A * q + Bc)
                no2 = jnp.maximum(w + o, kt)
                A2 = jnp.exp(w + o - no2)
                B2 = jnp.exp(kt - no2)
                return ((A2 * p + B2 * vt, A2 * q + B2, no2), y)
            b = k.shape[0]
            init = (jnp.zeros((b, C), jnp.float32), jnp.zeros((b, C), jnp.float32), jnp.full((b, C), -1e+38, jnp.float32))
            kT = jnp.swapaxes(k, 0, 1)
            vT = jnp.swapaxes(v, 0, 1)
            _, ys = jax.lax.scan(step, init, (kT, vT))
            return jnp.swapaxes(ys, 0, 1)
        xx = jnp.pad(x, ((0, 0), (1, 0), (0, 0)))[:, :-1, :]
        xk = x * time_mix_k + xx * (1.0 - time_mix_k)
        xv = x * time_mix_v + xx * (1.0 - time_mix_v)
        xr = x * time_mix_r + xx * (1.0 - time_mix_r)
        k = jnp.einsum('btc,oc->bto', xk, Wk)
        v = jnp.einsum('btc,oc->bto', xv, Wv)
        r = jnp.einsum('btc,oc->bto', xr, Wr)
        sr = jax.nn.sigmoid(r)
        y = _wkv(time_decay, time_first, k, v)
        return jnp.einsum('btc,oc->bto', sr * y, Wo)

    def _L0_ffn_ref(x, w_router, gamma1, beta1, w1, b1, w2, b2):
        import jax, jax.numpy as jnp
        import numpy as np
        DIM = 192
        NUM_EXPERTS = 4
        NUM_HEADS = 12
        HEAD_DIM = DIM // NUM_HEADS
        MLP_HID = 4 * DIM
        FC1_OUT = MLP_HID + 3 * DIM
        FC2_IN = MLP_HID + DIM
        FC2_OUT = 2 * DIM
        CAP_FACTOR = 0.5
        LN_EPS = 1e-06
        B, N, C = x.shape
        E = NUM_EXPERTS
        cap = int(CAP_FACTOR * N)
        m = np.array([C // 2 ** (E - 1 - e) for e in range(E)])
        in_mask = (np.arange(C)[None, :] < m[:, None]).astype(np.float32)
        in_mask = jnp.asarray(in_mask)
        out_mask = jnp.concatenate([in_mask, in_mask], axis=-1)
        logits = jnp.einsum('bnc,ec->bne', x, w_router)
        probs = jax.nn.softmax(logits, axis=-1)
        gate, idx = jax.lax.top_k(jnp.swapaxes(probs, 1, 2), cap)
        dispatch = jax.nn.one_hot(idx, N, dtype=x.dtype)
        combine = dispatch * gate[..., None]
        mu = jnp.mean(x, -1, keepdims=True)
        var = jnp.var(x, -1, keepdims=True)
        y = (x - mu) * jax.lax.rsqrt(var + LN_EPS) * gamma1 + beta1
        xg = jnp.einsum('becn,bnd->becd', dispatch, y)
        xg = xg * in_mask[None, :, None, :]
        h = jnp.einsum('becd,fd->becf', xg, w1) + b1
        h = jnp.einsum('becn,becf->bnf', dispatch, h)
        x_mlp, x_qkv = (h[..., :MLP_HID], h[..., MLP_HID:])
        qkv = x_qkv.reshape(B, N, 3, NUM_HEADS, HEAD_DIM).transpose(2, 0, 3, 1, 4)
        q, k, v = (qkv[0], qkv[1], qkv[2])
        scale = HEAD_DIM ** (-0.5)
        attn = jax.nn.softmax(jnp.einsum('bhqd,bhkd->bhqk', q, k) * scale, axis=-1)
        x_attn = jnp.einsum('bhqk,bhkd->bhqd', attn, v)
        x_attn = x_attn.transpose(0, 2, 1, 3).reshape(B, N, C)
        x_mlp = jax.nn.gelu(x_mlp, approximate=False)
        y2 = jnp.concatenate([x_mlp, x_attn], axis=-1)
        yg = jnp.einsum('becn,bnf->becf', dispatch, y2)
        o = jnp.einsum('becf,of->beco', yg, w2) + b2
        o = o * out_mask[None, :, None, :]
        z = jnp.einsum('becn,beco->bno', combine, o)
        x_mlp2, x_attn2 = (z[..., :C], z[..., C:])
        return x + x_mlp2 + x_attn2

    def _L1_attn_ref(x, ln1_w, ln1_b, ln2_w, ln2_b, in_proj_w, conv_w, conv_b, dt_bias, A_log, D_skip, ssm_norm_w, out_proj_w, fc1_w, fc2_w):
        import jax, jax.numpy as jnp
        import numpy as np
        B_SZ, SEQ = (1, 512)
        D_MODEL, D_STATE, D_CONV, EXPAND = (192, 64, 4, 2)
        D_INNER = EXPAND * D_MODEL
        HEADDIM = 64
        NHEADS = D_INNER // HEADDIM
        CONV_DIM = D_INNER + 2 * D_STATE
        D_IN_PROJ = 2 * D_INNER + 2 * D_STATE + NHEADS
        HIDDEN = (D_MODEL * EXPAND + 127) // 128 * 128
        EPS = 1e-05

        def _ln(x, w, b):
            m = x.mean(-1, keepdims=True)
            v = ((x - m) ** 2).mean(-1, keepdims=True)
            return (x - m) * jax.lax.rsqrt(v + EPS) * w + b

        def _block(x, ln1_w, ln1_b, ln2_w, ln2_b, in_proj_w, conv_w, conv_b, dt_bias, A_log, D_skip, ssm_norm_w, out_proj_w, fc1_w, fc2_w):
            Bb, L, _ = x.shape
            h = _ln(x, ln1_w, ln1_b)
            zxbcdt = jnp.einsum('bld,pd->blp', h, in_proj_w)
            z = zxbcdt[..., :D_INNER]
            xBC = zxbcdt[..., D_INNER:D_INNER + CONV_DIM]
            dt = zxbcdt[..., D_INNER + CONV_DIM:]
            xp = jnp.pad(xBC, ((0, 0), (D_CONV - 1, 0), (0, 0)))
            xBC = sum((xp[:, k:k + L, :] * conv_w[:, k] for k in range(D_CONV))) + conv_b
            xBC = jax.nn.silu(xBC)
            xs = xBC[..., :D_INNER].reshape(Bb, L, NHEADS, HEADDIM)
            Bm = xBC[..., D_INNER:D_INNER + D_STATE]
            Cm = xBC[..., D_INNER + D_STATE:]
            dt = jax.nn.softplus(dt + dt_bias)
            dA = jnp.exp(dt * -jnp.exp(A_log))
            dtx = dt[..., None] * xs

            def step(hprev, inp):
                dA_t, dtx_t, B_t, C_t = inp
                hn = hprev * dA_t[:, :, None, None] + dtx_t[..., None] * B_t[:, None, None, :]
                return (hn, jnp.einsum('bhps,bs->bhp', hn, C_t))
            h0 = jnp.zeros((Bb, NHEADS, HEADDIM, D_STATE), x.dtype)
            _, ys = jax.lax.scan(step, h0, (dA.swapaxes(0, 1), dtx.swapaxes(0, 1), Bm.swapaxes(0, 1), Cm.swapaxes(0, 1)))
            y = ys.swapaxes(0, 1) + D_skip[None, None, :, None] * xs
            y = y.reshape(Bb, L, D_INNER) * jax.nn.silu(z)
            y = y * jax.lax.rsqrt((y * y).mean(-1, keepdims=True) + EPS) * ssm_norm_w
            x = x + jnp.einsum('bli,di->bld', y, out_proj_w)
            h2 = _ln(x, ln2_w, ln2_b)
            f = jnp.einsum('bld,hd->blh', h2, fc1_w)
            f = f[..., :HIDDEN] * jax.nn.silu(f[..., HIDDEN:])
            return x + jnp.einsum('blh,dh->bld', f, fc2_w)
        return _block(x, ln1_w, ln1_b, ln2_w, ln2_b, in_proj_w, conv_w, conv_b, dt_bias, A_log, D_skip, ssm_norm_w, out_proj_w, fc1_w, fc2_w)

    def _L1_ffn_ref(x, Wr, w1, w3, w2, s1, s3, s2):
        import math
        import jax, jax.numpy as jnp
        import numpy as np
        NUM_EXPERTS = 8
        TOP_K = 2
        CAPACITY_FACTOR = 1.25
        H = 192
        INNER = 768
        B, S = (2, 512)
        b, s, h = x.shape
        n = b * s
        flat = x.reshape(n, h)
        logits = flat @ Wr
        probs = jax.nn.softmax(logits, axis=-1)
        topk_p, topk_i = jax.lax.top_k(probs, TOP_K)
        topk_p = topk_p / jnp.clip(topk_p.sum(-1, keepdims=True), 1e-09)
        capacity = max(1, math.ceil(n * TOP_K / NUM_EXPERTS * CAPACITY_FACTOR))
        onehot = topk_i[None, :, :] == jnp.arange(NUM_EXPERTS)[:, None, None]
        w_tok = jnp.sum(topk_p[None] * onehot, axis=-1)
        assigned = jnp.any(onehot, axis=-1)
        score = jnp.where(assigned, w_tok, -jnp.inf)
        order = jnp.argsort(-score, axis=1)[:, :capacity]
        score_sel = jnp.take_along_axis(score, order, axis=1)
        valid = jnp.isfinite(score_sel)
        weight_sel = jnp.where(valid, score_sel, 0.0)
        dispatch = flat[order]
        gate = jax.nn.silu(jnp.einsum('ech,ehi->eci', dispatch, w1))
        up = jnp.einsum('ech,ehi->eci', dispatch, w3)
        expert_out = jnp.einsum('eci,eih->ech', gate * up, w2)
        expert_out = expert_out * weight_sel[..., None]
        routed = jnp.zeros((n, h), dtype=flat.dtype)
        routed = routed.at[order.reshape(-1)].add(expert_out.reshape(-1, h))
        shared = jax.nn.silu(flat @ s1) * (flat @ s3) @ s2
        out = routed + shared
        return out.reshape(b, s, h)
    h = _L0_tok_ref(x, L0_tok_W)
    h = h + _L0_attn_ref(_layernorm(h, axis=-1), L0_attn_time_decay, L0_attn_time_first, L0_attn_time_mix_k, L0_attn_time_mix_v, L0_attn_time_mix_r, L0_attn_Wk, L0_attn_Wv, L0_attn_Wr, L0_attn_Wo)
    h = h + _L0_ffn_ref(_layernorm(h, axis=-1), L0_ffn_w_router, L0_ffn_gamma1, L0_ffn_beta1, L0_ffn_w1, L0_ffn_b1, L0_ffn_w2, L0_ffn_b2)
    h = h + _L1_attn_ref(_layernorm(h, axis=-1), L1_attn_ln1_w, L1_attn_ln1_b, L1_attn_ln2_w, L1_attn_ln2_b, L1_attn_in_proj_w, L1_attn_conv_w, L1_attn_conv_b, L1_attn_dt_bias, L1_attn_A_log, L1_attn_D_skip, L1_attn_ssm_norm_w, L1_attn_out_proj_w, L1_attn_fc1_w, L1_attn_fc2_w)
    h = h + _L1_ffn_ref(_layernorm(h, axis=-1), L1_ffn_Wr, L1_ffn_w1, L1_ffn_w3, L1_ffn_w2, L1_ffn_s1, L1_ffn_s3, L1_ffn_s2)
    return h

_drawn_inputs = setup_inputs


def setup_inputs(seed=0):
    import zlib

    import numpy as np

    out = dict(_drawn_inputs(seed))
    spreads = {'L0_ffn_gamma1': (1.0, 0.6),
     'L0_ffn_beta1': (0.0, 0.639),
     'L0_ffn_b1': (0.0, 0.1),
     'L0_ffn_b2': (0.0, 0.1),
     'L1_attn_ln1_w': (1.0, 0.2),
     'L1_attn_ln1_b': (0.0, 0.453),
     'L1_attn_ln2_w': (1.0, 0.6),
     'L1_attn_ln2_b': (0.0, 0.8),
     'L1_attn_conv_b': (0.0, 0.1),
     'L1_attn_D_skip': (1.0, 0.2),
     'L1_attn_ssm_norm_w': (1.0, 0.2)}
    factors = {'L1_attn_dt_bias': 8.0,
     'L1_attn_A_log': 8.0,
     'L1_attn_fc1_w': 6.273,
     'L1_attn_fc2_w': 6.239,
     'L1_ffn_Wr': 8.0,
     'L1_ffn_w1': 7.11,
     'L1_ffn_w3': 7.085,
     'L1_ffn_w2': 7.054,
     'L1_ffn_s1': 4.911,
     'L1_ffn_s3': 4.883,
     'L1_ffn_s2': 4.895}
    for name, (base, spread) in spreads.items():
        noise = np.random.default_rng([zlib.crc32(name.encode()), seed]).standard_normal(out[name].shape)
        drawn = base * np.exp(spread * noise) if base else spread * noise
        out[name] = jnp.asarray(drawn.astype(out[name].dtype))
    for name, factor in factors.items():
        out[name] = (out[name] * factor).astype(out[name].dtype)
    return out
```

```python
from contextlib import ExitStack, contextmanager

import concourse.bass as bass
from concourse import mybir

ALU = mybir.AluOpType
ACT = mybir.ActivationFunctionType
F32 = mybir.dt.float32
BF16 = mybir.dt.bfloat16
I32 = mybir.dt.int32
AX_X = mybir.AxisListType.X

P = 128
C = 192
CH = C // 2
B, T = 8, 512
N = B * T
NB = N // P
J = T // P
U = 2
TURNS = B // U
VOCAB = 8000
NEG_HUGE = -1e38


def need(eng, sem, t, per_turn, k, ago=0):
    eng.wait_ge(sem, t * per_turn + (U + k + 1 - ago))


class Kit:

    def __init__(self, nc, ctx):
        self.nc, self.ctx, self.whole, self.used = nc, ctx, ctx, []

    @contextmanager
    def phase(self):
        outer, self.used = self.ctx, []
        with ExitStack() as self.ctx:
            yield self.ctx
        self.ctx = outer
        with self.nc.Block() as block:
            @block.sync
            def _(sp):
                for x in self.used:
                    sp.sem_clear(x)

    def sem(self, name):
        self.used.append(self.ctx.enter_context(self.nc.semaphore(name)))
        return self.used[-1]

    def apart(self, pool):
        pool.sem_inc(self.passed, 1)

    def pool_dma_sem(self, name):
        return self.whole.enter_context(self.nc.semaphore(name))

    def sems(self, names):
        return [self.sem(n) for n in names.split()]


def tile_maker(nc, ctx):
    def sb(name, shape, dt=F32):
        return ctx.enter_context(nc.sbuf_tensor(name, shape, dt))
    return sb


def psum_maker(nc, ctx):
    def ps(name, shape, dt=F32):
        return ctx.enter_context(nc.psum_tensor(name, shape, dt))
    return ps


def bc(ap, n):
    return ap.unsqueeze(len(ap.shape)).broadcast_to([*ap.shape, n])


def setup_constants(kit):
    nc = kit.nc
    sb = tile_maker(nc, kit.ctx)
    kit.h = sb("h", [P, NB, C])
    kit.ident = sb("ident", [P, P])
    kit.ident16 = sb("ident16", [P, P], BF16)
    kit.minus_half = sb("minus_half", [P, 8])
    kit.passed = kit.pool_dma_sem("passed")
    made = kit.sem("const_made")
    with nc.Block() as block:
        @block.gpsimd
        def _(pool):
            pool.memset(kit.ident[:, :], 0.0).then_inc(made, 1)
            pool.memset(kit.ident16[:, :], 0.0).then_inc(made, 1)
            pool.memset(kit.minus_half[:, :], -0.5).then_inc(made, 1)
            pool.wait_ge(made, 3)
            for m in (kit.ident, kit.ident16):
                pool.affine_select(out=m[:, :], in_=m[:, :], compare_op=ALU.not_equal, fill=1.0, base=0,
                                   pattern=[[-1, P]], channel_multiplier=1).then_inc(made, 1)
            pool.wait_ge(made, 5)


def ln_stats(dve, src, stats, mv, var_eps, eps):
    for j in range(J):
        dve.bn_stats(stats[:, j, :], src[:, j, :])
    dve.drain()
    for j in range(J):
        dve.bn_aggr(mv[:, j, :], stats[:, j, :])
    dve.drain()
    return dve.tensor_scalar(var_eps[:, :], mv[:, :, 1], float(eps), None, ALU.add)


def ln_rstd(kit, pool, rstd, var_eps):
    return pool.tensor_tensor(rstd[:, :], var_eps[:, :], kit.minus_half[:, 0:J], ALU.pow)


def ln_apply(dve, out, src, mv, rstd):
    for j in range(J):
        last = dve.tensor_scalar(out[:, j, :], src[:, j, :], mv[:, j, 0:1], rstd[:, j:j + 1],
                                 ALU.subtract, ALU.mult)
    return last


def embed_and_time_mix(kit, a):
    nc = kit.nc
    with kit.phase() as ctx:
        sb, ps = tile_maker(nc, ctx), psum_maker(nc, ctx)
        tokens = sb("tokens", [P, NB], I32)
        tok_f = sb("tok_f", [P, NB])
        in_vocab = sb("in_vocab", [P, NB])
        tok_tmp = sb("tok_tmp", [P, NB])
        row_of = sb("row_of", [P, NB], I32)
        row_now = sb("row_now", [P, U, J], I32)
        emb = sb("emb", [P, U, J, C])
        h0 = sb("h0", [P, U, J, C])
        stats = sb("stats", [P, U, J, 6])
        mv = sb("mv", [P, U, J, 2])
        var_eps = sb("var_eps", [P, U, J])
        rstd = sb("rstd", [P, U, J])
        xn = sb("xn", [P, U, J, C])
        xT = sb("xT", [CH, U, 2, T + 1])
        diff = sb("diff", [CH, 2, T])
        mixed = sb("mixed", [CH, U, 3, 2, T])
        kT = sb("kT", [CH, U, 2, T])
        vT = sb("vT", [CH, U, 2, T])
        gate = sb("gate", [CH, U, 2, T])
        omax = sb("omax", [CH, 2, T + 1])
        gaps = sb("gaps", [CH, 2, 2, T])
        gap_lo = sb("gap_lo", [CH, U, 2, 2, T])
        gap_hi = sb("gap_hi", [CH, U, 2, 2, T])
        bv = sb("bv", [CH, 2, T])
        inject = sb("inject", [CH, 2, T])
        pnum = sb("pnum", [CH, 2, T + 1])
        qden = sb("qden", [CH, 2, T + 1])
        num = sb("num", [CH, 2, T])
        den = sb("den", [CH, 2, T])
        z = sb("z", [CH, U, 2, T])
        decay = sb("decay", [CH, 2])
        first = sb("first", [CH, 2])
        mix_of = sb("mix_of", [CH, 3, 2])
        wkvr = sb("wkvr", [CH, 3, 2, C])
        wo = sb("wo", [CH, 2, C])
        ps_t = ps("ps_t", [P, 2, T])
        ps_p = ps("ps_p", [P, 2, 2, T])
        ps_o = ps("ps_o", [P, J, 256])
        (loaded, rows_ready, rows_now_ready, h0_ready, rstd_ready, xn_ready, xT_psum, xT_ready, mixed_ready,
         proj_psum, proj_read, gaps_ready, exps_ready, bv_ready, z_ready, out_psum, h_written) = (
            kit.sem("a_" + n) for n in (
                "loaded rows_ready rows_now_ready h0_ready rstd_ready xn_ready xT_psum xT_ready mixed_ready "
                "proj_psum proj_read gaps_ready exps_ready bv_ready z_ready out_psum h_written").split())
        emb_in = [kit.pool_dma_sem(f"a_emb_in{u}") for u in range(U)]
        counted = (h0_ready, rstd_ready, xn_ready, xT_psum, xT_ready, mixed_ready, proj_psum, proj_read,
                   gaps_ready, exps_ready, bv_ready, z_ready, out_psum, h_written)
        block = ctx.enter_context(nc.Block())

        @block.sync
        def _(sp):
            for s in counted:
                sp.sem_inc(s, U)
            sp.dma_start(tokens[:, :], a["x"]).then_inc(loaded, 16)
            sp.dma_start(decay[:, :], a["decay"]).then_inc(loaded, 16)
            sp.dma_start(first[:, :], a["first"]).then_inc(loaded, 16)
            sp.dma_start(mix_of[:, :, :], a["mix"]).then_inc(loaded, 16)
            sp.dma_start(wkvr[:, :, :, :], a["wkvr"]).then_inc(loaded, 16)
            sp.dma_start(wo[:, :, :], a["wo"]).then_inc(loaded, 16)

        @block.gpsimd
        def _(pool):
            pool.wait_ge(rows_ready, 1)
            with pool.Fori(0, TURNS) as t:
                pool.tensor_copy(row_now[:, :, :], row_of[:, bass.ds(t * (U * J), U * J)].rearrange(
                    "p (u j) -> p u j", u=U)).then_inc(rows_now_ready, 1)
                pool.wait_ge(rows_now_ready, t + 1)
                for u in range(U):
                    need(pool, h0_ready, t, U, u, ago=U)
                    kit.apart(pool)
                    for j in range(J):
                        pool.indirect_dma_start(
                            out=emb[:, u, j, :], out_offset=None, in_=a["emb"],
                            in_offset=bass.IndirectOffsetOnAxis(ap=row_now[:, u, j:j + 1], axis=0)
                        ).then_inc(emb_in[u], 16)
                for u in range(U):
                    need(pool, h0_ready, t, U, u)
                    need(pool, xn_ready, t, U, u, ago=U)
                    ln_rstd(kit, pool, rstd[:, u, :], var_eps[:, u, :]).then_inc(rstd_ready, 1)

        @block.vector
        def _(dve):
            dve.memset(xT[:, :, :, 0:1], 0.0)
            dve.memset(omax[:, :, 0:1], NEG_HUGE)
            dve.memset(pnum[:, :, 0:1], 0.0)
            dve.memset(qden[:, :, 0:1], 0.0)
            dve.wait_ge(loaded, 96)
            dve.tensor_copy(tok_f[:, :], tokens[:, :])
            dve.drain()
            dve.tensor_scalar(tok_tmp[:, :], tok_f[:, :], 0.0, None, ALU.is_ge)
            dve.tensor_scalar(in_vocab[:, :], tok_f[:, :], float(VOCAB), None, ALU.is_lt)
            dve.tensor_scalar(tok_f[:, :], tok_f[:, :], 0.0, float(VOCAB - 1), ALU.max, ALU.min)
            dve.drain()
            dve.tensor_tensor(in_vocab[:, :], in_vocab[:, :], tok_tmp[:, :], ALU.mult)
            dve.tensor_copy(row_of[:, :], tok_f[:, :]).then_inc(rows_ready, 1)
            with dve.Fori(0, TURNS) as t:
                for u in range(U):
                    dve.drain()
                    dve.wait_ge(emb_in[u], t * (16 * J) + 16 * J)
                    dve.tensor_tensor(h0[:, u, :, :], emb[:, u, :, :],
                                      bc(in_vocab[:, bass.ds(t * (U * J) + u * J, J)], C), ALU.mult)
                    dve.drain()
                    ln_stats(dve, h0[:, u], stats[:, u], mv[:, u], var_eps[:, u], 1e-5).then_inc(h0_ready, 1)
                for u in range(U):
                    need(dve, rstd_ready, t, U, u)
                    need(dve, xT_psum, t, U, u, ago=U)
                    ln_apply(dve, xn[:, u], h0[:, u], mv[:, u], rstd[:, u]).then_inc(xn_ready, 1)
                for u in range(U):
                    now, prev = xT[:, u, :, 1:T + 1], xT[:, u, :, 0:T]
                    dve.drain()
                    need(dve, xT_ready, t, U, u)
                    dve.tensor_tensor(diff[:, :, :], now, prev, ALU.subtract)
                    dve.drain()
                    for o in range(3):
                        for c in range(2):
                            last = dve.scalar_tensor_tensor(
                                out=mixed[:, u, o, c, :], in0=diff[:, c, :], scalar=mix_of[:, o, c:c + 1],
                                in1=prev[:, c, :], op0=ALU.mult, op1=ALU.add)
                    last.then_inc(mixed_ready, 1)
                for u in range(U):
                    dve.drain()
                    need(dve, proj_read, t, 3 * U, 3 * u + 0)
                    for c in range(2):
                        dve.tensor_tensor_scan(omax[:, c, 1:T + 1], decay[:, c:c + 1].broadcast_to([CH, T]),
                                               kT[:, u, c, :], NEG_HUGE, ALU.add, ALU.max)
                    dve.drain()
                    for c in range(2):
                        dve.scalar_tensor_tensor(out=gaps[:, 0, c, :], in0=kT[:, u, c, :], scalar=first[:, c:c + 1],
                                                 in1=omax[:, c, 0:T], op0=ALU.add, op1=ALU.subtract)
                        dve.scalar_tensor_tensor(out=gaps[:, 1, c, :], in0=omax[:, c, 0:T], scalar=decay[:, c:c + 1],
                                                 in1=kT[:, u, c, :], op0=ALU.add, op1=ALU.subtract)
                    dve.drain()
                    dve.tensor_scalar(gap_lo[:, u], gaps[:, :, :, :], 0.0, None, ALU.min)
                    dve.tensor_scalar(gap_hi[:, u], gaps[:, :, :, :], 0.0, None, ALU.max).then_inc(gaps_ready, 1)
                for u in range(U):
                    eb, ea2 = gap_lo[:, u, 0], gap_lo[:, u, 1]
                    ea, eb2 = gap_hi[:, u, 0], gap_hi[:, u, 1]
                    dve.drain()
                    need(dve, exps_ready, t, U, u)
                    need(dve, proj_read, t, 3 * U, 3 * u + 2)
                    dve.tensor_tensor(inject[:, :, :], eb2, vT[:, u], ALU.mult)
                    dve.tensor_tensor(bv[:, :, :], eb, vT[:, u], ALU.mult)
                    dve.drain()
                    for c in range(2):
                        dve.tensor_tensor_scan(pnum[:, c, 1:T + 1], ea2[:, c, :], inject[:, c, :], 0.0,
                                               ALU.mult, ALU.add)
                        dve.tensor_tensor_scan(qden[:, c, 1:T + 1], ea2[:, c, :], eb2[:, c, :], 0.0,
                                               ALU.mult, ALU.add)
                    dve.drain()
                    dve.tensor_tensor(den[:, :, :], ea, qden[:, :, 0:T], ALU.mult)
                    dve.tensor_tensor(num[:, :, :], ea, pnum[:, :, 0:T], ALU.mult)
                    dve.drain()
                    dve.tensor_tensor(den[:, :, :], den[:, :, :], eb, ALU.add)
                    dve.tensor_tensor(num[:, :, :], num[:, :, :], bv[:, :, :], ALU.add)
                    dve.drain()
                    dve.reciprocal(den[:, :, :], den[:, :, :])
                    dve.tensor_tensor(num[:, :, :], num[:, :, :], gate[:, u], ALU.mult)
                    dve.drain()
                    need(dve, out_psum, t, U, u, ago=U)
                    dve.tensor_tensor(z[:, u], num[:, :, :], den[:, :, :], ALU.mult).then_inc(z_ready, 1)
                for u in range(U):
                    need(dve, out_psum, t, U, u)
                    dve.tensor_tensor(kit.h[:, bass.ds(t * (U * J) + u * J, J), :], ps_o[:, :, 0:C], h0[:, u],
                                      ALU.add).then_inc(h_written, 1)

        @block.tensor
        def _(pe):
            pe.wait_ge(loaded, 96)
            with pe.Fori(0, TURNS) as t:
                for u in range(U):
                    need(pe, xn_ready, t, U, u)
                    need(pe, xT_ready, t, U, u, ago=1)
                    for j in range(J):
                        for c in range(2):
                            last = pe.transpose(ps_t[0:CH, c, j * P:(j + 1) * P], xn[:, u, j, c * CH:(c + 1) * CH],
                                                kit.ident[:, :])
                    last.then_inc(xT_psum, 1)
                for u in range(U):
                    need(pe, mixed_ready, t, U, u)
                    for o in range(3):
                        need(pe, proj_read, t, 3 * U, 3 * u + o, ago=2)
                        for m in range(2):
                            for c in range(2):
                                last = pe.matmul(ps_p[0:CH, (u + o) % 2, m, :], wkvr[:, o, c, m * CH:(m + 1) * CH],
                                                 mixed[:, u, o, c, :], start=c == 0, stop=c == 1)
                        last.then_inc(proj_psum, 1)
                for u in range(U):
                    need(pe, z_ready, t, U, u)
                    need(pe, h_written, t, U, u, ago=1)
                    for j in range(J):
                        for c in range(2):
                            last = pe.matmul(ps_o[:, j, 0:C], z[:, u, c, j * P:(j + 1) * P], wo[:, c, :],
                                             start=c == 0, stop=c == 1)
                    last.then_inc(out_psum, 1)

        @block.scalar
        def _(act):
            with act.Fori(0, TURNS) as t:
                for u in range(U):
                    need(act, xT_psum, t, U, u)
                    need(act, mixed_ready, t, U, u, ago=U)
                    act.activation(xT[:, u, :, 1:T + 1], ps_t[0:CH, :, :], ACT.Copy).then_inc(xT_ready, 1)
                for u in range(U):
                    for o in range(3):
                        need(act, proj_psum, t, 3 * U, 3 * u + o)
                        if o == 0:
                            need(act, z_ready, t, U, u, ago=U)
                        act.activation((kT, vT, gate)[o][:, u], ps_p[0:CH, (u + o) % 2, :, :],
                                       ACT.Sigmoid if o == 2 else ACT.Copy).then_inc(proj_read, 1)
                for u in range(U):
                    need(act, gaps_ready, t, U, u)
                    act.activation(gap_lo[:, u], gap_lo[:, u], ACT.Exp)
                    act.activation(gap_hi[:, u], gap_hi[:, u], ACT.Exp, scale=-1.0).then_inc(exps_ready, 1)


EXPERTS0 = 4
CAP0 = T // 2
BANDS = ((0, 24), (24, 48), (48, 96), (96, 192))
TOP_BIT = 29


def kth_largest(dve, rows, scores, bits, cand, bit, count, keep, mark, k, total=None):
    dve.memset(bits[:, :], 0)
    dve.memset(bit[:, :], 1 << TOP_BIT)
    dve.drain()
    with dve.Fori(0, TOP_BIT + 1) as step:
        dve.tensor_tensor(cand[:, :], bits[:, :], bit[:, :], ALU.bitwise_or)
        dve.drain()
        last = dve.tensor_scalar(mark, scores, cand[:, :].bitcast(F32), 0.0, ALU.is_ge, ALU.add,
                                 accum_out=count[:, :])
        if total is None:
            dve.drain()
            counted = count
        else:
            counted = total(dve, step, last)
        dve.tensor_scalar(keep[:, :], counted[:, :], float(k), None, ALU.is_ge)
        dve.drain()
        dve.tensor_tensor(keep[:, :], keep[:, :], bit[:, :], ALU.mult)
        dve.tensor_scalar(bit[:, :], bit[:, :], 1, None, ALU.logical_shift_right)
        dve.drain()
        dve.tensor_tensor(bits[:, :], bits[:, :], keep[:, :], ALU.bitwise_or)
        dve.drain()


def route_tokens(kit, a, x1, bands):
    nc = kit.nc
    R = B * EXPERTS0
    with kit.phase() as ctx:
        sb, ps = tile_maker(nc, ctx), psum_maker(nc, ctx)
        stats = sb("b_stats", [P, U, J, 6])
        mv = sb("b_mv", [P, U, J, 2])
        var_eps = sb("b_var_eps", [P, U, J])
        rstd = sb("b_rstd", [P, U, J])
        xn = sb("b_xn", [P, U, J, C])
        xT = sb("b_xT", [CH, U, 2, T])
        w_router = sb("w_router", [CH, 2, EXPERTS0])
        probs = sb("probs", [P, NB, EXPERTS0])
        prob_rows = sb("prob_rows", [P, J, B, EXPERTS0])
        peak = sb("peak", [P, NB])
        mass = sb("mass", [P, NB])
        score = sb("score", [R, T])
        mark = sb("mark", [R, T])
        tie = sb("tie", [R, T])
        tie_rank = sb("tie_rank", [R, T])
        taken = sb("taken", [R, 2, T])
        ones = sb("b_ones", [R, T])
        bits = sb("bits", [R, 1], I32)
        cand = sb("cand", [R, 1], I32)
        bit = sb("bit", [R, 1], I32)
        keep = sb("keep", [R, 1], I32)
        count = sb("count", [R, 1])
        room = sb("room", [R, 1])
        ps_t = ps("b_ps_t", [P, 2, T])
        ps_l = ps("b_ps_l", [P, U, 512])
        ps_s = ps("b_ps_s", [R, J, P])
        ps_b = ps("b_ps_b", [P, 2, J, R])
        (loaded, var_ready, rstd_ready, xn_ready, x1_kept, xT_psum, xT_ready, logit_psum, logit_read, shifted,
         exp_ready, probs_ready, score_psum, taken_ready, taken_psum) = (
            kit.sem("b_" + n) for n in (
                "loaded var_ready rstd_ready xn_ready x1_kept xT_psum xT_ready logit_psum logit_read shifted "
                "exp_ready probs_ready score_psum taken_ready taken_psum").split())
        counted = (var_ready, rstd_ready, xn_ready, x1_kept, xT_psum, xT_ready, logit_psum, logit_read)
        block = ctx.enter_context(nc.Block())

        @block.sync
        def _(sp):
            for s in counted:
                sp.sem_inc(s, U)
            sp.dma_start(w_router[:, :, :], a["w_router"]).then_inc(loaded, 16)

        @block.gpsimd
        def _(pool):
            with pool.Fori(0, TURNS) as t:
                for u in range(U):
                    need(pool, var_ready, t, U, u)
                    ln_rstd(kit, pool, rstd[:, u, :], var_eps[:, u, :]).then_inc(rstd_ready, 1)
                for u in range(U):
                    need(pool, xn_ready, t, U, u)
                    kit.apart(pool)
                    pool.tensor_copy(x1[:, bass.ds(t * (U * J) + u * J, J), :], xn[:, u]).then_inc(x1_kept, 1)

        @block.vector
        def _(dve):
            dve.memset(ones[:, :], 1.0)
            with dve.Fori(0, TURNS) as t:
                for u in range(U):
                    dve.drain()
                    ln_stats(dve, kit.h[:, bass.ds(t * (U * J) + u * J, J), :], stats[:, u], mv[:, u],
                             var_eps[:, u], 1e-5).then_inc(var_ready, 1)
                for u in range(U):
                    need(dve, rstd_ready, t, U, u)
                    need(dve, xT_psum, t, U, u, ago=U)
                    need(dve, x1_kept, t, U, u, ago=U)
                    ln_apply(dve, xn[:, u], kit.h[:, bass.ds(t * (U * J) + u * J, J), :], mv[:, u],
                             rstd[:, u]).then_inc(xn_ready, 1)
                for u in range(U):
                    need(dve, logit_psum, t, U, u)
                    dve.tensor_copy(probs[:, bass.ds(t * (U * J) + u * J, J), :], ps_l[:, u, 0:J * EXPERTS0].rearrange(
                        "p (j e) -> p j e", j=J)).then_inc(logit_read, 1)
            dve.drain()
            dve.tensor_reduce(peak[:, :], probs[:, :, :], AX_X, ALU.max)
            dve.drain()
            dve.tensor_tensor(probs[:, :, :], probs[:, :, :], bc(peak[:, :], EXPERTS0), ALU.subtract).then_inc(shifted, 1)
            dve.wait_ge(exp_ready, 1)
            dve.tensor_reduce(mass[:, :], probs[:, :, :], AX_X, ALU.add)
            dve.drain()
            dve.reciprocal(mass[:, :], mass[:, :])
            dve.drain()
            dve.tensor_tensor(prob_rows[:, :, :, :].rearrange("p j b e -> p b j e"),
                              probs[:, :, :].rearrange("p (b j) e -> p b j e", j=J),
                              bc(mass[:, :].rearrange("p (b j) -> p b j", j=J), EXPERTS0), ALU.mult)\
               .then_inc(probs_ready, 1)
            dve.wait_ge(score_psum, 1)
            dve.tensor_copy(score[:, :], ps_s[:, :, :])
            dve.drain()
            kth_largest(dve, R, score[:, :], bits, cand, bit, count, keep, mark[:, :], CAP0)
            kth = bits[:, :].bitcast(F32)
            dve.tensor_scalar(mark[:, :], score[:, :], kth, 0.0, ALU.is_gt, ALU.add, accum_out=count[:, :])
            dve.tensor_scalar(tie[:, :], score[:, :], kth, None, ALU.is_equal)
            dve.drain()
            dve.tensor_scalar(room[:, :], count[:, :], -1.0, float(CAP0), ALU.mult, ALU.add)
            dve.tensor_tensor_scan(tie_rank[:, :], ones[:, :], tie[:, :], 0.0, ALU.mult, ALU.add)
            dve.drain()
            dve.scalar_tensor_tensor(out=tie[:, :], in0=tie_rank[:, :], scalar=room[:, :], in1=tie[:, :],
                                     op0=ALU.is_le, op1=ALU.mult)
            dve.drain()
            dve.tensor_tensor(taken[:, 0, :], mark[:, :], tie[:, :], ALU.add)
            dve.drain()
            dve.tensor_tensor(taken[:, 1, :], taken[:, 0, :], score[:, :], ALU.mult).then_inc(taken_ready, 1)
            dve.wait_ge(taken_psum, 1)
            for e in reversed(range(EXPERTS0)):
                for w in range(2):
                    src = ps_b[:, w, :, :].rearrange("p j (b e) -> p b j e", e=EXPERTS0)[:, :, :, e]
                    dst = bands[:, w, :, e].rearrange("p (b j) -> p b j", j=J)
                    if e == EXPERTS0 - 1:
                        dve.tensor_copy(dst, src)
                    else:
                        dve.tensor_tensor(dst, src, bands[:, w, :, e + 1].rearrange("p (b j) -> p b j", j=J), ALU.add)
                dve.drain()

        @block.tensor
        def _(pe):
            pe.wait_ge(loaded, 16)
            with pe.Fori(0, TURNS) as t:
                for u in range(U):
                    need(pe, xn_ready, t, U, u)
                    need(pe, xT_ready, t, U, u, ago=1)
                    for j in range(J):
                        for c in range(2):
                            last = pe.transpose(ps_t[0:CH, c, j * P:(j + 1) * P], xn[:, u, j, c * CH:(c + 1) * CH],
                                                kit.ident[:, :])
                    last.then_inc(xT_psum, 1)
                for u in range(U):
                    need(pe, xT_ready, t, U, u)
                    need(pe, logit_read, t, U, u, ago=U)
                    for j in range(J):
                        for c in range(2):
                            last = pe.matmul(ps_l[:, u, j * EXPERTS0:(j + 1) * EXPERTS0], xT[:, u, c, j * P:(j + 1) * P],
                                             w_router[:, c, :], start=c == 0, stop=c == 1)
                    last.then_inc(logit_psum, 1)
            pe.wait_ge(probs_ready, 1)
            for j in range(J):
                last = pe.transpose(ps_s[:, j, :], prob_rows[:, j].rearrange("p b e -> p (b e)"), kit.ident[:, :])
            last.then_inc(score_psum, 1)
            pe.wait_ge(taken_ready, 1)
            for w in range(2):
                for j in range(J):
                    last = pe.transpose(ps_b[:, w, j, :], taken[:, w, j * P:(j + 1) * P], kit.ident[0:R, 0:R])
            last.then_inc(taken_psum, 1)

        @block.scalar
        def _(act):
            with act.Fori(0, TURNS) as t:
                for u in range(U):
                    need(act, xT_psum, t, U, u)
                    need(act, logit_psum, t, U, u, ago=U)
                    act.activation(xT[:, u], ps_t[0:CH, :, :], ACT.Copy).then_inc(xT_ready, 1)
            act.wait_ge(shifted, 1)
            act.activation(probs[:, :, :], probs[:, :, :], ACT.Exp).then_inc(exp_ready, 1)


HEADS, HD = 12, C // 12
MLP = 4 * C
FC1_TILES = MLP // P
QSCALE = HD ** -0.5
G3 = HEADS // 4
PAIRS = 6
STACK = PAIRS * HD
LIVE_E = 8


def moe_attention_ffn(kit, a, x1, bands):
    nc = kit.nc
    with kit.phase() as ctx:
        sb, ps = tile_maker(nc, ctx), psum_maker(nc, ctx)
        gamma = sb("gamma", [P, C])
        beta = sb("beta", [P, C])
        w1 = sb("w1", [CH + 1, 2, MLP + 3 * C])
        w2_mlp = sb("w2_mlp", [P, FC1_TILES, 2, C])
        w2_att = sb("w2_att", [CH, 2, 2, C])
        b2 = sb("b2", [P, 2, C])
        stats = sb("c_stats", [P, J, 6])
        mv = sb("c_mv", [P, J, 2])
        var_eps = sb("c_var_eps", [P, J])
        rstd = sb("c_rstd", [P, J])
        y = sb("y", [P, J, C + 1])
        yT = sb("yT", [CH + 1, 2, T])
        parts = sb("parts", [P, 2, 3, 2 * C], BF16)
        rest = sb("rest", [P, 2 * C])
        stacked = sb("stacked", [P, 2, 2, HEADS, STACK], BF16)
        qT = sb("qT", [STACK + 1, HEADS, T], BF16)
        kT = sb("c_kT", [STACK + 1, HEADS, T], BF16)
        v = sb("v", [P, J, HEADS, 32])
        row_max = sb("row_max", [P, HEADS, J])
        neg_max = sb("neg_max", [P, HEADS, J])
        max_rows = sb("max_rows", [4 * J, G3, P], BF16)
        mlp = sb("mlp", [P, FC1_TILES, T])
        e = sb("e", [P, LIVE_E, T])
        att = sb("att", [P, 2, T])
        rden = sb("rden", [P, J, 4])
        xa = sb("xa", [P, J, C])
        xaT = sb("xaT", [CH, 2, T])
        o = sb("o", [P, J, C])
        ps_t = ps("c_ps_t", [P, 2, T])
        ps_m = ps("c_ps_m", [P, 2, T])
        ps_s = ps("c_ps_s", [P, 2, T])
        ps_a = ps("c_ps_a", [P, 2, T])
        (loaded, w2_ready, var_ready, rstd_ready, y_ready, yT_psum, yT_ready, qk_psum, qk_read, stack_ready, st_psum,
         st_read, v_psum, v_ready, m_psum, m_read, mx_ready, mxT_psum, mxT_ready, mlp_psum, mlp_ready, s_psum,
         e_ready, av_done, a_read, at_psum, xa_ready, xaT_psum, xaT_ready, o_psum, h_done) = (
            kit.sem("c_" + n) for n in (
                "loaded w2_ready var_ready rstd_ready y_ready yT_psum yT_ready qk_psum qk_read stack_ready st_psum "
                "st_read v_psum v_ready m_psum m_read mx_ready mxT_psum mxT_ready mlp_psum mlp_ready s_psum "
                "e_ready av_done a_read at_psum xa_ready xaT_psum xaT_ready o_psum h_done").split())
        max_placed = [kit.sem(f"c_max_placed{g}") for g in range(G3)]
        counted = (var_ready, rstd_ready, y_ready, yT_psum, yT_ready, qk_psum, qk_read, stack_ready, st_psum,
                   st_read, v_psum, v_ready, m_psum, m_read, mx_ready, mxT_psum, mxT_ready, mlp_psum, mlp_ready,
                   s_psum, e_ready, av_done, a_read, at_psum, xa_ready, xaT_psum, xaT_ready, o_psum, h_done)
        block = ctx.enter_context(nc.Block())
        NS = HEADS * J
        NM = 4 * J
        NT = 4 * J
        HH = HEADS // 2

        @block.sync
        def _(sp):
            for s in counted:
                sp.sem_inc(s, U)
            sp.dma_start(gamma[:, :], a["gamma1"].broadcast_to([P, C])).then_inc(loaded, 16)
            sp.dma_start(beta[:, :], a["beta1"].broadcast_to([P, C])).then_inc(loaded, 16)
            sp.dma_start(b2[:, :, :], a["b2"].broadcast_to([P, 2, C])).then_inc(loaded, 16)
            sp.dma_start(w1[:, :, :], a["w1"]).then_inc(loaded, 16)
            sp.dma_start(w2_mlp[:, :, :, :], a["w2_mlp"]).then_inc(loaded, 16)
            sp.dma_start(w2_att[:, :, :, :], a["w2_att"]).then_inc(loaded, 16)
            with sp.Fori(0, B) as t:
                for g in range(G3):
                    need(sp, mxT_ready, t, G3, g)
                    sp.dma_start(qT[STACK:STACK + 1, 4 * g:4 * g + 4, :], max_rows[:, g, :]).then_inc(max_placed[g], 16)

        @block.gpsimd
        def _(pool):
            with pool.Fori(0, B) as t:
                need(pool, var_ready, t, 1, 0)
                ln_rstd(kit, pool, rstd[:, :], var_eps[:, :]).then_inc(rstd_ready, 1)
                for j in range(J):
                    need(pool, qk_read, t, J, j)
                    if j >= 2:
                        need(pool, st_psum, t, NT, 4 * (j - 2) + 3)
                    kit.apart(pool)
                    hml = parts[:, j % 2].rearrange("p s (w h d) -> p w h s d", w=2, h=HEADS)
                    q_part, k_part = hml[:, 0], hml[:, 1]
                    qs = stacked[:, j % 2, 0].rearrange("p h (s d) -> p h s d", s=PAIRS)
                    ks = stacked[:, j % 2, 1].rearrange("p h (s d) -> p h s d", s=PAIRS)
                    pool.tensor_copy(qs[:, :, 0:3, :], q_part[:, :, 0:1, :].broadcast_to([P, HEADS, 3, HD]))
                    pool.tensor_copy(qs[:, :, 3:5, :], q_part[:, :, 1:2, :].broadcast_to([P, HEADS, 2, HD]))
                    pool.tensor_copy(qs[:, :, 5, :], q_part[:, :, 2, :])
                    pool.tensor_copy(ks[:, :, 0:3, :], k_part)
                    pool.tensor_copy(ks[:, :, 3:5, :], k_part[:, :, 0:2, :])
                    pool.tensor_copy(ks[:, :, 5, :], k_part[:, :, 0, :]).then_inc(stack_ready, 1)

        @block.vector
        def _(dve):
            dve.memset(v[:, :, :, HD:HD + 1], 1.0)
            dve.memset(v[:, :, :, HD + 1:32], 0.0)
            dve.memset(kT[STACK:STACK + 1, :, :], 1.0)
            dve.wait_ge(loaded, 96)
            dve.tensor_tensor(w2_mlp[:, :, 0, :], w2_mlp[:, :, 0, :], w2_mlp[:, :, 1, :], ALU.add)
            dve.tensor_tensor(w2_att[:, :, 0, :], w2_att[:, :, 0, :], w2_att[:, :, 1, :], ALU.add)
            dve.tensor_tensor(b2[:, 0, :], b2[:, 0, :], b2[:, 1, :], ALU.add).then_inc(w2_ready, 1)
            with dve.Fori(0, B) as t:
                blocks = bass.ds(t * J, J)
                dve.drain()
                ln_stats(dve, x1[:, blocks, :], stats, mv, var_eps, 1e-6).then_inc(var_ready, 1)
                need(dve, rstd_ready, t, 1, 0)
                need(dve, yT_psum, t, 1, 0, ago=1)
                ln_apply(dve, y[:, :, 0:C], x1[:, blocks, :], mv, rstd)
                dve.drain()
                dve.tensor_tensor(y[:, :, 0:C], y[:, :, 0:C], gamma[:, :].unsqueeze(1).broadcast_to([P, J, C]), ALU.mult)
                dve.drain()
                dve.tensor_tensor(y[:, :, 0:C], y[:, :, 0:C], beta[:, :].unsqueeze(1).broadcast_to([P, J, C]), ALU.add)
                dve.drain()
                for n, (lo, hi) in enumerate(BANDS):
                    dve.tensor_tensor(y[:, :, lo:hi], y[:, :, lo:hi], bc(bands[:, 0, blocks, n], hi - lo), ALU.mult)
                dve.tensor_copy(y[:, :, C], bands[:, 0, blocks, 0]).then_inc(y_ready, 1)
                for j in range(J):
                    need(dve, qk_psum, t, J, j)
                    if j >= 2:
                        need(dve, stack_ready, t, J, j, ago=2)
                    hml = parts[:, j % 2]
                    qk = ps_m[:, j % 2, 0:2 * C]
                    dve.tensor_copy(hml[:, 0, :], qk)
                    dve.drain()
                    dve.tensor_tensor(rest[:, :], qk, hml[:, 0, :], ALU.subtract)
                    dve.drain()
                    dve.tensor_copy(hml[:, 1, :], rest[:, :])
                    dve.drain()
                    dve.tensor_tensor(hml[:, 2, :], rest[:, :], hml[:, 1, :], ALU.subtract).then_inc(qk_read, 1)
                for j in range(J):
                    need(dve, v_psum, t, J, j)
                    dve.tensor_copy(v[:, j, :, 0:HD], ps_m[:, j % 2, 0:C].rearrange("p (h d) -> p h d", h=HEADS))\
                       .then_inc(v_ready, 1)
                for g in range(G3):
                    for n in range(NM * g, NM * (g + 1)):
                        need(dve, m_psum, t, NS, n)
                        dve.tensor_reduce(row_max[:, n // J, n % J:n % J + 1], ps_m[:, n % 2, :], AX_X, ALU.max)\
                           .then_inc(m_read, 1)
                    dve.drain()
                    dve.tensor_scalar(neg_max[:, 4 * g:4 * g + 4, :], row_max[:, 4 * g:4 * g + 4, :], -1.0, None,
                                      ALU.mult).then_inc(mx_ready, 1)
                    need(dve, mxT_psum, t, G3, g)
                    if g == 0:
                        for q in range(G3):
                            dve.wait_ge(max_placed[q], t * 16)
                    dve.tensor_copy(max_rows[:, g, :], ps_t[0:4 * J, 1, 0:P]).then_inc(mxT_ready, 1)
                for g in range(G3):
                    got = ps_t[:, g % 2, :].rearrange("p (j i d) -> p j i d", j=J, i=4)
                    dve.drain()
                    need(dve, at_psum, t, G3, g)
                    dve.reciprocal(rden[:, :, :], got[:, :, :, HD])
                    dve.drain()
                    for i in range(4):
                        last = dve.tensor_tensor(xa[:, :, (4 * g + i) * HD:(4 * g + i + 1) * HD], got[:, :, i, 0:HD],
                                                 bc(rden[:, :, i], HD), ALU.mult)
                    last.then_inc(xa_ready, 1)
                need(dve, o_psum, t, 1, 0)
                dve.tensor_tensor(o[:, :, :], ps_t[:, :, :].rearrange("p k (m n) -> p (k m) n", m=2)[:, :, 0:C],
                                  b2[:, 0:1, :].broadcast_to([P, J, C]), ALU.add)
                dve.drain()
                for n, (lo, hi) in enumerate(BANDS):
                    dve.tensor_tensor(o[:, :, lo:hi], o[:, :, lo:hi], bc(bands[:, 1, blocks, n], hi - lo), ALU.mult)
                dve.drain()
                dve.tensor_tensor(o[:, :, :], o[:, :, :], x1[:, blocks, :], ALU.add)
                dve.drain()
                dve.tensor_tensor(kit.h[:, blocks, :], kit.h[:, blocks, :], o[:, :, :], ALU.add).then_inc(h_done, 1)

        @block.tensor
        def _(pe):
            pe.wait_ge(loaded, 96)
            pe.wait_ge(w2_ready, 1)

            def turn(t):
                def maxima(n):
                    h, j = n // J, n % J
                    if n < 2:
                        need(pe, v_ready, t, J, 2 + n)
                    elif NM <= n < NM + 2:
                        need(pe, mlp_ready, t, FC1_TILES, FC1_TILES - 2 + n - NM)
                    else:
                        need(pe, m_read, t, NS, n, ago=2)
                    pe.matmul(ps_m[:, n % 2, :], qT[0:STACK, h, j * P:(j + 1) * P], kT[0:STACK, h, :],
                              start=True, stop=True).then_inc(m_psum, 1)

                def max_transpose(g):
                    need(pe, mx_ready, t, G3, g)
                    if g == 0:
                        need(pe, yT_ready, t, 1, 0)
                    else:
                        need(pe, mxT_ready, t, G3, g, ago=1)
                    pe.transpose(ps_t[0:4 * J, 1, 0:P], neg_max[:, 4 * g:4 * g + 4, :], kit.ident[:, :])\
                      .then_inc(mxT_psum, 1)

                def scores(grp):
                    g, kc = grp // J, grp % J
                    for i in range(4):
                        n = 4 * grp + i
                        if n < 2:
                            need(pe, st_read, t, NT, NT - 2 + n)
                        else:
                            need(pe, e_ready, t, NS, n, ago=2)
                        if kc == 0 and i == 0:
                            pe.wait_ge(max_placed[g], t * 16 + 16)
                        pe.matmul(ps_s[:, n % 2, :], kT[:, 4 * g + i, kc * P:(kc + 1) * P], qT[:, 4 * g + i, :],
                                  start=True, stop=True).then_inc(s_psum, 1)

                def weigh(grp):
                    g, kc = grp // J, grp % J
                    need(pe, e_ready, t, NS, 4 * grp + 3)
                    if kc == 0:
                        need(pe, a_read, t, G3, g, ago=1 if g == 0 else 2)
                    for i in range(4):
                        last = pe.matmul(ps_a[32 * i:32 * i + 32, g % 2, :], v[:, kc, 4 * g + i, :],
                                         e[:, (4 * grp + i) % LIVE_E, :], start=kc == 0, stop=kc == J - 1,
                                         tile_position=(0, 32 * i))
                    last.then_inc(av_done, 1)

                def att_transpose(g):
                    need(pe, a_read, t, G3, g)
                    if g == 1:
                        need(pe, mxT_ready, t, G3, G3 - 1)
                    if g == 2:
                        need(pe, xa_ready, t, G3, 0)
                    for j in range(J):
                        last = pe.transpose(ps_t[:, g % 2, j * P:(j + 1) * P], att[:, g % 2, j * P:(j + 1) * P],
                                            kit.ident[:, :])
                    last.then_inc(at_psum, 1)

                need(pe, y_ready, t, 1, 0)
                need(pe, h_done, t, 1, 0, ago=1)
                for j in range(J):
                    for c in range(2):
                        last = pe.transpose(ps_t[0:CH + c, c, j * P:(j + 1) * P], y[:, j, c * CH:(c + 1) * CH + c],
                                            kit.ident[:, :])
                last.then_inc(yT_psum, 1)
                need(pe, yT_ready, t, 1, 0)
                for j in range(J):
                    if j < 2:
                        need(pe, m_read, t, NS, j, ago=2)
                    else:
                        need(pe, qk_read, t, J, j, ago=2)
                    for c in range(2):
                        last = pe.matmul(ps_m[:, j % 2, 0:2 * C], yT[0:CH + c, c, j * P:(j + 1) * P],
                                         w1[0:CH + c, c, MLP:MLP + 2 * C], start=c == 0, stop=c == 1)
                    last.then_inc(qk_psum, 1)
                for j in range(J):
                    if j < 2:
                        need(pe, qk_read, t, J, j + 2)
                    else:
                        need(pe, v_ready, t, J, j, ago=2)
                    for c in range(2):
                        last = pe.matmul(ps_m[:, j % 2, 0:C], yT[0:CH + c, c, j * P:(j + 1) * P],
                                         w1[0:CH + c, c, MLP + 2 * C:], start=c == 0, stop=c == 1)
                    last.then_inc(v_psum, 1)
                for n in range(NT):
                    j, w, half = n // 4, n // 2 % 2, n % 2
                    need(pe, stack_ready, t, J, j)
                    if n < 2:
                        need(pe, e_ready, t, NS, n, ago=2)
                    else:
                        need(pe, st_read, t, NT, n, ago=2)
                    out16 = ps_s[:, n % 2, :].bitcast(BF16)
                    for i in range(HH):
                        last = pe.transpose(out16[0:STACK, i * P:(i + 1) * P], stacked[:, j % 2, w, half * HH + i, :],
                                            kit.ident16[:, :])
                    last.then_inc(st_psum, 1)
                need(pe, st_read, t, NT, NT - 1)
                for n in range(NM):
                    maxima(n)
                max_transpose(0)
                for m in range(FC1_TILES):
                    if m < 2:
                        need(pe, m_read, t, NS, NM - 2 + m)
                    else:
                        need(pe, mlp_ready, t, FC1_TILES, m, ago=2)
                    for c in range(2):
                        last = pe.matmul(ps_m[:, m % 2, :], w1[0:CH + c, c, m * P:(m + 1) * P], yT[0:CH + c, c, :],
                                         start=c == 0, stop=c == 1)
                    last.then_inc(mlp_psum, 1)
                for grp in range(G3 * J + 1):
                    if grp < G3 * J:
                        scores(grp)
                        if grp // J < G3 - 1:
                            for n in range(NM + 4 * grp, NM + 4 * grp + 4):
                                maxima(n)
                    if grp >= 1:
                        weigh(grp - 1)
                    if grp % J == J - 1 and grp // J < G3 - 1:
                        max_transpose(grp // J + 1)
                    if grp >= J + 2 and (grp - 2) % J == 0:
                        att_transpose((grp - 2) // J - 1)
                att_transpose(G3 - 1)
                need(pe, xa_ready, t, G3, G3 - 1)
                for j in range(J):
                    for c in range(2):
                        last = pe.transpose(ps_t[0:CH, c, j * P:(j + 1) * P], xa[:, j, c * CH:(c + 1) * CH],
                                            kit.ident[:, :])
                last.then_inc(xaT_psum, 1)
                need(pe, xaT_ready, t, 1, 0)
                for j in range(J):
                    out_j = ps_t[:, j // 2, (j % 2) * 256:(j % 2) * 256 + C]
                    for m in range(FC1_TILES):
                        pe.matmul(out_j, mlp[:, m, j * P:(j + 1) * P], w2_mlp[:, m, 0, :], start=m == 0, stop=False)
                    for c in range(2):
                        last = pe.matmul(out_j, xaT[:, c, j * P:(j + 1) * P], w2_att[:, c, 0, :], start=False,
                                         stop=c == 1)
                last.then_inc(o_psum, 1)

            with pe.Fori(0, B) as t:
                turn(t)

        @block.scalar
        def _(act):
            with act.Fori(0, B) as t:
                need(act, yT_psum, t, 1, 0)
                act.activation(yT[0:CH, 0, :], ps_t[0:CH, 0, :], ACT.Copy)
                act.activation(yT[:, 1, :], ps_t[0:CH + 1, 1, :], ACT.Copy).then_inc(yT_ready, 1)
                for n in range(NT):
                    j, w, half = n // 4, n // 2 % 2, n % 2
                    need(act, st_psum, t, NT, n)
                    act.activation((qT, kT)[w][0:STACK, half * HH:(half + 1) * HH, j * P:(j + 1) * P],
                                   ps_s[0:STACK, n % 2, :].bitcast(BF16)[:, 0:HH * P].rearrange(
                                       "p (h n) -> p h n", h=HH), ACT.Copy).then_inc(st_read, 1)
                for m in range(FC1_TILES):
                    need(act, mlp_psum, t, FC1_TILES, m)
                    if m == 0:
                        need(act, o_psum, t, 1, 0, ago=1)
                    act.activation(mlp[:, m, :], ps_m[:, m % 2, :], ACT.Gelu).then_inc(mlp_ready, 1)
                for n in range(NS):
                    grp = n // 4
                    need(act, s_psum, t, NS, n)
                    if n % 4 == 0:
                        need(act, av_done, t, G3 * J, grp, ago=2)
                    act.activation(e[:, n % LIVE_E, :], ps_s[:, n % 2, :], ACT.Exp, scale=QSCALE).then_inc(e_ready, 1)
                    if n % NM == 7 and n > NM or n == NS - 1:
                        for g in ([n // NM - 1] if n < NS - 1 else [G3 - 1]):
                            need(act, av_done, t, G3 * J, J * g + J - 1)
                            need(act, at_psum, t, G3, g, ago=2)
                            act.activation(att[:, g % 2, :], ps_a[:, g % 2, :], ACT.Copy).then_inc(a_read, 1)
                need(act, xaT_psum, t, 1, 0)
                act.activation(xaT[:, :, :], ps_t[0:CH, :, :], ACT.Copy).then_inc(xaT_ready, 1)


DI = 2 * C
NH, HP = 6, DI // 6
DS = 64
TAPS = 4
ZW = DI + NH
KD = DI // P
LOWEST_LOG = -1e30


def rows_of(ps_pair):
    return ps_pair[:, :, :].rearrange("p k (m n) -> p (k m) n", m=2)


def state_space_block(kit, a):
    nc = kit.nc
    with kit.phase() as ctx:
        sb, ps = tile_maker(nc, ctx), psum_maker(nc, ctx)
        ln = sb("ln", [P, 4, C])
        wz = sb("wz", [CH, 2, ZW])
        wx = sb("wx", [CH, 2, 4 * P])
        conv_w = sb("conv_w", [P, 4, TAPS])
        conv_b = sb("conv_b", [P, 4])
        dt_bias = sb("dt_bias", [P, NH])
        neg_a = sb("neg_a", [P, NH])
        d_skip = sb("d_skip", [P, NH])
        norm_w = sb("norm_w", [P, DI])
        w_out = sb("w_out", [P, KD, C])
        wf1 = sb("wf1", [CH, 2, 6 * P])
        wf2 = sb("wf2", [P, KD, C])
        upto = sb("upto", [P, P])
        after16 = sb("after16", [P, P], BF16)
        ones = sb("d_ones", [P, P])
        stats = sb("d_stats", [P, J, 6])
        mv = sb("d_mv", [P, J, 2])
        var_eps = sb("d_var_eps", [P, J])
        rstd = sb("d_rstd", [P, J])
        xm = sb("xm", [P, J, C])
        y = sb("d_y", [P, J, C])
        yT = sb("d_yT", [CH, 2, T])
        silu_z = sb("silu_z", [P, J, DI])
        dt_raw = sb("dt_raw", [P, J, NH])
        dt = sb("dt", [P, J, NH])
        dt_pos = sb("dt_pos", [P, J, NH])
        dt_e = sb("dt_e", [P, J, NH])
        dt_u = sb("dt_u", [P, J, NH])
        dt_d = sb("dt_d", [P, J, NH])
        dt_l = sb("dt_l", [P, J, NH])
        log_a = sb("log_a", [P, J, NH])
        sums = sb("sums", [P, 3, J, NH])
        neg_cs = sb("neg_cs", [P, J, NH])
        decays = sb("decays", [P, 3, J, NH])
        xin = sb("xin", [P, 4, TAPS - 1 + T])
        conv = sb("conv", [P, 4, T])
        c_low = sb("c_low", [DS, T])
        x_tm = sb("x_tm", [P, J, 4 * P])
        dtx = sb("dtx", [P, J, DI])
        dtx_rest = sb("dtx_rest", [P, J, DI])
        x_skip = sb("x_skip", [P, J, DI])
        seg = sb("seg", [P, J, NH, P])
        state = sb("state", [DS, DI])
        yy = sb("yy", [P, J, DI])
        square = sb("square", [P, DI])
        ms = sb("ms", [P, J])
        rms = sb("rms", [P, J])
        yyT = sb("yyT", [P, KD, T])
        x2 = sb("x2", [P, J, C])
        gate = sb("d_gate", [P, T])
        f = sb("f", [P, KD, T])
        ps_t = ps("d_ps_t", [P, 2, T])
        ps_m = ps("d_ps_m", [P, 2, T])
        ps_cb = ps("d_ps_cb", [P, J, P])
        ps_y = ps("d_ps_y", [P, T])
        ps_z = ps("d_ps_z", [P, T])
        ps_s = ps("d_ps_s", [P, T])
        names = ("var_ready rstd_ready y_ready yT_psum yT_ready z_psum z_read dt_read x_psum x_read conv_ready "
                 "silu_ready abs_ready e_ready u_ready l_ready log_ready sums_psum sums_ready decays_ready row_psum "
                 "seg_ready xtm_psum xtm_ready cb_psum dtx_ready skip_ready mt_ready diag_psum off_psum new_psum "
                 "state_ready chunk_ready square_ready ms_ready rms_ready norm_ready yyT_psum yyT_ready x2_psum "
                 "g_psum a_psum g_ready f_ready o_psum h_done")
        s = {n: kit.sem("d_" + n) for n in names.split()}
        loaded, tri_made, consts, a_exp = kit.sems("d_loaded d_tri_made d_consts d_a_exp")
        c_moved = kit.sem("d_c_moved")
        LOADS = 12
        block = ctx.enter_context(nc.Block())

        @block.sync
        def _(sp):
            for x in s.values():
                sp.sem_inc(x, U)
            for dst, src in ((ln[:, :, :], a["ln12"].broadcast_to([P, 4, C])), (wz[:, :, :], a["wz"]),
                             (wx[:, :, :], a["wx"]), (conv_w[:, :, :], a["conv_w"]), (conv_b[:, :], a["conv_b"]),
                             (dt_bias[:, :], a["dt_bias"].broadcast_to([P, NH])),
                             (neg_a[:, :], a["a_log"].broadcast_to([P, NH])),
                             (d_skip[:, :], a["d_skip"].broadcast_to([P, NH])),
                             (norm_w[:, :], a["norm_w"].broadcast_to([P, DI])), (w_out[:, :, :], a["w_out"]),
                             (wf1[:, :, :], a["wf1"]), (wf2[:, :, :], a["wf2"])):
                sp.dma_start(dst, src).then_inc(loaded, 16)
            with sp.Fori(0, B) as t:
                need(sp, s["silu_ready"], t, 4, 3)
                sp.dma_start(c_low[:, :], conv[DS:P, 3, :]).then_inc(c_moved, 16)

        @block.gpsimd
        def _(pool):
            pool.memset(ones[:, :], 1.0).then_inc(tri_made, 1)
            pool.memset(after16[:, :], 0.0).then_inc(tri_made, 1)
            pool.wait_ge(tri_made, 2)
            pool.affine_select(out=upto[:, :], in_=ones[:, :], compare_op=ALU.is_ge, fill=0.0, base=0,
                               pattern=[[1, P]], channel_multiplier=-1).then_inc(consts, 1)
            pool.affine_select(out=after16[:, :], in_=after16[:, :], compare_op=ALU.is_ge, fill=LOWEST_LOG, base=0,
                               pattern=[[1, P]], channel_multiplier=-1).then_inc(consts, 1)
            with pool.Fori(0, B) as t:
                for k in range(3):
                    if k == 2:
                        for j in range(J):
                            need(pool, s["xtm_ready"], t, J, j)
                            pool.tensor_tensor(x_skip[:, j].rearrange("p (h d) -> p h d", h=NH),
                                               x_tm[:, j, 0:DI].rearrange("p (h d) -> p h d", h=NH),
                                               bc(d_skip[:, :], HP), ALU.mult).then_inc(s["skip_ready"], 1)
                        need(pool, s["ms_ready"], t, 1, 0)
                        pool.tensor_tensor(rms[:, :], ms[:, :], kit.minus_half[:, 0:J], ALU.pow)\
                            .then_inc(s["rms_ready"], 1)
                    need(pool, s["var_ready"], t, 3, k)
                    ln_rstd(kit, pool, rstd[:, :], var_eps[:, :]).then_inc(s["rstd_ready"], 1)

        @block.vector
        def _(dve):
            dve.memset(xin[:, :, 0:TAPS - 1], 0.0)
            dve.wait_ge(loaded, 16 * LOADS)
            dve.wait_ge(a_exp, 1)
            dve.tensor_scalar(neg_a[:, :], neg_a[:, :], -1.0, None, ALU.mult)

            def affine(dst, k):
                dve.drain()
                dve.tensor_tensor(dst, dst, ln[:, 2 * k:2 * k + 1, :].broadcast_to([P, J, C]), ALU.mult)
                dve.drain()
                return dve.tensor_tensor(dst, dst, ln[:, 2 * k + 1:2 * k + 2, :].broadcast_to([P, J, C]), ALU.add)

            with dve.Fori(0, B) as t:
                blocks = bass.ds(t * J, J)
                dve.drain()
                ln_stats(dve, kit.h[:, blocks, :], stats, mv, var_eps, 1e-5).then_inc(s["var_ready"], 1)
                need(dve, s["rstd_ready"], t, 3, 0)
                ln_apply(dve, xm, kit.h[:, blocks, :], mv, rstd)
                dve.drain()
                ln_stats(dve, xm, stats, mv, var_eps, 1e-5).then_inc(s["var_ready"], 1)
                need(dve, s["rstd_ready"], t, 3, 1)
                ln_apply(dve, y, xm, mv, rstd)
                affine(y[:, :, :], 0).then_inc(s["y_ready"], 1)
                for j in range(J):
                    need(dve, s["z_read"], t, J, j)
                    last = dve.tensor_tensor(dt[:, j, :], dt_raw[:, j, :], dt_bias[:, :], ALU.add)
                last.then_inc(s["dt_read"], 1)
                dve.drain()
                dve.tensor_scalar(dt_pos[:, :, :], dt[:, :, :], 0.0, None, ALU.max)
                dve.tensor_scalar(dt_d[:, :, :], dt[:, :, :], -1.0, None, ALU.mult)
                dve.drain()
                dve.tensor_tensor(dt_e[:, :, :], dt[:, :, :], dt_d[:, :, :], ALU.min).then_inc(s["abs_ready"], 1)
                for m in range(4):
                    need(dve, s["x_read"], t, 4, m)
                    dve.tensor_scalar(conv[:, m, :], xin[:, m, 0:T], conv_w[:, m, 0:1], conv_b[:, m:m + 1],
                                      ALU.mult, ALU.add)
                    for k in range(1, TAPS):
                        dve.drain()
                        last = dve.scalar_tensor_tensor(out=conv[:, m, :], in0=xin[:, m, k:k + T],
                                                        scalar=conv_w[:, m, k:k + 1], in1=conv[:, m, :],
                                                        op0=ALU.mult, op1=ALU.add)
                    last.then_inc(s["conv_ready"], 1)
                need(dve, s["e_ready"], t, 1, 0)
                dve.tensor_scalar(dt_u[:, :, :], dt_e[:, :, :], 1.0, None, ALU.add).then_inc(s["u_ready"], 1)
                dve.drain()
                dve.tensor_scalar(dt_d[:, :, :], dt_u[:, :, :], 1.0, None, ALU.subtract)
                dve.drain()
                dve.tensor_scalar(dt[:, :, :], dt_d[:, :, :], 0.0, None, ALU.is_equal)
                dve.tensor_scalar(dt_d[:, :, :], dt_d[:, :, :], 1e-30, None, ALU.max)
                dve.drain()
                dve.reciprocal(dt_d[:, :, :], dt_d[:, :, :])
                dve.drain()
                need(dve, s["l_ready"], t, 1, 0)
                dve.tensor_tensor(dt_d[:, :, :], dt_d[:, :, :], dt_l[:, :, :], ALU.mult)
                dve.drain()
                dve.tensor_tensor(dt_d[:, :, :], dt_d[:, :, :], dt[:, :, :], ALU.add)
                dve.drain()
                dve.tensor_tensor(dt_d[:, :, :], dt_d[:, :, :], dt_e[:, :, :], ALU.mult)
                dve.drain()
                dve.tensor_tensor(dt[:, :, :], dt_d[:, :, :], dt_pos[:, :, :], ALU.add)
                dve.drain()
                dve.tensor_tensor(log_a[:, :, :], dt[:, :, :], neg_a[:, :].unsqueeze(1).broadcast_to([P, J, NH]), ALU.mult)
                dve.drain()
                dve.tensor_scalar(log_a[:, :, :], log_a[:, :, :], LOWEST_LOG, None, ALU.max).then_inc(s["log_ready"], 1)
                need(dve, s["sums_psum"], t, 1, 0)
                got = ps_s[:, DI:DI + 2 * J * NH].rearrange("p (w j h) -> p w j h", w=2, j=J)
                dve.tensor_copy(sums[:, 0:2], got)
                dve.drain()
                dve.tensor_scalar(neg_cs[:, :, :], sums[:, 0], -1.0, None, ALU.mult)
                dve.tensor_tensor(sums[:, 2], sums[:, 1], sums[:, 0], ALU.subtract).then_inc(s["sums_ready"], 1)
                need(dve, s["decays_ready"], t, 1, 0)
                by_head = lambda x: x.rearrange("p (h d) -> p h d", h=NH)
                for j in range(J):
                    need(dve, s["xtm_ready"], t, J, j)
                    dve.tensor_tensor(by_head(dtx[:, j]), by_head(x_tm[:, j, 0:DI]), bc(dt[:, j, :], HP), ALU.mult)
                    dve.drain()
                    dve.tensor_tensor(by_head(dtx_rest[:, j]), by_head(dtx[:, j]), bc(decays[:, 2, j, :], HP), ALU.mult)\
                       .then_inc(s["dtx_ready"], 1)
                need(dve, s["cb_psum"], t, 1, 0)
                for j in range(J):
                    need(dve, s["seg_ready"], t, 2 * J, 2 * j + 1)
                    dve.tensor_tensor(seg[:, j], seg[:, j], ps_cb[:, j:j + 1, :].broadcast_to([P, NH, P]), ALU.mult)\
                       .then_inc(s["mt_ready"], 1)
                for j in range(J):
                    if j < J - 1:
                        need(dve, s["new_psum"], t, J - 1, j)
                        if j > 0:
                            need(dve, s["off_psum"], t, J - 1, j - 1)
                            dve.tensor_tensor(by_head(state[:, :]), by_head(state[:, :]),
                                              bc(decays[0:DS, 1, j, :], HP), ALU.mult)
                            dve.drain()
                            dve.tensor_tensor(state[:, :], state[:, :], ps_s[0:DS, 0:DI], ALU.add)\
                               .then_inc(s["state_ready"], 1)
                        else:
                            dve.tensor_copy(state[:, :], ps_s[0:DS, 0:DI]).then_inc(s["state_ready"], 1)
                    need(dve, s["diag_psum"], t, J, j)
                    need(dve, s["skip_ready"], t, J, j)
                    dve.tensor_tensor(x_skip[:, j], x_skip[:, j], ps_y[:, 0:DI], ALU.add)
                    if j > 0:
                        need(dve, s["off_psum"], t, J - 1, j - 1)
                        dve.tensor_tensor(by_head(yy[:, j]), by_head(ps_z[:, 0:DI]), bc(decays[:, 0, j, :], HP), ALU.mult)
                        dve.drain()
                        dve.tensor_tensor(x_skip[:, j], x_skip[:, j], yy[:, j], ALU.add)
                    dve.drain()
                    dve.tensor_tensor(yy[:, j], x_skip[:, j], silu_z[:, j], ALU.mult).then_inc(s["chunk_ready"], 1)
                need(dve, s["square_ready"], t, J, J - 1)
                dve.tensor_scalar(ms[:, :], ms[:, :], 1.0 / DI, 1e-5, ALU.mult, ALU.add).then_inc(s["ms_ready"], 1)
                need(dve, s["rms_ready"], t, 1, 0)
                for j in range(J):
                    dve.scalar_tensor_tensor(out=yy[:, j], in0=yy[:, j], scalar=rms[:, j:j + 1], in1=norm_w[:, :],
                                             op0=ALU.mult, op1=ALU.mult).then_inc(s["norm_ready"], 1)
                need(dve, s["x2_psum"], t, 1, 0)
                dve.tensor_tensor(x2[:, :, :], rows_of(ps_t)[:, :, 0:C], xm[:, :, :], ALU.add)
                dve.drain()
                ln_stats(dve, x2, stats, mv, var_eps, 1e-5).then_inc(s["var_ready"], 1)
                need(dve, s["rstd_ready"], t, 3, 2)
                ln_apply(dve, y, x2, mv, rstd)
                affine(y[:, :, :], 1).then_inc(s["y_ready"], 1)
                for m in range(KD):
                    need(dve, s["a_psum"], t, KD, m)
                    need(dve, s["g_ready"], t, KD, m)
                    dve.tensor_tensor(f[:, m, :], ps_m[:, 1, :], gate[:, :], ALU.mult).then_inc(s["f_ready"], 1)
                need(dve, s["o_psum"], t, 1, 0)
                dve.tensor_tensor(x2[:, :, :], x2[:, :, :], rows_of(ps_t)[:, :, 0:C], ALU.add)
                dve.drain()
                dve.tensor_tensor(kit.h[:, blocks, :], kit.h[:, blocks, :], x2[:, :, :], ALU.add)\
                   .then_inc(s["h_done"], 1)

        @block.tensor
        def _(pe):
            pe.wait_ge(loaded, 16 * LOADS)
            pe.wait_ge(consts, 2)

            def turn_rows(k):
                for j in range(J):
                    for c in range(2):
                        last = pe.transpose(ps_t[0:CH, c, j * P:(j + 1) * P], y[:, j, c * CH:(c + 1) * CH],
                                            kit.ident[:, :])
                last.then_inc(s["yT_psum"], 1)

            with pe.Fori(0, B) as t:
                need(pe, s["y_ready"], t, 2, 0)
                need(pe, s["h_done"], t, 1, 0, ago=1)
                turn_rows(0)
                need(pe, s["yT_ready"], t, 2, 0)
                for j in range(J):
                    if j < 2:
                        need(pe, s["f_ready"], t, KD, 0, ago=1)
                    else:
                        need(pe, s["z_read"], t, J, j, ago=2)
                    for c in range(2):
                        last = pe.matmul(ps_m[:, j % 2, 0:ZW], yT[:, c, j * P:(j + 1) * P], wz[:, c, :],
                                         start=c == 0, stop=c == 1)
                    last.then_inc(s["z_psum"], 1)
                for m in range(4):
                    if m < 2:
                        need(pe, s["z_read"], t, J, J - 2 + m)
                    else:
                        need(pe, s["x_read"], t, 4, m, ago=2)
                    for c in range(2):
                        last = pe.matmul(ps_m[:, m % 2, :], wx[:, c, m * P:(m + 1) * P], yT[:, c, :],
                                         start=c == 0, stop=c == 1)
                    last.then_inc(s["x_psum"], 1)
                need(pe, s["log_ready"], t, 1, 0)
                flat = log_a[:, :, :].rearrange("p j h -> p (j h)")
                pe.matmul(ps_s[:, DI:DI + J * NH], upto[:, :], flat, start=True, stop=True)
                pe.matmul(ps_s[:, DI + J * NH:DI + 2 * J * NH], ones[:, :], flat, start=True, stop=True)\
                  .then_inc(s["sums_psum"], 1)
                for n in range(2 * J):
                    j, half = n // 2, n % 2
                    if n >= 2:
                        need(pe, s["seg_ready"], t, 2 * J, n, ago=2)
                    for i in range(3):
                        dst = ps_t[:, half, i * P:(i + 1) * P]
                        pe.matmul(dst, log_a[:, j, 3 * half + i:3 * half + i + 1].broadcast_to([P, P]), upto[:, :],
                                  start=True, stop=False)
                        last = pe.matmul(dst, kit.ident16[:, :], after16[:, :], start=False, stop=True)
                    last.then_inc(s["row_psum"], 1)
                for j in range(J):
                    if j == 0:
                        need(pe, s["silu_ready"], t, 4, 3)
                    if j < 2:
                        need(pe, s["x_read"], t, 4, 2 + j)
                    else:
                        need(pe, s["xtm_ready"], t, J, j, ago=2)
                    for m in range(4):
                        last = pe.transpose(ps_m[:, j % 2, m * P:(m + 1) * P], conv[:, m, j * P:(j + 1) * P],
                                            kit.ident[:, :])
                    last.then_inc(s["xtm_psum"], 1)
                pe.wait_ge(c_moved, t * 16 + 16)
                for j in range(J):
                    last = pe.matmul(ps_cb[:, j, :], conv[0:DS, 3, j * P:(j + 1) * P], c_low[:, j * P:(j + 1) * P],
                                     start=True, stop=True)
                last.then_inc(s["cb_psum"], 1)
                for j in range(J):
                    need(pe, s["dtx_ready"], t, J, j)
                    if j < J - 1:
                        if j > 0:
                            need(pe, s["state_ready"], t, J - 1, j - 1)
                        pe.matmul(ps_s[0:DS, 0:DI], x_tm[:, j, DI:DI + DS], dtx_rest[:, j, :], start=True, stop=True)\
                          .then_inc(s["new_psum"], 1)
                    need(pe, s["mt_ready"], t, J, j)
                    if j > 0:
                        need(pe, s["chunk_ready"], t, J, j - 1)
                    for h in range(NH):
                        last = pe.matmul(ps_y[:, h * HP:(h + 1) * HP], seg[:, j, h, :], dtx[:, j, h * HP:(h + 1) * HP],
                                         start=True, stop=True)
                    last.then_inc(s["diag_psum"], 1)
                    if j > 0:
                        need(pe, s["state_ready"], t, J - 1, j - 1)
                        pe.matmul(ps_z[:, 0:DI], c_low[:, j * P:(j + 1) * P], state[:, :], start=True, stop=True)\
                          .then_inc(s["off_psum"], 1)
                for j in range(J):
                    need(pe, s["norm_ready"], t, J, j)
                    if j >= 2:
                        need(pe, s["yyT_ready"], t, J, j, ago=2)
                    for m in range(KD):
                        last = pe.transpose(ps_m[:, j % 2, m * P:(m + 1) * P], yy[:, j, m * P:(m + 1) * P],
                                            kit.ident[:, :])
                    last.then_inc(s["yyT_psum"], 1)
                need(pe, s["yyT_ready"], t, J, J - 1)
                for j in range(J):
                    for m in range(KD):
                        last = pe.matmul(rows_of(ps_t)[:, j, 0:C], yyT[:, m, j * P:(j + 1) * P], w_out[:, m, :],
                                         start=m == 0, stop=m == KD - 1)
                last.then_inc(s["x2_psum"], 1)
                need(pe, s["y_ready"], t, 2, 1)
                turn_rows(1)
                need(pe, s["yT_ready"], t, 2, 1)
                for m in range(KD):
                    if m == 0:
                        need(pe, s["yyT_ready"], t, J, J - 1)
                    else:
                        need(pe, s["g_ready"], t, KD, m - 1)
                    for c in range(2):
                        last = pe.matmul(ps_m[:, 0, :], wf1[:, c, (KD + m) * P:(KD + m + 1) * P], yT[:, c, :],
                                         start=c == 0, stop=c == 1)
                    last.then_inc(s["g_psum"], 1)
                    if m > 0:
                        need(pe, s["f_ready"], t, KD, m - 1)
                    for c in range(2):
                        last = pe.matmul(ps_m[:, 1, :], wf1[:, c, m * P:(m + 1) * P], yT[:, c, :],
                                         start=c == 0, stop=c == 1)
                    last.then_inc(s["a_psum"], 1)
                need(pe, s["f_ready"], t, KD, KD - 1)
                for j in range(J):
                    for m in range(KD):
                        last = pe.matmul(rows_of(ps_t)[:, j, 0:C], f[:, m, j * P:(j + 1) * P], wf2[:, m, :],
                                         start=m == 0, stop=m == KD - 1)
                last.then_inc(s["o_psum"], 1)

        @block.scalar
        def _(act):
            act.wait_ge(loaded, 16 * LOADS)
            act.activation(neg_a[:, :], neg_a[:, :], ACT.Exp).then_inc(a_exp, 1)

            with act.Fori(0, B) as t:
                need(act, s["yT_psum"], t, 2, 0)
                act.activation(yT[:, :, :], ps_t[0:CH, :, :], ACT.Copy).then_inc(s["yT_ready"], 1)
                for j in range(J):
                    need(act, s["z_psum"], t, J, j)
                    if j == 0:
                        need(act, s["dt_read"], t, 1, 0, ago=1)
                    act.activation(dt_raw[:, j], ps_m[:, j % 2, DI:ZW], ACT.Copy)
                    act.activation(silu_z[:, j], ps_m[:, j % 2, 0:DI], ACT.Silu).then_inc(s["z_read"], 1)
                for m in range(4):
                    need(act, s["x_psum"], t, 4, m)
                    act.activation(xin[:, m, TAPS - 1:], ps_m[:, m % 2, :], ACT.Copy).then_inc(s["x_read"], 1)
                for m in range(4):
                    need(act, s["conv_ready"], t, 4, m)
                    act.activation(conv[:, m, :], conv[:, m, :], ACT.Silu).then_inc(s["silu_ready"], 1)
                need(act, s["abs_ready"], t, 1, 0)
                act.activation(dt_e[:, :, :], dt_e[:, :, :], ACT.Exp).then_inc(s["e_ready"], 1)
                need(act, s["u_ready"], t, 1, 0)
                act.activation(dt_l[:, :, :], dt_u[:, :, :], ACT.Ln).then_inc(s["l_ready"], 1)
                need(act, s["sums_ready"], t, 1, 0)
                act.activation(decays[:, :, :, :], sums[:, :, :, :], ACT.Exp).then_inc(s["decays_ready"], 1)
                for n in range(2 * J):
                    j, half = n // 2, n % 2
                    need(act, s["row_psum"], t, 2 * J, n)
                    for i in range(3):
                        h = 3 * half + i
                        last = act.activation(seg[:, j, h, :], ps_t[:, half, i * P:(i + 1) * P], ACT.Exp,
                                              bias=neg_cs[:, j, h:h + 1])
                    last.then_inc(s["seg_ready"], 1)
                for j in range(J):
                    need(act, s["xtm_psum"], t, J, j)
                    act.activation(x_tm[:, j, :], ps_m[:, j % 2, :], ACT.Copy).then_inc(s["xtm_ready"], 1)
                for j in range(J):
                    act.drain()
                    need(act, s["chunk_ready"], t, J, j)
                    act.activation(square[:, :], yy[:, j], ACT.Square, accum_out=ms[:, j:j + 1])\
                       .then_inc(s["square_ready"], 1)
                for j in range(J):
                    need(act, s["yyT_psum"], t, J, j)
                    act.activation(yyT[:, :, j * P:(j + 1) * P], ps_m[:, j % 2, 0:DI].rearrange(
                        "p (m n) -> p m n", m=KD), ACT.Copy).then_inc(s["yyT_ready"], 1)
                need(act, s["yT_psum"], t, 2, 1)
                act.activation(yT[:, :, :], ps_t[0:CH, :, :], ACT.Copy).then_inc(s["yT_ready"], 1)
                for m in range(KD):
                    need(act, s["g_psum"], t, KD, m)
                    if m > 0:
                        need(act, s["f_ready"], t, KD, m - 1)
                    act.activation(gate[:, :], ps_m[:, 0, :], ACT.Silu).then_inc(s["g_ready"], 1)


E8 = 8
INNER = 4 * C
IT = INNER // P
CAP = 1280
SLOTS = E8 * CAP
NOWHERE = float(1 << 20)
LO = P // E8


def shared_expert_and_router(kit, a, x1, logits):
    nc = kit.nc
    with kit.phase() as ctx:
        sb, ps = tile_maker(nc, ctx), psum_maker(nc, ctx)
        wr = sb("wr", [CH, 2, E8])
        s1 = sb("s1", [CH, 2, INNER])
        s3 = sb("s3", [CH, 2, INNER])
        s2 = sb("s2", [P, IT, C])
        stats = sb("e_stats", [P, U, J, 6])
        mv = sb("e_mv", [P, U, J, 2])
        var_eps = sb("e_var_eps", [P, U, J])
        rstd = sb("e_rstd", [P, U, J])
        xn = sb("e_xn", [P, U, J, C])
        xT = sb("e_xT", [CH, U, 2, T])
        gate = sb("e_gate", [P, 2, T])
        f = sb("e_f", [P, U, IT, T])
        ps_t = ps("e_ps_t", [P, 2, T])
        ps_g = ps("e_ps_g", [P, 2, T])
        ps_u = ps("e_ps_u", [P, 2, T])
        ps_o = ps("e_ps_o", [P, 2, T])
        names = ("var_ready rstd_ready xn_ready x1_kept xT_psum xT_ready logit_psum logit_read g_psum g_ready u_psum "
                 "f_ready o_psum h_done")
        s = {n: kit.sem("e_" + n) for n in names.split()}
        loaded = kit.sem("e_loaded")
        block = ctx.enter_context(nc.Block())

        @block.sync
        def _(sp):
            for x in s.values():
                sp.sem_inc(x, U)
            for dst, src in ((wr[:, :, :], a["wr"]), (s1[:, :, :], a["s1"]), (s3[:, :, :], a["s3"]),
                             (s2[:, :, :], a["s2"])):
                sp.dma_start(dst, src).then_inc(loaded, 16)

        @block.gpsimd
        def _(pool):
            with pool.Fori(0, TURNS) as t:
                for u in range(U):
                    need(pool, s["var_ready"], t, U, u)
                    ln_rstd(kit, pool, rstd[:, u, :], var_eps[:, u, :]).then_inc(s["rstd_ready"], 1)
                for u in range(U):
                    need(pool, s["xn_ready"], t, U, u)
                    kit.apart(pool)
                    pool.tensor_copy(x1[:, bass.ds(t * (U * J) + u * J, J), :], xn[:, u]).then_inc(s["x1_kept"], 1)

        @block.vector
        def _(dve):
            with dve.Fori(0, TURNS) as t:
                for u in range(U):
                    dve.drain()
                    ln_stats(dve, kit.h[:, bass.ds(t * (U * J) + u * J, J), :], stats[:, u], mv[:, u],
                             var_eps[:, u], 1e-5).then_inc(s["var_ready"], 1)
                for u in range(U):
                    need(dve, s["rstd_ready"], t, U, u)
                    need(dve, s["xT_psum"], t, U, u, ago=U)
                    need(dve, s["x1_kept"], t, U, u, ago=U)
                    ln_apply(dve, xn[:, u], kit.h[:, bass.ds(t * (U * J) + u * J, J), :], mv[:, u],
                             rstd[:, u]).then_inc(s["xn_ready"], 1)
                for u in range(U):
                    need(dve, s["logit_psum"], t, U, u)
                    dve.tensor_copy(logits[:, bass.ds(t * (U * J) + u * J, J), :],
                                    ps_t[:, 0, 0:J * E8].rearrange("p (j e) -> p j e", j=J)).then_inc(s["logit_read"], 1)
                for u in range(U):
                    need(dve, s["o_psum"], t, U, u, ago=U)
                    for m in range(IT):
                        need(dve, s["g_ready"], t, U * IT, u * IT + m)
                        need(dve, s["u_psum"], t, U * IT, u * IT + m)
                        dve.tensor_tensor(f[:, u, m, :], ps_u[:, m % 2, :], gate[:, m % 2, :], ALU.mult)\
                           .then_inc(s["f_ready"], 1)
                for u in range(U):
                    need(dve, s["o_psum"], t, U, u)
                    blocks = bass.ds(t * (U * J) + u * J, J)
                    dve.tensor_tensor(kit.h[:, blocks, :], kit.h[:, blocks, :], rows_of(ps_o)[:, :, 0:C], ALU.add)\
                       .then_inc(s["h_done"], 1)

        @block.tensor
        def _(pe):
            pe.wait_ge(loaded, 64)
            with pe.Fori(0, TURNS) as t:
                for u in range(U):
                    need(pe, s["xn_ready"], t, U, u)
                    need(pe, s["logit_read"], t, U, u, ago=1)
                    for j in range(J):
                        for c in range(2):
                            last = pe.transpose(ps_t[0:CH, c, j * P:(j + 1) * P], xn[:, u, j, c * CH:(c + 1) * CH],
                                                kit.ident[:, :])
                    last.then_inc(s["xT_psum"], 1)
                    need(pe, s["xT_ready"], t, U, u)
                    for j in range(J):
                        for c in range(2):
                            last = pe.matmul(ps_t[:, 0, j * E8:(j + 1) * E8], xT[:, u, c, j * P:(j + 1) * P],
                                             wr[:, c, :], start=c == 0, stop=c == 1)
                    last.then_inc(s["logit_psum"], 1)
                for u in range(U):
                    for m in range(IT):
                        n = u * IT + m
                        need(pe, s["g_ready"], t, U * IT, n, ago=2)
                        for c in range(2):
                            last = pe.matmul(ps_g[:, m % 2, :], s1[:, c, m * P:(m + 1) * P], xT[:, u, c, :],
                                             start=c == 0, stop=c == 1)
                        last.then_inc(s["g_psum"], 1)
                        need(pe, s["f_ready"], t, U * IT, n, ago=2)
                        for c in range(2):
                            last = pe.matmul(ps_u[:, m % 2, :], s3[:, c, m * P:(m + 1) * P], xT[:, u, c, :],
                                             start=c == 0, stop=c == 1)
                        last.then_inc(s["u_psum"], 1)
                for u in range(U):
                    need(pe, s["f_ready"], t, U * IT, u * IT + IT - 1)
                    need(pe, s["h_done"], t, U, u, ago=1)
                    for j in range(J):
                        for m in range(IT):
                            last = pe.matmul(rows_of(ps_o)[:, j, 0:C], f[:, u, m, j * P:(j + 1) * P], s2[:, m, :],
                                             start=m == 0, stop=m == IT - 1)
                    last.then_inc(s["o_psum"], 1)

        @block.scalar
        def _(act):
            with act.Fori(0, TURNS) as t:
                for u in range(U):
                    need(act, s["xT_psum"], t, U, u)
                    act.activation(xT[:, u], ps_t[0:CH, :, :], ACT.Copy).then_inc(s["xT_ready"], 1)
                for u in range(U):
                    for m in range(IT):
                        n = u * IT + m
                        need(act, s["g_psum"], t, U * IT, n)
                        need(act, s["f_ready"], t, U * IT, n, ago=2)
                        act.activation(gate[:, m % 2, :], ps_g[:, m % 2, :], ACT.Silu).then_inc(s["g_ready"], 1)


def choose_slots(kit, logits, weight, slot):
    nc = kit.nc
    with kit.phase() as ctx:
        sb, ps = tile_maker(nc, ctx), psum_maker(nc, ctx)
        V = [P, NB, E8]
        probs, probs2, mark8, rank8 = sb("r_probs", V), sb("r_probs2", V), sb("r_mark8", V), sb("r_rank8", V)
        hot = [sb("r_hot0", V), sb("r_hot1", V)]
        score = sb("r_score", V)
        order = sb("order", [P, E8])
        peak = sb("r_peak", [P, 2, NB])
        mass = sb("r_mass", [P, NB])
        slot_f = sb("slot_f", [P, 2, NB])
        rows = sb("r_rows", [P, 2, P])
        mark = sb("r_mark", [P, 2, P])
        tie = sb("r_tie", [P, 2, P])
        rank = sb("r_rank", [P, 2, P])
        ones = sb("r_ones", [P, P])
        same = sb("same", [P, P])
        before = sb("before", [P, P])
        hotT = sb("hotT", [E8, P])
        first_i = sb("first_i", [E8, 1], I32)
        first_f = sb("first_f", [E8, 1])
        first_slot = sb("first_slot", [P, 1])
        bits = sb("r_bits", [P, 1], I32)
        cand = sb("r_cand", [P, 1], I32)
        bit = sb("r_bit", [P, 1], I32)
        keep = sb("r_keep", [P, 1], I32)
        count = sb("r_count", [P, 1])
        room = sb("r_room", [P, 1])
        offset = sb("r_offset", [P, 2])
        ps_c = ps("r_ps_c", [P, 512])
        ps_r = ps("r_ps_r", [P, 2, P])
        ps_k = ps("r_ps_k", [P, 512])
        made, made_f, same_psum, same_ready, before_ready, shifted, exp_ready = kit.sems(
            "r_made r_made_f r_same_psum r_same_ready r_before_ready r_shifted r_exp_ready")
        score_ready, rows_psum, counted, total_ready, more_counted, more_total, slots_ready, slots_psum = kit.sems(
            "r_score_ready r_rows_psum r_counted r_total_ready r_more_counted r_more_total r_slots_ready r_slots_psum")
        block = ctx.enter_context(nc.Block())

        @block.gpsimd
        def _(pool):
            for e in range(E8):
                pool.memset(order[:, e:e + 1], float(E8 - e))
            pool.memset(ones[:, :], 1.0)
            pool.memset(hotT[:, :], 0.0).then_inc(made, 1)
            pool.wait_ge(made, 1)
            pool.affine_select(out=hotT[:, :].rearrange("e (b f) -> e b f", f=E8),
                               in_=hotT[:, :].rearrange("e (b f) -> e b f", f=E8), compare_op=ALU.not_equal,
                               fill=1.0, base=0, pattern=[[0, LO], [-1, E8]], channel_multiplier=1)
            pool.iota(first_i[:, :], pattern=[[0, 1]], base=-1, channel_multiplier=CAP).then_inc(made, 1)
            pool.wait_ge(same_ready, 1)
            pool.affine_select(out=before[:, :], in_=same[:, :], compare_op=ALU.is_gt, fill=0.0, base=0,
                               pattern=[[1, P]], channel_multiplier=-1).then_inc(before_ready, 1)

        @block.vector
        def _(dve):
            dve.wait_ge(made, 2)
            dve.tensor_copy(first_f[:, :], first_i[:, :]).then_inc(made_f, 1)
            dve.wait_ge(same_psum, 1)
            dve.tensor_copy(same[:, :], ps_c[:, 0:P])
            dve.tensor_copy(first_slot[:, :], ps_c[:, P:P + 1]).then_inc(same_ready, 1)
            dve.tensor_reduce(peak[:, 0, :], logits[:, :, :], AX_X, ALU.max)
            dve.drain()
            dve.tensor_tensor(probs[:, :, :], logits[:, :, :], bc(peak[:, 0, :], E8), ALU.subtract).then_inc(shifted, 1)
            dve.wait_ge(exp_ready, 1)
            dve.tensor_reduce(mass[:, :], probs[:, :, :], AX_X, ALU.add)
            dve.drain()
            dve.reciprocal(mass[:, :], mass[:, :])
            dve.drain()
            dve.tensor_tensor(probs[:, :, :], probs[:, :, :], bc(mass[:, :], E8), ALU.mult)
            dve.drain()
            for k, p in enumerate((probs, probs2)):
                dve.tensor_reduce(peak[:, k, :], p[:, :, :], AX_X, ALU.max)
                dve.drain()
                dve.tensor_tensor(mark8[:, :, :], p[:, :, :], bc(peak[:, k, :], E8), ALU.is_equal)
                dve.drain()
                dve.tensor_tensor(mark8[:, :, :], mark8[:, :, :], order[:, :].unsqueeze(1).broadcast_to(V), ALU.mult)
                dve.drain()
                dve.tensor_reduce(mass[:, :], mark8[:, :, :], AX_X, ALU.max)
                dve.drain()
                dve.tensor_tensor(hot[k][:, :, :], mark8[:, :, :], bc(mass[:, :], E8), ALU.is_equal)
                dve.drain()
                if k == 0:
                    dve.scalar_tensor_tensor(out=probs2[:, :, :], in0=hot[0][:, :, :], scalar=-4.0, in1=probs[:, :, :],
                                             op0=ALU.mult, op1=ALU.add)
                    dve.drain()
            dve.tensor_tensor(mass[:, :], peak[:, 0, :], peak[:, 1, :], ALU.add)
            dve.drain()
            dve.tensor_scalar(mass[:, :], mass[:, :], 1e-9, None, ALU.max)
            dve.drain()
            dve.reciprocal(mass[:, :], mass[:, :])
            dve.drain()
            dve.tensor_tensor(weight[:, :, :], peak[:, :, :], mass[:, :].unsqueeze(1).broadcast_to([P, 2, NB]), ALU.mult)
            dve.drain()
            dve.tensor_tensor(score[:, :, :], hot[0][:, :, :], bc(weight[:, 0, :], E8), ALU.mult)
            dve.tensor_tensor(mark8[:, :, :], hot[1][:, :, :], bc(weight[:, 1, :], E8), ALU.mult)
            dve.tensor_tensor(rank8[:, :, :], hot[0][:, :, :], hot[1][:, :, :], ALU.add)
            dve.drain()
            dve.tensor_tensor(score[:, :, :], score[:, :, :], mark8[:, :, :], ALU.add)
            dve.drain()
            dve.scalar_tensor_tensor(out=score[:, :, :], in0=rank8[:, :, :], scalar=-1.0, in1=score[:, :, :],
                                     op0=ALU.add, op1=ALU.add).then_inc(score_ready, 1)
            dve.wait_ge(rows_psum, 1)
            dve.tensor_copy(rows[:, :, :], ps_r[:, :, :])
            dve.drain()

            def total(dve, step, last):
                last.then_inc(counted, 1)
                dve.wait_ge(total_ready, step + 1)
                return ps_k[:, 0:1]

            flat = rows[:, :, :].rearrange("p a b -> p (a b)")
            mark_flat = mark[:, :, :].rearrange("p a b -> p (a b)")
            kth_largest(dve, P, flat, bits, cand, bit, count, keep, mark_flat, CAP, total)
            kth = bits[:, :].bitcast(F32)
            dve.tensor_scalar(mark_flat, flat, kth, 0.0, ALU.is_gt, ALU.add, accum_out=count[:, :])\
               .then_inc(more_counted, 1)
            dve.tensor_scalar(tie[:, :, :], rows[:, :, :], kth, None, ALU.is_equal)
            dve.wait_ge(more_total, 1)
            dve.tensor_scalar(room[:, :], ps_k[:, 1:2], -1.0, float(CAP), ALU.mult, ALU.add)

            def ranks(src, n):
                dve.drain()
                for hi in range(2):
                    last = dve.tensor_tensor_scan(rank[:, hi, :], ones[:, :], src[:, hi, :], 0.0, ALU.mult, ALU.add)
                last.then_inc(more_counted, 1)
                dve.wait_ge(more_total, n)
                dve.tensor_copy(offset[:, :], ps_k[:, 2:4])
                dve.drain()
                for hi in range(2):
                    dve.tensor_scalar(rank[:, hi, :], rank[:, hi, :], offset[:, hi:hi + 1], None, ALU.add)
                dve.drain()

            ranks(tie, 2)
            dve.scalar_tensor_tensor(out=tie[:, :, :], in0=rank[:, :, :], scalar=room[:, :], in1=tie[:, :, :],
                                     op0=ALU.is_le, op1=ALU.mult)
            dve.drain()
            dve.tensor_tensor(mark[:, :, :], mark[:, :, :], tie[:, :, :], ALU.add)
            ranks(mark, 3)
            dve.tensor_scalar(rank[:, :, :], rank[:, :, :], first_slot[:, :], -NOWHERE, ALU.add, ALU.add)
            dve.drain()
            dve.tensor_tensor(rank[:, :, :], rank[:, :, :], mark[:, :, :], ALU.mult)
            dve.drain()
            dve.tensor_scalar(rank[:, :, :], rank[:, :, :], NOWHERE, None, ALU.add).then_inc(slots_ready, 1)
            dve.wait_ge(slots_psum, 1)
            dve.tensor_copy(rank8[:, :, :], ps_r[:, :, :].rearrange("p a (b e) -> p (a b) e", e=E8))
            dve.drain()
            for k in range(2):
                dve.tensor_tensor(mark8[:, :, :], hot[k][:, :, :], rank8[:, :, :], ALU.mult)
                dve.drain()
                dve.tensor_reduce(slot_f[:, k, :], mark8[:, :, :], AX_X, ALU.add)
                dve.drain()
            dve.tensor_copy(slot[:, :, :], slot_f[:, :, :])
            dve.scalar_tensor_tensor(out=weight[:, :, :], in0=slot_f[:, :, :], scalar=float(SLOTS), in1=weight[:, :, :],
                                     op0=ALU.is_lt, op1=ALU.mult)

        @block.tensor
        def _(pe):
            pe.wait_ge(made_f, 1)
            pe.matmul(ps_c[:, 0:P], hotT[:, :], hotT[:, :], start=True, stop=True)
            pe.matmul(ps_c[:, P:P + 1], hotT[:, :], first_f[:, :], start=True, stop=True).then_inc(same_psum, 1)
            pe.wait_ge(score_ready, 1)
            for hi in range(2):
                last = pe.transpose(ps_r[:, hi, :], score[:, hi * LO:(hi + 1) * LO, :].rearrange("p b e -> p (b e)"),
                                    kit.ident[:, :])
            last.then_inc(rows_psum, 1)
            pe.wait_ge(before_ready, 1)
            with pe.Fori(0, TOP_BIT + 1) as step:
                pe.wait_ge(counted, step + 1)
                pe.matmul(ps_k[:, 0:1], same[:, :], count[:, :], start=True, stop=True).then_inc(total_ready, 1)
            pe.wait_ge(more_counted, 1)
            pe.matmul(ps_k[:, 1:2], same[:, :], count[:, :], start=True, stop=True).then_inc(more_total, 1)
            for n in (2, 3):
                pe.wait_ge(more_counted, n)
                pe.matmul(ps_k[:, 2:3], before[:, :], rank[:, 0, P - 1:P], start=True, stop=True)
                pe.matmul(ps_k[:, 3:4], before[:, :], rank[:, 1, P - 1:P], start=True, stop=False)
                pe.matmul(ps_k[:, 3:4], same[:, :], rank[:, 0, P - 1:P], start=False, stop=True)\
                  .then_inc(more_total, 1)
            pe.wait_ge(slots_ready, 1)
            for hi in range(2):
                last = pe.transpose(ps_r[:, hi, :], rank[:, hi, :], kit.ident[:, :])
            last.then_inc(slots_psum, 1)

        @block.scalar
        def _(act):
            act.wait_ge(shifted, 1)
            act.activation(probs[:, :, :], probs[:, :, :], ACT.Exp).then_inc(exp_ready, 1)


def deal_out(kit, x1, slot, dealt):
    nc = kit.nc
    ZC = SLOTS // E8 * C // P
    with kit.phase() as ctx:
        sb = tile_maker(nc, ctx)
        zeros = sb("zeros", [P, ZC])
        rows = sb("s_rows", [P, U, J, C])
        where = sb("s_where", [P, U, 2, J], I32)
        zeroed, cleared, rows_ready, where_ready = kit.sems("s_zeroed s_cleared s_rows_ready s_where_ready")
        scattered = [kit.pool_dma_sem(f"s_scattered{u}") for u in range(U)]
        block = ctx.enter_context(nc.Block())

        @block.sync
        def _(sp):
            sp.wait_ge(zeroed, 1)
            for e in range(E8):
                sp.dma_start(dealt[e * CAP:(e + 1) * CAP, :].rearrange("(p r) c -> p (r c)", p=P), zeros[:, :])\
                  .then_inc(cleared, 16)

        @block.vector
        def _(dve):
            dve.memset(zeros[:, :], 0.0).then_inc(zeroed, 1)

        @block.scalar
        def _(act):
            with act.Fori(0, TURNS) as t:
                for u in range(U):
                    act.wait_ge(scattered[u], t * (2 * J * 16))
                    act.activation(rows[:, u], x1[:, bass.ds(t * (U * J) + u * J, J), :], ACT.Copy)\
                       .then_inc(rows_ready, 1)

        @block.gpsimd
        def _(pool):
            pool.wait_ge(cleared, 16 * E8)
            with pool.Fori(0, TURNS) as t:
                for u in range(U):
                    pool.wait_ge(scattered[u], t * (2 * J * 16))
                    kit.apart(pool)
                    pool.tensor_copy(where[:, u], slot[:, :, bass.ds(t * (U * J) + u * J, J)]).then_inc(where_ready, 1)
                for u in range(U):
                    pool.wait_ge(where_ready, t * U + (u + 1))
                    pool.wait_ge(rows_ready, t * U + (u + 1))
                    kit.apart(pool)
                    for k in range(2):
                        for j in range(J):
                            pool.indirect_dma_start(
                                out=dealt, out_offset=bass.IndirectOffsetOnAxis(ap=where[:, u, k, j:j + 1], axis=0),
                                in_=rows[:, u, j, :], in_offset=None, bounds_check=SLOTS - 1, oob_is_err=False
                            ).then_inc(scattered[u], 16)
            for u in range(U):
                pool.wait_ge(scattered[u], TURNS * 2 * J * 16)


CB = 2
CHUNKS = CAP // (CB * P)
CT = CB * P


def routed_experts(kit, a, dealt, done):
    nc = kit.nc
    NC = U * CHUNKS
    with kit.phase() as ctx:
        sb, ps = tile_maker(nc, ctx), psum_maker(nc, ctx)
        w1 = sb("m_w1", [CH, U, 2, INNER])
        w3 = sb("m_w3", [CH, U, 2, INNER])
        w2 = sb("m_w2", [P, U, IT, C])
        x = sb("m_x", [P, 2, CB, C])
        xT = sb("m_xT", [CH, 2, 2, CT])
        gate = sb("m_gate", [P, 2, 2, CT])
        f = sb("m_f", [P, 2, IT, CT])
        o = sb("m_o", [P, 2, CB, C])
        ps_t = ps("m_ps_t", [CH, 2, 2, CT])
        ps_g = ps("m_ps_g", [P, 2, 2, CT])
        ps_u = ps("m_ps_u", [P, 2, 2, CT])
        ps_o = ps("m_ps_o", [P, 2, CB, 256])
        names = "xT_psum xT_ready g_psum g_ready u_psum f_ready o_psum o_ready"
        s = {n: kit.sem("m_" + n) for n in names.split()}
        w_in = [kit.sem(f"m_w_in{u}") for u in range(U)]
        x_in = [kit.sem(f"m_x_in{k}") for k in range(2)]
        stored = [kit.pool_dma_sem(f"m_stored{k}") for k in range(2)]
        block = ctx.enter_context(nc.Block())
        IP = IT // 2

        @block.sync
        def _(sp):
            for v in s.values():
                sp.sem_inc(v, U)
            with sp.Fori(0, TURNS) as t:
                for n in range(NC):
                    u, k = n // CHUNKS, n % CHUNKS
                    if k == 0:
                        need(sp, s["o_psum"], t, NC, n, ago=1)
                        e = t * U + u
                        for dst, src in ((w1, a["w1e"]), (w3, a["w3e"]), (w2, a["w2e"])):
                            sp.dma_start(dst[:, u], src[bass.ds(e, 1)].rearrange("e p k n -> p (e k) n"))\
                              .then_inc(w_in[u], 16)
                    need(sp, s["xT_psum"], t, NC, n, ago=2)
                    sp.dma_start(x[:, n % 2], dealt[bass.ds((t * U + u) * CAP + k * CT, CT), :].rearrange(
                        "(b p) c -> p b c", p=P)).then_inc(x_in[n % 2], 16)

        @block.gpsimd
        def _(pool):
            with pool.Fori(0, TURNS) as t:
                for n in range(NC):
                    u, k = n // CHUNKS, n % CHUNKS
                    need(pool, s["o_ready"], t, NC, n)
                    pool.dma_start(done[bass.ds((t * U + u) * CAP + k * CT, CT), :].rearrange("(b p) c -> p b c", p=P),
                                   o[:, n % 2]).then_inc(stored[n % 2], 16)
            for k in range(2):
                pool.wait_ge(stored[k], TURNS * NC // 2 * 16)

        @block.tensor
        def _(pe):
            with pe.Fori(0, TURNS) as t:
                for n in range(NC):
                    u, k, b = n // CHUNKS, n % CHUNKS, n % 2
                    pe.wait_ge(x_in[b], t * (NC // 2 * 16) + (n // 2 + 1) * 16)
                    need(pe, s["xT_ready"], t, NC, n, ago=2)
                    for r in range(CB):
                        for c in range(2):
                            last = pe.transpose(ps_t[:, b, c, r * P:(r + 1) * P], x[:, b, r, c * CH:(c + 1) * CH],
                                                kit.ident[:, :])
                    last.then_inc(s["xT_psum"], 1)
                    if k == 0:
                        pe.wait_ge(w_in[u], t * 48 + 48)
                    need(pe, s["xT_ready"], t, NC, n)
                    for i in range(IP):
                        q = n * IP + i
                        need(pe, s["g_ready"], t, NC * IP, q, ago=2)
                        for m in (2 * i, 2 * i + 1):
                            for c in range(2):
                                last = pe.matmul(ps_g[:, q % 2, m % 2, :], w1[:, u, c, m * P:(m + 1) * P],
                                                 xT[:, b, c, :], start=c == 0, stop=c == 1)
                        last.then_inc(s["g_psum"], 1)
                        need(pe, s["f_ready"], t, NC * IP, q, ago=2)
                        for m in (2 * i, 2 * i + 1):
                            for c in range(2):
                                last = pe.matmul(ps_u[:, q % 2, m % 2, :], w3[:, u, c, m * P:(m + 1) * P],
                                                 xT[:, b, c, :], start=c == 0, stop=c == 1)
                        last.then_inc(s["u_psum"], 1)
                    need(pe, s["f_ready"], t, NC * IP, n * IP + IP - 1)
                    need(pe, s["o_ready"], t, NC, n, ago=2)
                    for r in range(CB):
                        for m in range(IT):
                            last = pe.matmul(ps_o[:, b, r, 0:C], f[:, b, m, r * P:(r + 1) * P], w2[:, u, m, :],
                                             start=m == 0, stop=m == IT - 1)
                    last.then_inc(s["o_psum"], 1)

        @block.scalar
        def _(act):
            with act.Fori(0, TURNS) as t:
                for n in range(NC):
                    b = n % 2
                    need(act, s["xT_psum"], t, NC, n)
                    need(act, s["o_psum"], t, NC, n, ago=2)
                    act.activation(xT[:, b], ps_t[:, b], ACT.Copy).then_inc(s["xT_ready"], 1)
                    for i in range(IP):
                        q = n * IP + i
                        need(act, s["g_psum"], t, NC * IP, q)
                        need(act, s["f_ready"], t, NC * IP, q, ago=2)
                        act.activation(gate[:, q % 2], ps_g[:, q % 2], ACT.Silu).then_inc(s["g_ready"], 1)

        @block.vector
        def _(dve):
            with dve.Fori(0, TURNS) as t:
                for n in range(NC):
                    b = n % 2
                    need(dve, s["o_psum"], t, NC, n, ago=2)
                    for i in range(IP):
                        q = n * IP + i
                        need(dve, s["g_ready"], t, NC * IP, q)
                        need(dve, s["u_psum"], t, NC * IP, q)
                        dve.tensor_tensor(f[:, b, 2 * i:2 * i + 2, :], ps_u[:, q % 2], gate[:, q % 2], ALU.mult)\
                           .then_inc(s["f_ready"], 1)
                    need(dve, s["o_psum"], t, NC, n)
                    dve.wait_ge(stored[b], t * (NC // 2 * 16) + n // 2 * 16)
                    dve.tensor_copy(o[:, b], ps_o[:, b, :, 0:C]).then_inc(s["o_ready"], 1)


def gather_and_store(kit, weight, slot, done, out):
    nc = kit.nc
    with kit.phase() as ctx:
        sb = tile_maker(nc, ctx)
        where = sb("g_where", [P, U, 2, J], I32)
        got = sb("got", [P, U, 2, J, C])
        res = sb("res", [P, U, J, C])
        where_ready, summed = kit.sems("g_where_ready g_summed")
        gathered = [kit.pool_dma_sem(f"g_gathered{u}") for u in range(U)]
        stored = [kit.sem(f"g_stored{u}") for u in range(U)]
        block = ctx.enter_context(nc.Block())

        @block.gpsimd
        def _(pool):
            with pool.Fori(0, TURNS) as t:
                for u in range(U):
                    need(pool, summed, t, U, u, ago=U)
                    kit.apart(pool)
                    pool.tensor_copy(where[:, u], slot[:, :, bass.ds(t * (U * J) + u * J, J)])
                    pool.memset(got[:, u], 0.0).then_inc(where_ready, 1)
                for u in range(U):
                    pool.wait_ge(where_ready, t * U + (u + 1))
                    kit.apart(pool)
                    for k in range(2):
                        for j in range(J):
                            pool.indirect_dma_start(
                                out=got[:, u, k, j, :], out_offset=None, in_=done,
                                in_offset=bass.IndirectOffsetOnAxis(ap=where[:, u, k, j:j + 1], axis=0),
                                bounds_check=SLOTS - 1, oob_is_err=False).then_inc(gathered[u], 16)

        @block.vector
        def _(dve):
            dve.sem_inc(summed, U)
            with dve.Fori(0, TURNS) as t:
                for u in range(U):
                    blocks = bass.ds(t * (U * J) + u * J, J)
                    dve.wait_ge(gathered[u], t * (2 * J * 16) + 2 * J * 16)
                    for k in range(2):
                        dve.tensor_tensor(got[:, u, k], got[:, u, k], bc(weight[:, k, blocks], C), ALU.mult)
                    dve.drain()
                    dve.tensor_tensor(got[:, u, 0], got[:, u, 0], got[:, u, 1], ALU.add)
                    dve.drain()
                    dve.wait_ge(stored[u], t * 16)
                    dve.tensor_tensor(res[:, u], got[:, u, 0], kit.h[:, blocks, :], ALU.add).then_inc(summed, 1)

        @block.sync
        def _(sp):
            with sp.Fori(0, TURNS) as t:
                for u in range(U):
                    need(sp, summed, t, U, u)
                    sp.dma_start(out[:, bass.ds(t * (U * J) + u * J, J), :], res[:, u]).then_inc(stored[u], 16)
            for u in range(U):
                sp.wait_ge(stored[u], TURNS * 16)


def store_output(kit, out):
    nc = kit.nc
    stored = kit.sem("stored")
    with nc.Block() as block:
        @block.sync
        def _(sp):
            sp.dma_start(out, kit.h[:, :, :]).then_inc(stored, 16)
            sp.wait_ge(stored, 16)


PHASES = 4


def lm_tower(nc, a, out):
    with ExitStack() as ctx:
        kit = Kit(nc, ctx)
        setup_constants(kit)
        embed_and_time_mix(kit, a)
        if PHASES > 1:
            with ExitStack() as layer:
                sb = tile_maker(nc, layer)
                x1 = sb("x1", [P, NB, C])
                bands = sb("bands", [P, 2, NB, EXPERTS0])
                route_tokens(kit, a, x1, bands)
                moe_attention_ffn(kit, a, x1, bands)
        if PHASES > 2:
            state_space_block(kit, a)
        if PHASES > 3:
            dealt = nc.dram_tensor("dealt", (SLOTS, C), F32, kind="Internal").ap()
            done = nc.dram_tensor("done", (SLOTS, C), F32, kind="Internal").ap()
            sb = tile_maker(nc, ctx)
            weight = sb("weight", [P, 2, NB])
            slot = sb("slot", [P, 2, NB], I32)
            with ExitStack() as layer:
                sb = tile_maker(nc, layer)
                x1 = sb("e_x1", [P, NB, C])
                logits = sb("logits", [P, NB, E8])
                shared_expert_and_router(kit, a, x1, logits)
                choose_slots(kit, logits, weight, slot)
                deal_out(kit, x1, slot, dealt)
            routed_experts(kit, a, dealt, done)
            gather_and_store(kit, weight, slot, done, out)
        else:
            store_output(kit, out)


def lay_out(i):
    import numpy as np

    def col(v):
        return np.ascontiguousarray(np.asarray(v).reshape(2, CH).T)

    def rows(w):
        w = np.asarray(w)
        return np.ascontiguousarray(w.reshape(2, CH, w.shape[1]).transpose(1, 0, 2))

    w1 = np.zeros((CH + 1, 2, MLP + 3 * C), np.float32)
    w1[0:CH] = rows(np.asarray(i["L0_ffn_w1"]).T)
    w1[CH, 1] = np.asarray(i["L0_ffn_b1"])
    w2 = np.asarray(i["L0_ffn_w2"]).T
    in_proj = np.asarray(i["L1_attn_in_proj_w"]).T

    return {
        "x": np.ascontiguousarray(np.asarray(i["x"]).reshape(NB, P).T),
        "emb": np.asarray(i["L0_tok_W"]),
        "decay": col(i["L0_attn_time_decay"]),
        "first": col(i["L0_attn_time_first"]),
        "mix": np.stack([col(np.asarray(i[f"L0_attn_time_mix_{n}"]).reshape(-1)) for n in "kvr"], axis=1),
        "wkvr": np.stack([rows(np.asarray(i[f"L0_attn_W{n}"]).T) for n in "kvr"], axis=1),
        "wo": rows(np.asarray(i["L0_attn_Wo"]).T),
        "w_router": rows(np.asarray(i["L0_ffn_w_router"]).T),
        "gamma1": np.asarray(i["L0_ffn_gamma1"])[None],
        "beta1": np.asarray(i["L0_ffn_beta1"])[None],
        "w1": w1,
        "w2_mlp": w2[0:MLP].reshape(FC1_TILES, P, 2, C).transpose(1, 0, 2, 3),
        "w2_att": w2[MLP:].reshape(2, CH, 2, C).transpose(1, 0, 2, 3),
        "b2": np.asarray(i["L0_ffn_b2"]).reshape(1, 2, C),
        "ln12": np.stack([np.asarray(i[f"L1_attn_{n}"]) for n in ("ln1_w", "ln1_b", "ln2_w", "ln2_b")])[None],
        "wz": rows(np.concatenate([in_proj[:, 0:DI], in_proj[:, DI + 4 * P:]], axis=1)),
        "wx": rows(in_proj[:, DI:DI + 4 * P]),
        "conv_w": np.asarray(i["L1_attn_conv_w"]).reshape(4, P, TAPS).transpose(1, 0, 2),
        "conv_b": np.asarray(i["L1_attn_conv_b"]).reshape(4, P).T,
        "dt_bias": np.asarray(i["L1_attn_dt_bias"])[None],
        "a_log": np.asarray(i["L1_attn_A_log"])[None],
        "d_skip": np.asarray(i["L1_attn_D_skip"])[None],
        "norm_w": np.asarray(i["L1_attn_ssm_norm_w"])[None],
        "w_out": np.asarray(i["L1_attn_out_proj_w"]).T.reshape(KD, P, C).transpose(1, 0, 2),
        "wf1": rows(np.asarray(i["L1_attn_fc1_w"]).T),
        "wr": rows(np.asarray(i["L1_ffn_Wr"])),
        "s1": rows(np.asarray(i["L1_ffn_s1"])),
        "s3": rows(np.asarray(i["L1_ffn_s3"])),
        "s2": np.asarray(i["L1_ffn_s2"]).reshape(IT, P, C).transpose(1, 0, 2),
        "w1e": np.asarray(i["L1_ffn_w1"]).reshape(E8, 2, CH, INNER).transpose(0, 2, 1, 3),
        "w3e": np.asarray(i["L1_ffn_w3"]).reshape(E8, 2, CH, INNER).transpose(0, 2, 1, 3),
        "w2e": np.asarray(i["L1_ffn_w2"]).reshape(E8, IT, P, C).transpose(0, 2, 1, 3),
        "wf2": np.asarray(i["L1_attn_fc2_w"]).T.reshape(KD, P, C).transpose(1, 0, 2),
    }


def kernel(**inputs):
    import numpy as np
    import concourse.bacc as bacc
    from concourse.bass_utils import run_bass_kernel_spmd

    nc = bacc.Bacc("TRN2", target_bir_lowering=False, num_devices=1)
    arrays = {f"in_{n}": np.ascontiguousarray(v) for n, v in lay_out(inputs).items()}
    aps = {n[3:]: nc.dram_tensor(n, v.shape, mybir.dt.from_np(v.dtype), kind="ExternalInput").ap()
           for n, v in arrays.items()}
    out = nc.dram_tensor("out", (N, C), F32, kind="ExternalOutput").ap()
    lm_tower(nc, aps, out.rearrange("(b p) c -> p b c", p=P))
    got = run_bass_kernel_spmd(nc, [arrays], core_ids=[0]).results[0]["out"]
    return got.reshape(B, T, C)
```

```python
from contextlib import ExitStack, contextmanager

import concourse.bass as bass
from concourse import mybir

ALU = mybir.AluOpType
ACT = mybir.ActivationFunctionType
F32 = mybir.dt.float32
BF16 = mybir.dt.bfloat16
I32 = mybir.dt.int32
AX_X = mybir.AxisListType.X

P = 128
C = 192
CH = C // 2
B, T = 8, 512
N = B * T
NB = N // P
J = T // P
U = 2
TURNS = B // U
VOCAB = 8000
NEG_HUGE = -1e38
DMA = 16


def need(eng, sem, t, per_turn, k, ago=0):
    eng.wait_ge(sem, t * per_turn + (U + k + 1 - ago))


class Kit:

    def __init__(self, nc, ctx):
        self.nc, self.ctx, self.whole, self.used = nc, ctx, ctx, []

    @contextmanager
    def phase(self):
        outer, self.used = self.ctx, []
        with ExitStack() as self.ctx:
            yield self.ctx
        self.ctx = outer
        with self.nc.Block() as block:
            @block.sync
            def _(sp):
                for x in self.used:
                    sp.sem_clear(x)

    def sem(self, name):
        self.used.append(self.ctx.enter_context(self.nc.semaphore(name)))
        return self.used[-1]

    def apart(self, pool):
        pool.sem_inc(self.passed, 1)

    def pool_dma_sem(self, name):
        return self.whole.enter_context(self.nc.semaphore(name))

    def sems(self, names):
        return [self.sem(n) for n in names.split()]


def tile_maker(nc, ctx):
    def sb(name, shape, dt=F32):
        return ctx.enter_context(nc.sbuf_tensor(name, shape, dt))
    return sb


def psum_maker(nc, ctx):
    def ps(name, shape, dt=F32):
        return ctx.enter_context(nc.psum_tensor(name, shape, dt))
    return ps


def bc(ap, n):
    return ap.unsqueeze(len(ap.shape)).broadcast_to([*ap.shape, n])


def setup_constants(kit):
    nc = kit.nc
    sb = tile_maker(nc, kit.ctx)
    kit.h = sb("h", [P, NB, C])
    kit.ident = sb("ident", [P, P])
    kit.ident16 = sb("ident16", [P, P], BF16)
    kit.minus_half = sb("minus_half", [P, 8])
    kit.passed = kit.pool_dma_sem("passed")
    made = kit.sem("const_made")
    with nc.Block() as block:
        @block.gpsimd
        def _(pool):
            pool.memset(kit.ident[:, :], 0.0).then_inc(made, 1)
            pool.memset(kit.ident16[:, :], 0.0).then_inc(made, 1)
            pool.memset(kit.minus_half[:, :], -0.5).then_inc(made, 1)
            pool.wait_ge(made, 3)
            for m in (kit.ident, kit.ident16):
                pool.affine_select(out=m[:, :], in_=m[:, :], compare_op=ALU.not_equal, fill=1.0, base=0,
                                   pattern=[[-1, P]], channel_multiplier=1).then_inc(made, 1)
            pool.wait_ge(made, 5)


def ln_stats(dve, src, stats, mv, var_eps, eps):
    for j in range(J):
        dve.bn_stats(stats[:, j, :], src[:, j, :])
    dve.drain()
    for j in range(J):
        dve.bn_aggr(mv[:, j, :], stats[:, j, :])
    dve.drain()
    return dve.tensor_scalar(var_eps[:, :], mv[:, :, 1], float(eps), None, ALU.add)


def ln_rstd(kit, pool, rstd, var_eps):
    return pool.tensor_tensor(rstd[:, :], var_eps[:, :], kit.minus_half[:, 0:J], ALU.pow)


def ln_apply(dve, out, src, mv, rstd):
    for j in range(J):
        last = dve.tensor_scalar(out[:, j, :], src[:, j, :], mv[:, j, 0:1], rstd[:, j:j + 1],
                                 ALU.subtract, ALU.mult)
    return last


def embed_and_time_mix(kit, a):
    nc = kit.nc
    with kit.phase() as ctx:
        sb, ps = tile_maker(nc, ctx), psum_maker(nc, ctx)
        tokens = sb("tokens", [P, NB], I32)
        tok_f = sb("tok_f", [P, NB])
        in_vocab = sb("in_vocab", [P, NB])
        tok_tmp = sb("tok_tmp", [P, NB])
        row_of = sb("row_of", [P, NB], I32)
        row_now = sb("row_now", [P, U, J], I32)
        emb = sb("emb", [P, U, J, C])
        h0 = sb("h0", [P, U, J, C])
        stats = sb("stats", [P, U, J, 6])
        mv = sb("mv", [P, U, J, 2])
        var_eps = sb("var_eps", [P, U, J])
        rstd = sb("rstd", [P, U, J])
        xn = sb("xn", [P, U, J, C])
        xT = sb("xT", [CH, U, 2, T + 1])
        diff = sb("diff", [CH, 2, T])
        mixed = sb("mixed", [CH, U, 3, 2, T])
        kT = sb("kT", [CH, U, 2, T])
        vT = sb("vT", [CH, U, 2, T])
        gate = sb("gate", [CH, U, 2, T])
        omax = sb("omax", [CH, 2, T + 1])
        gaps = sb("gaps", [CH, 2, 2, T])
        gap_lo = sb("gap_lo", [CH, U, 2, 2, T])
        gap_hi = sb("gap_hi", [CH, U, 2, 2, T])
        bv = sb("bv", [CH, 2, T])
        inject = sb("inject", [CH, 2, T])
        pnum = sb("pnum", [CH, 2, T + 1])
        qden = sb("qden", [CH, 2, T + 1])
        num = sb("num", [CH, 2, T])
        den = sb("den", [CH, 2, T])
        z = sb("z", [CH, U, 2, T])
        decay = sb("decay", [CH, 2])
        first = sb("first", [CH, 2])
        mix_of = sb("mix_of", [CH, 3, 2])
        wkvr = sb("wkvr", [CH, 3, 2, C])
        wo = sb("wo", [CH, 2, C])
        ps_t = ps("ps_t", [P, 2, T])
        ps_p = ps("ps_p", [P, 2, 2, T])
        ps_o = ps("ps_o", [P, J, 256])
        (loaded, rows_ready, rows_now_ready, h0_ready, rstd_ready, xn_ready, xT_psum, xT_ready, mixed_ready,
         proj_psum, proj_read, gaps_ready, exps_ready, bv_ready, z_ready, out_psum, h_written) = (
            kit.sem("a_" + n) for n in (
                "loaded rows_ready rows_now_ready h0_ready rstd_ready xn_ready xT_psum xT_ready mixed_ready "
                "proj_psum proj_read gaps_ready exps_ready bv_ready z_ready out_psum h_written").split())
        emb_in = [kit.pool_dma_sem(f"a_emb_in{u}") for u in range(U)]
        counted = (h0_ready, rstd_ready, xn_ready, xT_psum, xT_ready, mixed_ready, proj_psum, proj_read,
                   gaps_ready, exps_ready, bv_ready, z_ready, out_psum, h_written)
        block = ctx.enter_context(nc.Block())

        @block.sync
        def _(sp):
            for s in counted:
                sp.sem_inc(s, U)
            sp.dma_start(tokens[:, :], a["x"]).then_inc(loaded, 16)
            sp.dma_start(decay[:, :], a["decay"]).then_inc(loaded, 16)
            sp.dma_start(first[:, :], a["first"]).then_inc(loaded, 16)
            sp.dma_start(mix_of[:, :, :], a["mix"]).then_inc(loaded, 16)
            sp.dma_start(wkvr[:, :, :, :], a["wkvr"]).then_inc(loaded, 16)
            sp.dma_start(wo[:, :, :], a["wo"]).then_inc(loaded, 16)

        @block.gpsimd
        def _(pool):
            pool.wait_ge(rows_ready, 1)
            with pool.Fori(0, TURNS) as t:
                pool.tensor_copy(row_now[:, :, :], row_of[:, bass.ds(t * (U * J), U * J)].rearrange(
                    "p (u j) -> p u j", u=U)).then_inc(rows_now_ready, 1)
                pool.wait_ge(rows_now_ready, t + 1)
                for u in range(U):
                    need(pool, h0_ready, t, U, u, ago=U)
                    kit.apart(pool)
                    for j in range(J):
                        pool.indirect_dma_start(
                            out=emb[:, u, j, :], out_offset=None, in_=a["emb"],
                            in_offset=bass.IndirectOffsetOnAxis(ap=row_now[:, u, j:j + 1], axis=0)
                        ).then_inc(emb_in[u], 16)
                for u in range(U):
                    need(pool, h0_ready, t, U, u)
                    need(pool, xn_ready, t, U, u, ago=U)
                    ln_rstd(kit, pool, rstd[:, u, :], var_eps[:, u, :]).then_inc(rstd_ready, 1)

        @block.vector
        def _(dve):
            dve.memset(xT[:, :, :, 0:1], 0.0)
            dve.memset(omax[:, :, 0:1], NEG_HUGE)
            dve.memset(pnum[:, :, 0:1], 0.0)
            dve.memset(qden[:, :, 0:1], 0.0)
            dve.wait_ge(loaded, 96)
            dve.tensor_copy(tok_f[:, :], tokens[:, :])
            dve.drain()
            dve.tensor_scalar(tok_tmp[:, :], tok_f[:, :], 0.0, None, ALU.is_ge)
            dve.tensor_scalar(in_vocab[:, :], tok_f[:, :], float(VOCAB), None, ALU.is_lt)
            dve.tensor_scalar(tok_f[:, :], tok_f[:, :], 0.0, float(VOCAB - 1), ALU.max, ALU.min)
            dve.drain()
            dve.tensor_tensor(in_vocab[:, :], in_vocab[:, :], tok_tmp[:, :], ALU.mult)
            dve.tensor_copy(row_of[:, :], tok_f[:, :]).then_inc(rows_ready, 1)
            with dve.Fori(0, TURNS) as t:
                for u in range(U):
                    dve.drain()
                    dve.wait_ge(emb_in[u], t * (16 * J) + 16 * J)
                    dve.tensor_tensor(h0[:, u, :, :], emb[:, u, :, :],
                                      bc(in_vocab[:, bass.ds(t * (U * J) + u * J, J)], C), ALU.mult)
                    dve.drain()
                    ln_stats(dve, h0[:, u], stats[:, u], mv[:, u], var_eps[:, u], 1e-5).then_inc(h0_ready, 1)
                for u in range(U):
                    need(dve, rstd_ready, t, U, u)
                    need(dve, xT_psum, t, U, u, ago=U)
                    ln_apply(dve, xn[:, u], h0[:, u], mv[:, u], rstd[:, u]).then_inc(xn_ready, 1)
                for u in range(U):
                    now, prev = xT[:, u, :, 1:T + 1], xT[:, u, :, 0:T]
                    dve.drain()
                    need(dve, xT_ready, t, U, u)
                    dve.tensor_tensor(diff[:, :, :], now, prev, ALU.subtract)
                    dve.drain()
                    for o in range(3):
                        for c in range(2):
                            last = dve.scalar_tensor_tensor(
                                out=mixed[:, u, o, c, :], in0=diff[:, c, :], scalar=mix_of[:, o, c:c + 1],
                                in1=prev[:, c, :], op0=ALU.mult, op1=ALU.add)
                    last.then_inc(mixed_ready, 1)
                for u in range(U):
                    dve.drain()
                    need(dve, proj_read, t, 3 * U, 3 * u + 0)
                    for c in range(2):
                        dve.tensor_tensor_scan(omax[:, c, 1:T + 1], decay[:, c:c + 1].broadcast_to([CH, T]),
                                               kT[:, u, c, :], NEG_HUGE, ALU.add, ALU.max)
                    dve.drain()
                    for c in range(2):
                        dve.scalar_tensor_tensor(out=gaps[:, 0, c, :], in0=kT[:, u, c, :], scalar=first[:, c:c + 1],
                                                 in1=omax[:, c, 0:T], op0=ALU.add, op1=ALU.subtract)
                        dve.scalar_tensor_tensor(out=gaps[:, 1, c, :], in0=omax[:, c, 0:T], scalar=decay[:, c:c + 1],
                                                 in1=kT[:, u, c, :], op0=ALU.add, op1=ALU.subtract)
                    dve.drain()
                    dve.tensor_scalar(gap_lo[:, u], gaps[:, :, :, :], 0.0, None, ALU.min)
                    dve.tensor_scalar(gap_hi[:, u], gaps[:, :, :, :], 0.0, None, ALU.max).then_inc(gaps_ready, 1)
                for u in range(U):
                    eb, ea2 = gap_lo[:, u, 0], gap_lo[:, u, 1]
                    ea, eb2 = gap_hi[:, u, 0], gap_hi[:, u, 1]
                    dve.drain()
                    need(dve, exps_ready, t, U, u)
                    need(dve, proj_read, t, 3 * U, 3 * u + 2)
                    dve.tensor_tensor(inject[:, :, :], eb2, vT[:, u], ALU.mult)
                    dve.tensor_tensor(bv[:, :, :], eb, vT[:, u], ALU.mult)
                    dve.drain()
                    for c in range(2):
                        dve.tensor_tensor_scan(pnum[:, c, 1:T + 1], ea2[:, c, :], inject[:, c, :], 0.0,
                                               ALU.mult, ALU.add)
                        dve.tensor_tensor_scan(qden[:, c, 1:T + 1], ea2[:, c, :], eb2[:, c, :], 0.0,
                                               ALU.mult, ALU.add)
                    dve.drain()
                    dve.tensor_tensor(den[:, :, :], ea, qden[:, :, 0:T], ALU.mult)
                    dve.tensor_tensor(num[:, :, :], ea, pnum[:, :, 0:T], ALU.mult)
                    dve.drain()
                    dve.tensor_tensor(den[:, :, :], den[:, :, :], eb, ALU.add)
                    dve.tensor_tensor(num[:, :, :], num[:, :, :], bv[:, :, :], ALU.add)
                    dve.drain()
                    dve.reciprocal(den[:, :, :], den[:, :, :])
                    dve.tensor_tensor(num[:, :, :], num[:, :, :], gate[:, u], ALU.mult)
                    dve.drain()
                    need(dve, out_psum, t, U, u, ago=U)
                    dve.tensor_tensor(z[:, u], num[:, :, :], den[:, :, :], ALU.mult).then_inc(z_ready, 1)
                for u in range(U):
                    need(dve, out_psum, t, U, u)
                    dve.tensor_tensor(kit.h[:, bass.ds(t * (U * J) + u * J, J), :], ps_o[:, :, 0:C], h0[:, u],
                                      ALU.add).then_inc(h_written, 1)

        @block.tensor
        def _(pe):
            pe.wait_ge(loaded, 96)
            with pe.Fori(0, TURNS) as t:
                for u in range(U):
                    need(pe, xn_ready, t, U, u)
                    need(pe, xT_ready, t, U, u, ago=1)
                    for j in range(J):
                        for c in range(2):
                            last = pe.transpose(ps_t[0:CH, c, j * P:(j + 1) * P], xn[:, u, j, c * CH:(c + 1) * CH],
                                                kit.ident[:, :])
                    last.then_inc(xT_psum, 1)
                for u in range(U):
                    need(pe, mixed_ready, t, U, u)
                    for o in range(3):
                        need(pe, proj_read, t, 3 * U, 3 * u + o, ago=2)
                        for m in range(2):
                            for c in range(2):
                                last = pe.matmul(ps_p[0:CH, (u + o) % 2, m, :], wkvr[:, o, c, m * CH:(m + 1) * CH],
                                                 mixed[:, u, o, c, :], start=c == 0, stop=c == 1)
                        last.then_inc(proj_psum, 1)
                for u in range(U):
                    need(pe, z_ready, t, U, u)
                    need(pe, h_written, t, U, u, ago=1)
                    for j in range(J):
                        for c in range(2):
                            last = pe.matmul(ps_o[:, j, 0:C], z[:, u, c, j * P:(j + 1) * P], wo[:, c, :],
                                             start=c == 0, stop=c == 1)
                    last.then_inc(out_psum, 1)

        @block.scalar
        def _(act):
            with act.Fori(0, TURNS) as t:
                for u in range(U):
                    need(act, xT_psum, t, U, u)
                    need(act, mixed_ready, t, U, u, ago=U)
                    act.activation(xT[:, u, :, 1:T + 1], ps_t[0:CH, :, :], ACT.Copy).then_inc(xT_ready, 1)
                for u in range(U):
                    for o in range(3):
                        need(act, proj_psum, t, 3 * U, 3 * u + o)
                        if o == 0:
                            need(act, z_ready, t, U, u, ago=U)
                        act.activation((kT, vT, gate)[o][:, u], ps_p[0:CH, (u + o) % 2, :, :],
                                       ACT.Sigmoid if o == 2 else ACT.Copy).then_inc(proj_read, 1)
                for u in range(U):
                    need(act, gaps_ready, t, U, u)
                    act.activation(gap_lo[:, u], gap_lo[:, u], ACT.Exp)
                    act.activation(gap_hi[:, u], gap_hi[:, u], ACT.Exp, scale=-1.0).then_inc(exps_ready, 1)


EXPERTS0 = 4
CAP0 = T // 2
BANDS = ((0, 24), (24, 48), (48, 96), (96, 192))
TOP_BIT = 29


def kth_largest(dve, rows, scores, bits, cand, bit, count, keep, mark, k, total=None):
    dve.memset(bits[:, :], 0)
    dve.memset(bit[:, :], 1 << TOP_BIT)
    dve.drain()
    with dve.Fori(0, TOP_BIT + 1) as step:
        dve.tensor_tensor(cand[:, :], bits[:, :], bit[:, :], ALU.bitwise_or)
        dve.drain()
        last = dve.tensor_scalar(mark, scores, cand[:, :].bitcast(F32), 0.0, ALU.is_ge, ALU.add,
                                 accum_out=count[:, :])
        if total is None:
            dve.drain()
            counted = count
        else:
            counted = total(dve, step, last)
        dve.tensor_scalar(keep[:, :], counted[:, :], float(k), None, ALU.is_ge)
        dve.drain()
        dve.tensor_tensor(keep[:, :], keep[:, :], bit[:, :], ALU.mult)
        dve.tensor_scalar(bit[:, :], bit[:, :], 1, None, ALU.logical_shift_right)
        dve.drain()
        dve.tensor_tensor(bits[:, :], bits[:, :], keep[:, :], ALU.bitwise_or)
        dve.drain()


def route_tokens(kit, a, x1, bands):
    nc = kit.nc
    R = B * EXPERTS0
    with kit.phase() as ctx:
        sb, ps = tile_maker(nc, ctx), psum_maker(nc, ctx)
        stats = sb("b_stats", [P, U, J, 6])
        mv = sb("b_mv", [P, U, J, 2])
        var_eps = sb("b_var_eps", [P, U, J])
        rstd = sb("b_rstd", [P, U, J])
        xn = sb("b_xn", [P, U, J, C])
        xT = sb("b_xT", [CH, U, 2, T])
        w_router = sb("w_router", [CH, 2, EXPERTS0])
        probs = sb("probs", [P, NB, EXPERTS0])
        prob_rows = sb("prob_rows", [P, J, B, EXPERTS0])
        peak = sb("peak", [P, NB])
        mass = sb("mass", [P, NB])
        score = sb("score", [R, T])
        mark = sb("mark", [R, T])
        tie = sb("tie", [R, T])
        tie_rank = sb("tie_rank", [R, T])
        taken = sb("taken", [R, 2, T])
        ones = sb("b_ones", [R, T])
        bits = sb("bits", [R, 1], I32)
        cand = sb("cand", [R, 1], I32)
        bit = sb("bit", [R, 1], I32)
        keep = sb("keep", [R, 1], I32)
        count = sb("count", [R, 1])
        room = sb("room", [R, 1])
        ps_t = ps("b_ps_t", [P, 2, T])
        ps_l = ps("b_ps_l", [P, U, 512])
        ps_s = ps("b_ps_s", [R, J, P])
        ps_b = ps("b_ps_b", [P, 2, J, R])
        (loaded, var_ready, rstd_ready, xn_ready, x1_kept, xT_psum, xT_ready, logit_psum, logit_read, shifted,
         exp_ready, probs_ready, score_psum, taken_ready, taken_psum) = (
            kit.sem("b_" + n) for n in (
                "loaded var_ready rstd_ready xn_ready x1_kept xT_psum xT_ready logit_psum logit_read shifted "
                "exp_ready probs_ready score_psum taken_ready taken_psum").split())
        counted = (var_ready, rstd_ready, xn_ready, x1_kept, xT_psum, xT_ready, logit_psum, logit_read)
        block = ctx.enter_context(nc.Block())

        @block.sync
        def _(sp):
            for s in counted:
                sp.sem_inc(s, U)
            sp.dma_start(w_router[:, :, :], a["w_router"]).then_inc(loaded, 16)

        @block.gpsimd
        def _(pool):
            with pool.Fori(0, TURNS) as t:
                for u in range(U):
                    need(pool, var_ready, t, U, u)
                    ln_rstd(kit, pool, rstd[:, u, :], var_eps[:, u, :]).then_inc(rstd_ready, 1)
                for u in range(U):
                    need(pool, xn_ready, t, U, u)
                    kit.apart(pool)
                    pool.tensor_copy(x1[:, bass.ds(t * (U * J) + u * J, J), :], xn[:, u]).then_inc(x1_kept, 1)

        @block.vector
        def _(dve):
            dve.memset(ones[:, :], 1.0)
            with dve.Fori(0, TURNS) as t:
                for u in range(U):
                    dve.drain()
                    ln_stats(dve, kit.h[:, bass.ds(t * (U * J) + u * J, J), :], stats[:, u], mv[:, u],
                             var_eps[:, u], 1e-5).then_inc(var_ready, 1)
                for u in range(U):
                    need(dve, rstd_ready, t, U, u)
                    need(dve, xT_psum, t, U, u, ago=U)
                    need(dve, x1_kept, t, U, u, ago=U)
                    ln_apply(dve, xn[:, u], kit.h[:, bass.ds(t * (U * J) + u * J, J), :], mv[:, u],
                             rstd[:, u]).then_inc(xn_ready, 1)
                for u in range(U):
                    need(dve, logit_psum, t, U, u)
                    dve.tensor_copy(probs[:, bass.ds(t * (U * J) + u * J, J), :], ps_l[:, u, 0:J * EXPERTS0].rearrange(
                        "p (j e) -> p j e", j=J)).then_inc(logit_read, 1)
            dve.drain()
            dve.tensor_reduce(peak[:, :], probs[:, :, :], AX_X, ALU.max)
            dve.drain()
            dve.tensor_tensor(probs[:, :, :], probs[:, :, :], bc(peak[:, :], EXPERTS0), ALU.subtract).then_inc(shifted, 1)
            dve.wait_ge(exp_ready, 1)
            dve.tensor_reduce(mass[:, :], probs[:, :, :], AX_X, ALU.add)
            dve.drain()
            dve.reciprocal(mass[:, :], mass[:, :])
            dve.drain()
            dve.tensor_tensor(prob_rows[:, :, :, :].rearrange("p j b e -> p b j e"),
                              probs[:, :, :].rearrange("p (b j) e -> p b j e", j=J),
                              bc(mass[:, :].rearrange("p (b j) -> p b j", j=J), EXPERTS0), ALU.mult)\
               .then_inc(probs_ready, 1)
            dve.wait_ge(score_psum, 1)
            dve.tensor_copy(score[:, :], ps_s[:, :, :])
            dve.drain()
            kth_largest(dve, R, score[:, :], bits, cand, bit, count, keep, mark[:, :], CAP0)
            kth = bits[:, :].bitcast(F32)
            dve.tensor_scalar(mark[:, :], score[:, :], kth, 0.0, ALU.is_gt, ALU.add, accum_out=count[:, :])
            dve.tensor_scalar(tie[:, :], score[:, :], kth, None, ALU.is_equal)
            dve.drain()
            dve.tensor_scalar(room[:, :], count[:, :], -1.0, float(CAP0), ALU.mult, ALU.add)
            dve.tensor_tensor_scan(tie_rank[:, :], ones[:, :], tie[:, :], 0.0, ALU.mult, ALU.add)
            dve.drain()
            dve.scalar_tensor_tensor(out=tie[:, :], in0=tie_rank[:, :], scalar=room[:, :], in1=tie[:, :],
                                     op0=ALU.is_le, op1=ALU.mult)
            dve.drain()
            dve.tensor_tensor(taken[:, 0, :], mark[:, :], tie[:, :], ALU.add)
            dve.drain()
            dve.tensor_tensor(taken[:, 1, :], taken[:, 0, :], score[:, :], ALU.mult).then_inc(taken_ready, 1)
            dve.wait_ge(taken_psum, 1)
            for e in reversed(range(EXPERTS0)):
                for w in range(2):
                    src = ps_b[:, w, :, :].rearrange("p j (b e) -> p b j e", e=EXPERTS0)[:, :, :, e]
                    dst = bands[:, w, :, e].rearrange("p (b j) -> p b j", j=J)
                    if e == EXPERTS0 - 1:
                        dve.tensor_copy(dst, src)
                    else:
                        dve.tensor_tensor(dst, src, bands[:, w, :, e + 1].rearrange("p (b j) -> p b j", j=J), ALU.add)
                dve.drain()

        @block.tensor
        def _(pe):
            pe.wait_ge(loaded, 16)
            with pe.Fori(0, TURNS) as t:
                for u in range(U):
                    need(pe, xn_ready, t, U, u)
                    need(pe, xT_ready, t, U, u, ago=1)
                    for j in range(J):
                        for c in range(2):
                            last = pe.transpose(ps_t[0:CH, c, j * P:(j + 1) * P], xn[:, u, j, c * CH:(c + 1) * CH],
                                                kit.ident[:, :])
                    last.then_inc(xT_psum, 1)
                for u in range(U):
                    need(pe, xT_ready, t, U, u)
                    need(pe, logit_read, t, U, u, ago=U)
                    for j in range(J):
                        for c in range(2):
                            last = pe.matmul(ps_l[:, u, j * EXPERTS0:(j + 1) * EXPERTS0], xT[:, u, c, j * P:(j + 1) * P],
                                             w_router[:, c, :], start=c == 0, stop=c == 1)
                    last.then_inc(logit_psum, 1)
            pe.wait_ge(probs_ready, 1)
            for j in range(J):
                last = pe.transpose(ps_s[:, j, :], prob_rows[:, j].rearrange("p b e -> p (b e)"), kit.ident[:, :])
            last.then_inc(score_psum, 1)
            pe.wait_ge(taken_ready, 1)
            for w in range(2):
                for j in range(J):
                    last = pe.transpose(ps_b[:, w, j, :], taken[:, w, j * P:(j + 1) * P], kit.ident[0:R, 0:R])
            last.then_inc(taken_psum, 1)

        @block.scalar
        def _(act):
            with act.Fori(0, TURNS) as t:
                for u in range(U):
                    need(act, xT_psum, t, U, u)
                    need(act, logit_psum, t, U, u, ago=U)
                    act.activation(xT[:, u], ps_t[0:CH, :, :], ACT.Copy).then_inc(xT_ready, 1)
            act.wait_ge(shifted, 1)
            act.activation(probs[:, :, :], probs[:, :, :], ACT.Exp).then_inc(exp_ready, 1)


HEADS, HD = 12, C // 12
MLP = 4 * C
FC1_TILES = MLP // P
QSCALE = HD ** -0.5
G3 = HEADS // 4
PAIRS = 6
STACK = PAIRS * HD
LIVE_E = 8


def moe_attention_ffn(kit, a, x1, bands):
    nc = kit.nc
    with kit.phase() as ctx:
        sb, ps = tile_maker(nc, ctx), psum_maker(nc, ctx)
        gamma = sb("gamma", [P, C])
        beta = sb("beta", [P, C])
        w1 = sb("w1", [CH + 1, 2, MLP + 3 * C])
        w2_mlp = sb("w2_mlp", [P, FC1_TILES, 2, C])
        w2_att = sb("w2_att", [CH, 2, 2, C])
        b2 = sb("b2", [P, 2, C])
        stats = sb("c_stats", [P, J, 6])
        mv = sb("c_mv", [P, J, 2])
        var_eps = sb("c_var_eps", [P, J])
        rstd = sb("c_rstd", [P, J])
        y = sb("y", [P, J, C + 1])
        yT = sb("yT", [CH + 1, 2, T])
        parts = sb("parts", [P, 2, 3, 2 * C], BF16)
        rest = sb("rest", [P, 2 * C])
        stacked = sb("stacked", [P, J, 2, HEADS, STACK], BF16)
        qT = sb("qT", [STACK + 1, HEADS, T], BF16)
        kT = sb("c_kT", [STACK + 1, HEADS, T], BF16)
        v = sb("v", [P, J, HEADS, 32])
        row_max = sb("row_max", [P, HEADS, J])
        neg_max = sb("neg_max", [P, HEADS, J])
        max_rows = sb("max_rows", [4 * J, G3, P], BF16)
        mlp = sb("mlp", [P, FC1_TILES, T])
        e = sb("e", [P, LIVE_E, T])
        att = sb("att", [P, 2, T])
        rden = sb("rden", [P, J, 4])
        xa = sb("xa", [P, J, C])
        xaT = sb("xaT", [CH, 2, T])
        o = sb("o", [P, J, C])
        ps_t = ps("c_ps_t", [P, 2, T])
        ps_m = ps("c_ps_m", [P, 2, T])
        ps_s = ps("c_ps_s", [P, 2, T])
        ps_a = ps("c_ps_a", [P, 2, T])
        loaded, w2_ready = kit.sems("c_loaded c_w2_ready")
        counted = [kit.sem("c_" + n) for n in (
            "var_ready rstd_ready yn_ready y_ready yT_psum yT_ready qk_psum qk_read stack_ready st_psum "
            "q_read k_read v_psum v_ready m_psum m_read mx_ready mxT_psum mxT_ready mlp_psum mlp_ready "
            "s_psum e_ready av_done a_read at_psum xa_ready xaT_psum xaT_ready o_psum o_read h_done").split()]
        (var_ready, rstd_ready, yn_ready, y_ready, yT_psum, yT_ready, qk_psum, qk_read, stack_ready, st_psum,
                   q_read, k_read, v_psum, v_ready, m_psum, m_read, mx_ready, mxT_psum, mxT_ready, mlp_psum, mlp_ready,
                   s_psum, e_ready, av_done, a_read, at_psum, xa_ready, xaT_psum, xaT_ready, o_psum, o_read, h_done) = counted
        max_placed = [kit.sem(f"c_max_placed{g}") for g in range(G3)]
        block = ctx.enter_context(nc.Block())
        NS = HEADS * J
        NM = 4 * J
        NT = 4 * J
        HH = HEADS // 2
        AHEAD = 1

        @block.sync
        def _(sp):
            for s in counted:
                sp.sem_inc(s, U)
            sp.dma_start(gamma[:, :], a["gamma1"].broadcast_to([P, C])).then_inc(loaded, 16)
            sp.dma_start(beta[:, :], a["beta1"].broadcast_to([P, C])).then_inc(loaded, 16)
            sp.dma_start(b2[:, :, :], a["b2"].broadcast_to([P, 2, C])).then_inc(loaded, 16)
            sp.dma_start(w1[:, :, :], a["w1"]).then_inc(loaded, 16)
            sp.dma_start(w2_mlp[:, :, :, :], a["w2_mlp"]).then_inc(loaded, 16)
            sp.dma_start(w2_att[:, :, :, :], a["w2_att"]).then_inc(loaded, 16)
            with sp.Fori(0, B) as t:
                for g in range(G3):
                    need(sp, mxT_ready, t, G3, g)
                    sp.dma_start(qT[STACK:STACK + 1, 4 * g:4 * g + 4, :], max_rows[:, g, :]).then_inc(max_placed[g], 16)

        @block.gpsimd
        def _(pool):
            def finish_y(t, ahead):
                blocks = bass.ds((t + ahead) * J, J)
                need(pool, var_ready, t, 1, ahead)
                ln_rstd(kit, pool, rstd[:, :], var_eps[:, :]).then_inc(rstd_ready, 1)
                need(pool, yn_ready, t, 1, ahead)
                pool.tensor_tensor(y[:, :, 0:C], y[:, :, 0:C], gamma[:, :].unsqueeze(1).broadcast_to([P, J, C]), ALU.mult)
                pool.drain()
                pool.tensor_tensor(y[:, :, 0:C], y[:, :, 0:C], beta[:, :].unsqueeze(1).broadcast_to([P, J, C]), ALU.add)
                pool.drain()
                for n, (lo, hi) in enumerate(BANDS):
                    pool.tensor_tensor(y[:, :, lo:hi], y[:, :, lo:hi], bc(bands[:, 0, blocks, n], hi - lo), ALU.mult)
                pool.tensor_copy(y[:, :, C], bands[:, 0, blocks, 0]).then_inc(y_ready, 1)

            def finish_h(t, ahead):
                blocks = bass.ds((t + ahead) * J, J)
                need(pool, o_read, t, 1, ahead)
                for n, (lo, hi) in enumerate(BANDS):
                    pool.tensor_tensor(o[:, :, lo:hi], o[:, :, lo:hi], bc(bands[:, 1, blocks, n], hi - lo), ALU.mult)
                pool.tensor_tensor(kit.h[:, blocks, :], kit.h[:, blocks, :], x1[:, blocks, :], ALU.add)
                pool.drain()
                pool.tensor_tensor(kit.h[:, blocks, :], kit.h[:, blocks, :], o[:, :, :], ALU.add).then_inc(h_done, 1)

            def stack(t, ahead, first):
                for j in range(J):
                    need(pool, qk_read, t, J, j + ahead * J)
                    if j == 0 and not first:
                        need(pool, st_psum, t, NT, NT - 1 + (ahead - 1) * NT)
                    kit.apart(pool)
                    hml = parts[:, j % 2].rearrange("p s (w h d) -> p w h s d", w=2, h=HEADS)
                    q_part, k_part = hml[:, 0], hml[:, 1]
                    qs = stacked[:, j, 0].rearrange("p h (s d) -> p h s d", s=PAIRS)
                    ks = stacked[:, j, 1].rearrange("p h (s d) -> p h s d", s=PAIRS)
                    pool.tensor_copy(qs[:, :, 0:3, :], q_part[:, :, 0:1, :].broadcast_to([P, HEADS, 3, HD]))
                    pool.tensor_copy(qs[:, :, 3:5, :], q_part[:, :, 1:2, :].broadcast_to([P, HEADS, 2, HD]))
                    pool.tensor_copy(qs[:, :, 5, :], q_part[:, :, 2, :])
                    pool.tensor_copy(ks[:, :, 0:3, :], k_part)
                    pool.tensor_copy(ks[:, :, 3:5, :], k_part[:, :, 0:2, :])
                    pool.tensor_copy(ks[:, :, 5, :], k_part[:, :, 0, :]).then_inc(stack_ready, 1)

            def turn(t, first=False, last=False):
                if not last:
                    finish_y(t, AHEAD)
                if not first:
                    finish_h(t, -1)
                if not last:
                    stack(t, AHEAD, False)

            finish_y(0, 0)
            stack(0, 0, True)
            turn(0, first=True)
            with pool.Fori(1, B - 1) as t:
                turn(t)
            turn(B - 1, last=True)
            finish_h(B - 1, 0)

        @block.vector
        def _(dve):
            def norm_stats(t, ahead):
                blocks = bass.ds((t + ahead) * J, J)
                dve.drain()
                ln_stats(dve, x1[:, blocks, :], stats, mv, var_eps, 1e-6).then_inc(var_ready, 1)

            def norm_apply(t, ahead, first=False):
                blocks = bass.ds((t + ahead) * J, J)
                need(dve, rstd_ready, t, 1, ahead)
                if not first:
                    need(dve, yT_psum, t, 1, ahead - 1)
                ln_apply(dve, y[:, :, 0:C], x1[:, blocks, :], mv, rstd).then_inc(yn_ready, 1)

            def split_qk(t, ahead, j):
                qk = ps_t[:, j % 2, 0:2 * C]
                hml = parts[:, j % 2]
                need(dve, qk_psum, t, J, j + ahead * J)
                need(dve, stack_ready, t, J, j + ahead * J, ago=2)
                dve.tensor_copy(hml[:, 0, :], qk)
                dve.drain()
                dve.tensor_tensor(rest[:, :], qk, hml[:, 0, :], ALU.subtract)
                dve.drain()
                dve.tensor_copy(hml[:, 1, :], rest[:, :])
                dve.drain()
                dve.tensor_tensor(hml[:, 2, :], rest[:, :], hml[:, 1, :], ALU.subtract).then_inc(qk_read, 1)

            def k_copy(t, i):
                j, half = i // 2, i % 2
                need(dve, st_psum, t, NT, 2 * i + 1)
                dve.tensor_copy(kT[0:STACK, half * HH:(half + 1) * HH, j * P:(j + 1) * P],
                                ps_s[0:STACK, 1, :].bitcast(BF16)[:, 0:HH * P].rearrange("p (h n) -> p h n", h=HH))\
                   .then_inc(k_read, 1)

            def v_copy(t, j):
                need(dve, v_psum, t, J, j)
                dve.tensor_copy(v[:, j, :, 0:HD], ps_m[:, j % 2, 0:C].rearrange("p (h d) -> p h d", h=HEADS))\
                   .then_inc(v_ready, 1)

            def row_maximum(t, n):
                need(dve, m_psum, t, NS, n)
                dve.tensor_reduce(row_max[:, n // J, n % J:n % J + 1], ps_m[:, n % 2, :], AX_X, ALU.max)\
                   .then_inc(m_read, 1)

            def place_maxima(t, g, first):
                dve.drain()
                dve.tensor_scalar(neg_max[:, 4 * g:4 * g + 4, :], row_max[:, 4 * g:4 * g + 4, :], -1.0, None,
                                  ALU.mult).then_inc(mx_ready, 1)
                need(dve, mxT_psum, t, G3, g)
                if not first:
                    dve.wait_ge(max_placed[g], t * 16)
                dve.tensor_copy(max_rows[:, g, :], ps_m[0:4 * J, 0, 0:P]).then_inc(mxT_ready, 1)

            def over_sum(t, g):
                got = ps_t[:, g % 2, :].rearrange("p (j i d) -> p j i d", j=J, i=4)
                dve.drain()
                need(dve, at_psum, t, G3, g)
                dve.reciprocal(rden[:, :, :], got[:, :, :, HD])
                dve.drain()
                for i in range(4):
                    last = dve.tensor_tensor(xa[:, :, (4 * g + i) * HD:(4 * g + i + 1) * HD], got[:, :, i, 0:HD],
                                             bc(rden[:, :, i], HD), ALU.mult)
                last.then_inc(xa_ready, 1)

            def o_copy(t, ahead):
                need(dve, o_psum, t, 1, ahead)
                need(dve, h_done, t, 1, ahead, ago=1)
                dve.tensor_tensor(o[:, :, :], ps_t[:, :, :].rearrange("p k (m n) -> p (k m) n", m=2)[:, :, 0:C],
                                  b2[:, 0:1, :].broadcast_to([P, J, C]), ALU.add).then_inc(o_read, 1)

            def turn(t, first=False, last=False):
                k_copy(t, 0)
                k_copy(t, 1)
                if not last:
                    norm_stats(t, AHEAD)
                k_copy(t, 2)
                k_copy(t, 3)
                v_copy(t, 0)
                v_copy(t, 1)
                if not last:
                    norm_apply(t, AHEAD)
                k_copy(t, 4)
                k_copy(t, 5)
                v_copy(t, 2)
                v_copy(t, 3)
                k_copy(t, 6)
                k_copy(t, 7)
                if not first:
                    o_copy(t, -1)
                for n in range(NM):
                    row_maximum(t, n)
                place_maxima(t, 0, first)
                for grp in range(G3 * J):
                    if grp // J < G3 - 1:
                        for n in range(NM + 4 * grp, NM + 4 * grp + 4):
                            row_maximum(t, n)
                    if grp % J == J - 1 and grp // J < G3 - 1:
                        place_maxima(t, grp // J + 1, first)
                    if not last and 2 <= grp < 2 + J:
                        split_qk(t, AHEAD, grp - 2)
                    if grp in (8, 10):
                        over_sum(t, (grp - 8) // 2)
                over_sum(t, G3 - 1)

            dve.memset(v[:, :, :, HD:HD + 1], 1.0)
            dve.memset(v[:, :, :, HD + 1:32], 0.0)
            dve.memset(kT[STACK:STACK + 1, :, :], 1.0)
            dve.wait_ge(loaded, 96)
            dve.tensor_tensor(w2_mlp[:, :, 0, :], w2_mlp[:, :, 0, :], w2_mlp[:, :, 1, :], ALU.add)
            dve.tensor_tensor(w2_att[:, :, 0, :], w2_att[:, :, 0, :], w2_att[:, :, 1, :], ALU.add)
            dve.tensor_tensor(b2[:, 0, :], b2[:, 0, :], b2[:, 1, :], ALU.add).then_inc(w2_ready, 1)
            norm_stats(0, 0)
            norm_apply(0, 0, first=True)
            for j in range(J):
                split_qk(0, 0, j)
            turn(0, first=True)
            with dve.Fori(1, B - 1) as t:
                turn(t)
            turn(B - 1, last=True)
            o_copy(B - 1, 0)

        @block.tensor
        def _(pe):
            def y_transpose(t, ahead):
                need(pe, y_ready, t, 1, ahead)
                need(pe, o_read, t, 1, ahead, ago=2)
                for j in range(J):
                    for c in range(2):
                        last = pe.transpose(ps_t[0:CH + c, c, j * P:(j + 1) * P], y[:, j, c * CH:(c + 1) * CH + c],
                                            kit.ident[:, :])
                last.then_inc(yT_psum, 1)

            def qk(t, ahead, j):
                if j < 2:
                    need(pe, yT_ready, t, 1, ahead)
                else:
                    need(pe, qk_read, t, J, j + ahead * J, ago=2)
                for c in range(2):
                    last = pe.matmul(ps_t[:, j % 2, 0:2 * C], yT[0:CH + c, c, j * P:(j + 1) * P],
                                     w1[0:CH + c, c, MLP:MLP + 2 * C], start=c == 0, stop=c == 1)
                last.then_inc(qk_psum, 1)

            def stack_transpose(t, n, first):
                j, half, w = n // 4, n // 2 % 2, n % 2
                need(pe, stack_ready, t, J, j)
                if n >= 2:
                    need(pe, (q_read, k_read)[w], t, NT // 2, n // 2, ago=1)
                elif not first:
                    need(pe, e_ready, t, NS, n, ago=2)
                out16 = ps_s[:, w, :].bitcast(BF16)
                for i in range(HH):
                    last = pe.transpose(out16[0:STACK, i * P:(i + 1) * P], stacked[:, j, w, half * HH + i, :],
                                        kit.ident16[:, :])
                last.then_inc(st_psum, 1)

            def values(t, j):
                if j < 2:
                    need(pe, m_read, t, NS, j, ago=2)
                else:
                    need(pe, v_ready, t, J, j, ago=2)
                for c in range(2):
                    last = pe.matmul(ps_m[:, j % 2, 0:C], yT[0:CH + c, c, j * P:(j + 1) * P],
                                     w1[0:CH + c, c, MLP + 2 * C:], start=c == 0, stop=c == 1)
                last.then_inc(v_psum, 1)

            def mlp_tile(t, m):
                if m < 2:
                    need(pe, a_read, t, G3, m, ago=1 + m)
                else:
                    need(pe, mlp_ready, t, FC1_TILES, m, ago=2)
                for c in range(2):
                    last = pe.matmul(ps_a[:, m % 2, :], w1[0:CH + c, c, m * P:(m + 1) * P], yT[0:CH + c, c, :],
                                     start=c == 0, stop=c == 1)
                last.then_inc(mlp_psum, 1)

            def maxima(t, n):
                h, j = n // J, n % J
                if n < 2:
                    need(pe, v_ready, t, J, 2 + n)
                else:
                    need(pe, m_read, t, NS, n, ago=2)
                if n % NM == 0 and n > 0:
                    need(pe, mxT_ready, t, G3, n // NM - 1)
                if n == 0:
                    need(pe, k_read, t, NT // 2, NT // 2 - 1)
                    need(pe, q_read, t, NT // 2, NT // 2 - 1)
                pe.matmul(ps_m[:, n % 2, :], qT[0:STACK, h, j * P:(j + 1) * P], kT[0:STACK, h, :],
                          start=True, stop=True).then_inc(m_psum, 1)

            def max_transpose(t, g):
                need(pe, mx_ready, t, G3, g)
                pe.transpose(ps_m[0:4 * J, 0, 0:P], neg_max[:, 4 * g:4 * g + 4, :], kit.ident[:, :])\
                  .then_inc(mxT_psum, 1)

            def scores(t, grp):
                g, kc = grp // J, grp % J
                for i in range(4):
                    n = 4 * grp + i
                    if n >= 2:
                        need(pe, e_ready, t, NS, n, ago=2)
                    if kc == 0 and i == 0:
                        pe.wait_ge(max_placed[g], t * 16 + 16)
                    pe.matmul(ps_s[:, n % 2, :], kT[:, 4 * g + i, kc * P:(kc + 1) * P], qT[:, 4 * g + i, :],
                              start=True, stop=True).then_inc(s_psum, 1)

            def weigh(t, grp):
                g, kc = grp // J, grp % J
                need(pe, e_ready, t, NS, 4 * grp + 3)
                if kc == 0:
                    if g < 2:
                        need(pe, mlp_ready, t, FC1_TILES, FC1_TILES - 2 + g)
                    else:
                        need(pe, a_read, t, G3, g, ago=2)
                for i in range(4):
                    last = pe.matmul(ps_a[32 * i:32 * i + 32, g % 2, :], v[:, kc, 4 * g + i, :],
                                     e[:, (4 * grp + i) % LIVE_E, :], start=kc == 0, stop=kc == J - 1,
                                     tile_position=(0, 32 * i))
                last.then_inc(av_done, 1)

            def att_transpose(t, g, no_qk):
                need(pe, a_read, t, G3, g)
                if g == 2:
                    need(pe, xa_ready, t, G3, 0)
                elif no_qk:
                    need(pe, o_read, t, 1, 0, ago=1)
                else:
                    need(pe, qk_read, t, J, J + 2 + g)
                for j in range(J):
                    last = pe.transpose(ps_t[:, g % 2, j * P:(j + 1) * P], att[:, g % 2, j * P:(j + 1) * P],
                                        kit.ident[:, :])
                last.then_inc(at_psum, 1)

            def xa_transpose(t, ahead):
                need(pe, xa_ready, t, G3, G3 - 1 + ahead * G3)
                for j in range(J):
                    for c in range(2):
                        last = pe.transpose(ps_t[0:CH, c, j * P:(j + 1) * P], xa[:, j, c * CH:(c + 1) * CH],
                                            kit.ident[:, :])
                last.then_inc(xaT_psum, 1)

            def out_rows(t, ahead, j):
                if j == 0:
                    need(pe, xaT_ready, t, 1, ahead)
                out_j = ps_t[:, j // 2, (j % 2) * 256:(j % 2) * 256 + C]
                for m in range(FC1_TILES):
                    pe.matmul(out_j, mlp[:, m, j * P:(j + 1) * P], w2_mlp[:, m, 0, :], start=m == 0, stop=False)
                for c in range(2):
                    last = pe.matmul(out_j, xaT[:, c, j * P:(j + 1) * P], w2_att[:, c, 0, :], start=False,
                                     stop=c == 1)
                if j == J - 1:
                    last.then_inc(o_psum, 1)

            def turn(t, first=False, last=False):
                for n in range(4):
                    stack_transpose(t, n, first)
                if not first:
                    xa_transpose(t, -1)
                for n in range(4, 8):
                    stack_transpose(t, n, first)
                values(t, 0)
                values(t, 1)
                if not first:
                    out_rows(t, -1, 0)
                    out_rows(t, -1, 1)
                for n in range(8, 12):
                    stack_transpose(t, n, first)
                values(t, 2)
                values(t, 3)
                if not first:
                    out_rows(t, -1, 2)
                for n in range(12, 16):
                    stack_transpose(t, n, first)
                if not first:
                    out_rows(t, -1, 3)
                for n in range(NM):
                    maxima(t, n)
                    if n % 4 == 3:
                        mlp_tile(t, n // 4)
                max_transpose(t, 0)
                mlp_tile(t, 4)
                mlp_tile(t, 5)
                for grp in range(G3 * J + 1):
                    if grp < G3 * J:
                        scores(t, grp)
                        if grp // J < G3 - 1:
                            for n in range(NM + 4 * grp, NM + 4 * grp + 4):
                                maxima(t, n)
                    if grp >= 1:
                        weigh(t, grp - 1)
                    if grp % J == J - 1 and grp // J < G3 - 1:
                        max_transpose(t, grp // J + 1)
                    if not last and grp == 0:
                        y_transpose(t, AHEAD)
                    if not last and 1 <= grp < 1 + J:
                        qk(t, AHEAD, grp - 1)
                    if grp in (7, 9):
                        att_transpose(t, (grp - 7) // 2, last)
                att_transpose(t, G3 - 1, last)

            pe.wait_ge(loaded, 96)
            pe.wait_ge(w2_ready, 1)
            y_transpose(0, 0)
            for j in range(J):
                qk(0, 0, j)
            turn(0, first=True)
            with pe.Fori(1, B - 1) as t:
                turn(t)
            turn(B - 1, last=True)
            xa_transpose(B - 1, 0)
            for j in range(J):
                out_rows(B - 1, 0, j)

        @block.scalar
        def _(act):
            def y_copy(t, ahead):
                need(act, yT_psum, t, 1, ahead)
                act.activation(yT[0:CH, 0, :], ps_t[0:CH, 0, :], ACT.Copy)
                act.activation(yT[:, 1, :], ps_t[0:CH + 1, 1, :], ACT.Copy).then_inc(yT_ready, 1)

            def xa_copy(t, ahead):
                need(act, xaT_psum, t, 1, ahead)
                act.activation(xaT[:, :, :], ps_t[0:CH, :, :], ACT.Copy).then_inc(xaT_ready, 1)

            def att_copy(t, g):
                need(act, av_done, t, G3 * J, J * g + J - 1)
                need(act, at_psum, t, G3, g, ago=2)
                act.activation(att[:, g % 2, :], ps_a[:, g % 2, :], ACT.Copy).then_inc(a_read, 1)

            def turn(t, first=False, last=False):
                for i in range(NT // 2):
                    j, half = i // 2, i % 2
                    need(act, st_psum, t, NT, 2 * i)
                    act.activation(qT[0:STACK, half * HH:(half + 1) * HH, j * P:(j + 1) * P],
                                   ps_s[0:STACK, 0, :].bitcast(BF16)[:, 0:HH * P].rearrange("p (h n) -> p h n", h=HH),
                                   ACT.Copy).then_inc(q_read, 1)
                    if i == 1 and not first:
                        xa_copy(t, -1)
                for m in range(FC1_TILES):
                    need(act, mlp_psum, t, FC1_TILES, m)
                    if m == 0:
                        need(act, o_psum, t, 1, 0, ago=1)
                    act.activation(mlp[:, m, :], ps_a[:, m % 2, :], ACT.Gelu).then_inc(mlp_ready, 1)
                for n in range(NS):
                    grp = n // 4
                    need(act, s_psum, t, NS, n)
                    if n % 4 == 0:
                        need(act, av_done, t, G3 * J, grp, ago=2)
                    act.activation(e[:, n % LIVE_E, :], ps_s[:, n % 2, :], ACT.Exp, scale=QSCALE).then_inc(e_ready, 1)
                    if n == 3 and not last:
                        y_copy(t, AHEAD)
                    if n % NM == 7 and n > NM:
                        att_copy(t, n // NM - 1)
                att_copy(t, G3 - 1)

            y_copy(0, 0)
            turn(0, first=True)
            with act.Fori(1, B - 1) as t:
                turn(t)
            turn(B - 1, last=True)
            xa_copy(B - 1, 0)


DI = 2 * C
NH, HP = 6, DI // 6
DS = 64
TAPS = 4
ZW = DI + NH
KD = DI // P
LOWEST_LOG = -1e30


def rows_of(ps_pair):
    return ps_pair[:, :, :].rearrange("p k (m n) -> p (k m) n", m=2)


def state_space_block(kit, a):
    nc = kit.nc
    with kit.phase() as ctx:
        sb, ps = tile_maker(nc, ctx), psum_maker(nc, ctx)
        ln = sb("ln", [P, 4, C])
        wz = sb("wz", [CH, 2, ZW])
        wx = sb("wx", [CH, 2, 4 * P])
        conv_w = sb("conv_w", [P, 4, TAPS])
        conv_b = sb("conv_b", [P, 4])
        dt_bias = sb("dt_bias", [P, NH])
        neg_a = sb("neg_a", [P, NH])
        d_skip = sb("d_skip", [P, NH])
        norm_w = sb("norm_w", [P, DI])
        w_out = sb("w_out", [P, KD, C])
        wf1 = sb("wf1", [CH, 2, 6 * P])
        wf2 = sb("wf2", [P, KD, C])
        upto = sb("upto", [P, P])
        after16 = sb("after16", [P, P], BF16)
        ones = sb("d_ones", [P, P])
        stats = sb("d_stats", [P, J, 6])
        mv = sb("d_mv", [P, J, 2])
        var_eps = sb("d_var_eps", [P, J])
        rstd = sb("d_rstd", [P, J])
        xm = sb("xm", [P, J, C])
        y = sb("d_y", [P, J, C])
        y2 = sb("d_y2", [P, J, C])
        yT = sb("d_yT", [CH, 2, T])
        silu_z = sb("silu_z", [P, J, DI])
        dt_raw = sb("dt_raw", [P, J, NH])
        dt = sb("dt", [P, J, NH])
        dt_pos = sb("dt_pos", [P, J, NH])
        dt_e = sb("dt_e", [P, J, NH])
        dt_u = sb("dt_u", [P, J, NH])
        dt_d = sb("dt_d", [P, J, NH])
        dt_l = sb("dt_l", [P, J, NH])
        log_a = sb("log_a", [P, J, NH])
        sums = sb("sums", [P, 3, J, NH])
        neg_cs = sb("neg_cs", [P, J, NH])
        decays = sb("decays", [P, 3, J, NH])
        xin = sb("xin", [P, 4, TAPS - 1 + T])
        conv = sb("conv", [P, 4, T])
        c_low = sb("c_low", [DS, T])
        x_tm = sb("x_tm", [P, J, 4 * P])
        dtx = sb("dtx", [P, J, DI])
        dtx_rest = sb("dtx_rest", [P, J, DI])
        x_skip = sb("x_skip", [P, J, DI])
        seg = sb("seg", [P, J, NH, P])
        state = sb("state", [DS, DI])
        yy = sb("yy", [P, J, DI])
        square = sb("square", [P, DI])
        ms = sb("ms", [P, J])
        rms = sb("rms", [P, J])
        yyT = sb("yyT", [P, KD, T])
        x2 = sb("x2", [P, J, C])
        gate = sb("d_gate", [P, T])
        f = sb("f", [P, KD, T])
        ps_t = ps("d_ps_t", [P, 2, T])
        ps_m = ps("d_ps_m", [P, 2, T])
        ps_cb = ps("d_ps_cb", [P, J, P])
        ps_y = ps("d_ps_y", [P, T])
        ps_z = ps("d_ps_z", [P, T])
        ps_s = ps("d_ps_s", [P, T])
        names = ("var_ready rstd_ready y_ready yT_psum yT_ready z_psum z_read dt_read x_psum x_read conv_ready "
                 "silu_ready abs_ready e_ready u_ready l_ready log_ready sums_psum sums_ready decays_ready row_psum "
                 "seg_ready xtm_psum xtm_ready cb_psum dtx_ready skip_ready mt_ready diag_psum off_psum new_psum "
                 "state_ready chunk_ready square_ready ms_ready rms_ready norm_ready yyT_psum yyT_ready x2_psum "
                 "g_psum a_psum g_ready f_ready o_psum o_read")
        s = {n: kit.sem("d_" + n) for n in names.split()}
        loaded, tri_made, consts, a_exp = kit.sems("d_loaded d_tri_made d_consts d_a_exp")
        c_moved = kit.sem("d_c_moved")
        LOADS = 12
        block = ctx.enter_context(nc.Block())

        @block.sync
        def _(sp):
            for x in s.values():
                sp.sem_inc(x, U)
            for dst, src in ((ln[:, :, :], a["ln12"].broadcast_to([P, 4, C])), (wz[:, :, :], a["wz"]),
                             (wx[:, :, :], a["wx"]), (conv_w[:, :, :], a["conv_w"]), (conv_b[:, :], a["conv_b"]),
                             (dt_bias[:, :], a["dt_bias"].broadcast_to([P, NH])),
                             (neg_a[:, :], a["a_log"].broadcast_to([P, NH])),
                             (d_skip[:, :], a["d_skip"].broadcast_to([P, NH])),
                             (norm_w[:, :], a["norm_w"].broadcast_to([P, DI])), (w_out[:, :, :], a["w_out"]),
                             (wf1[:, :, :], a["wf1"]), (wf2[:, :, :], a["wf2"])):
                sp.dma_start(dst, src).then_inc(loaded, 16)
            with sp.Fori(0, B) as t:
                need(sp, s["silu_ready"], t, 4, 3)
                sp.dma_start(c_low[:, :], conv[DS:P, 3, :]).then_inc(c_moved, 16)

        @block.gpsimd
        def _(pool):
            pool.memset(ones[:, :], 1.0).then_inc(tri_made, 1)
            pool.memset(after16[:, :], 0.0).then_inc(tri_made, 1)
            pool.wait_ge(tri_made, 2)
            pool.affine_select(out=upto[:, :], in_=ones[:, :], compare_op=ALU.is_ge, fill=0.0, base=0,
                               pattern=[[1, P]], channel_multiplier=-1).then_inc(consts, 1)
            pool.affine_select(out=after16[:, :], in_=after16[:, :], compare_op=ALU.is_ge, fill=LOWEST_LOG, base=0,
                               pattern=[[1, P]], channel_multiplier=-1).then_inc(consts, 1)

            def norm(t, k):
                need(pool, s["var_ready"], t, 3, k)
                ln_rstd(kit, pool, rstd[:, :], var_eps[:, :]).then_inc(s["rstd_ready"], 1)

            def turn(t, last=False):
                for j in range(J):
                    need(pool, s["xtm_ready"], t, J, j)
                    pool.tensor_tensor(x_skip[:, j].rearrange("p (h d) -> p h d", h=NH),
                                       x_tm[:, j, 0:DI].rearrange("p (h d) -> p h d", h=NH),
                                       bc(d_skip[:, :], HP), ALU.mult).then_inc(s["skip_ready"], 1)
                need(pool, s["ms_ready"], t, 1, 0)
                pool.tensor_tensor(rms[:, :], ms[:, :], kit.minus_half[:, 0:J], ALU.pow).then_inc(s["rms_ready"], 1)
                for k in (2,) if last else (2, 3, 4):
                    norm(t, k)

            norm(0, 0)
            norm(0, 1)
            with pool.Fori(0, B - 1) as t:
                turn(t)
            turn(B - 1, last=True)

        @block.vector
        def _(dve):
            dve.memset(xin[:, :, 0:TAPS - 1], 0.0)
            dve.wait_ge(loaded, 16 * LOADS)
            dve.wait_ge(a_exp, 1)
            dve.tensor_scalar(neg_a[:, :], neg_a[:, :], -1.0, None, ALU.mult)

            def affine(dst, k):
                dve.drain()
                dve.tensor_tensor(dst, dst, ln[:, 2 * k:2 * k + 1, :].broadcast_to([P, J, C]), ALU.mult)
                dve.drain()
                return dve.tensor_tensor(dst, dst, ln[:, 2 * k + 1:2 * k + 2, :].broadcast_to([P, J, C]), ALU.add)

            def norm_1(t, ahead):
                blocks = bass.ds((t + ahead) * J, J)
                dve.drain()
                ln_stats(dve, kit.h[:, blocks, :], stats, mv, var_eps, 1e-5).then_inc(s["var_ready"], 1)
                need(dve, s["rstd_ready"], t, 3, 3 * ahead)
                ln_apply(dve, xm, kit.h[:, blocks, :], mv, rstd)
                dve.drain()

            def norm_2(t, ahead):
                ln_stats(dve, xm, stats, mv, var_eps, 1e-5).then_inc(s["var_ready"], 1)
                need(dve, s["rstd_ready"], t, 3, 3 * ahead + 1)
                ln_apply(dve, y, xm, mv, rstd)

            def conv_tile(t, m):
                need(dve, s["x_read"], t, 4, m)
                dve.tensor_scalar(conv[:, m, :], xin[:, m, 0:T], conv_w[:, m, 0:1], conv_b[:, m:m + 1],
                                  ALU.mult, ALU.add)
                for k in range(1, TAPS):
                    dve.drain()
                    last = dve.scalar_tensor_tensor(out=conv[:, m, :], in0=xin[:, m, k:k + T],
                                                    scalar=conv_w[:, m, k:k + 1], in1=conv[:, m, :],
                                                    op0=ALU.mult, op1=ALU.add)
                last.then_inc(s["conv_ready"], 1)

            def turn(t, last_turn=False):
                blocks = bass.ds(t * J, J)
                for j in range(J):
                    need(dve, s["z_read"], t, J, j)
                    last = dve.tensor_tensor(dt[:, j, :], dt_raw[:, j, :], dt_bias[:, :], ALU.add)
                last.then_inc(s["dt_read"], 1)
                dve.drain()
                dve.tensor_scalar(dt_pos[:, :, :], dt[:, :, :], 0.0, None, ALU.max)
                dve.tensor_scalar(dt_d[:, :, :], dt[:, :, :], -1.0, None, ALU.mult)
                dve.drain()
                dve.tensor_tensor(dt_e[:, :, :], dt[:, :, :], dt_d[:, :, :], ALU.min).then_inc(s["abs_ready"], 1)
                conv_tile(t, 0)
                need(dve, s["e_ready"], t, 1, 0)
                dve.tensor_scalar(dt_u[:, :, :], dt_e[:, :, :], 1.0, None, ALU.add).then_inc(s["u_ready"], 1)
                dve.drain()
                dve.tensor_scalar(dt_d[:, :, :], dt_u[:, :, :], 1.0, None, ALU.subtract)
                dve.drain()
                dve.tensor_scalar(dt[:, :, :], dt_d[:, :, :], 0.0, None, ALU.is_equal)
                dve.tensor_scalar(dt_d[:, :, :], dt_d[:, :, :], 1e-30, None, ALU.max)
                dve.drain()
                dve.reciprocal(dt_d[:, :, :], dt_d[:, :, :])
                conv_tile(t, 1)
                dve.drain()
                need(dve, s["l_ready"], t, 1, 0)
                dve.tensor_tensor(dt_d[:, :, :], dt_d[:, :, :], dt_l[:, :, :], ALU.mult)
                dve.drain()
                dve.tensor_tensor(dt_d[:, :, :], dt_d[:, :, :], dt[:, :, :], ALU.add)
                dve.drain()
                dve.tensor_tensor(dt_d[:, :, :], dt_d[:, :, :], dt_e[:, :, :], ALU.mult)
                dve.drain()
                dve.tensor_tensor(dt[:, :, :], dt_d[:, :, :], dt_pos[:, :, :], ALU.add)
                dve.drain()
                dve.tensor_tensor(log_a[:, :, :], dt[:, :, :], neg_a[:, :].unsqueeze(1).broadcast_to([P, J, NH]), ALU.mult)
                dve.drain()
                dve.tensor_scalar(log_a[:, :, :], log_a[:, :, :], LOWEST_LOG, None, ALU.max).then_inc(s["log_ready"], 1)
                conv_tile(t, 2)
                need(dve, s["sums_psum"], t, 1, 0)
                got = ps_s[:, DI:DI + 2 * J * NH].rearrange("p (w j h) -> p w j h", w=2, j=J)
                dve.tensor_copy(sums[:, 0:2], got)
                dve.drain()
                dve.tensor_scalar(neg_cs[:, :, :], sums[:, 0], -1.0, None, ALU.mult)
                dve.tensor_tensor(sums[:, 2], sums[:, 1], sums[:, 0], ALU.subtract).then_inc(s["sums_ready"], 1)
                conv_tile(t, 3)
                need(dve, s["decays_ready"], t, 1, 0)
                by_head = lambda x: x.rearrange("p (h d) -> p h d", h=NH)
                for j in range(J):
                    need(dve, s["xtm_ready"], t, J, j)
                    dve.tensor_tensor(by_head(dtx[:, j]), by_head(x_tm[:, j, 0:DI]), bc(dt[:, j, :], HP), ALU.mult)
                    dve.drain()
                    dve.tensor_tensor(by_head(dtx_rest[:, j]), by_head(dtx[:, j]), bc(decays[:, 2, j, :], HP), ALU.mult)\
                       .then_inc(s["dtx_ready"], 1)
                need(dve, s["cb_psum"], t, 1, 0)
                for j in range(J):
                    need(dve, s["seg_ready"], t, 2 * J, 2 * j + 1)
                    dve.tensor_tensor(seg[:, j], seg[:, j], ps_cb[:, j:j + 1, :].broadcast_to([P, NH, P]), ALU.mult)\
                       .then_inc(s["mt_ready"], 1)
                for j in range(J):
                    if j < J - 1:
                        need(dve, s["new_psum"], t, J - 1, j)
                        if j > 0:
                            need(dve, s["off_psum"], t, J - 1, j - 1)
                            dve.tensor_tensor(by_head(state[:, :]), by_head(state[:, :]),
                                              bc(decays[0:DS, 1, j, :], HP), ALU.mult)
                            dve.drain()
                            dve.tensor_tensor(state[:, :], state[:, :], ps_s[0:DS, 0:DI], ALU.add)\
                               .then_inc(s["state_ready"], 1)
                        else:
                            dve.tensor_copy(state[:, :], ps_s[0:DS, 0:DI]).then_inc(s["state_ready"], 1)
                    need(dve, s["diag_psum"], t, J, j)
                    need(dve, s["skip_ready"], t, J, j)
                    dve.tensor_tensor(x_skip[:, j], x_skip[:, j], ps_y[:, 0:DI], ALU.add)
                    if j > 0:
                        need(dve, s["off_psum"], t, J - 1, j - 1)
                        dve.tensor_tensor(by_head(yy[:, j]), by_head(ps_z[:, 0:DI]), bc(decays[:, 0, j, :], HP), ALU.mult)
                        dve.drain()
                        dve.tensor_tensor(x_skip[:, j], x_skip[:, j], yy[:, j], ALU.add)
                    dve.drain()
                    dve.tensor_tensor(yy[:, j], x_skip[:, j], silu_z[:, j], ALU.mult).then_inc(s["chunk_ready"], 1)
                need(dve, s["square_ready"], t, J, J - 1)
                dve.tensor_scalar(ms[:, :], ms[:, :], 1.0 / DI, 1e-5, ALU.mult, ALU.add).then_inc(s["ms_ready"], 1)
                need(dve, s["rms_ready"], t, 1, 0)
                for j in range(J):
                    dve.scalar_tensor_tensor(out=yy[:, j], in0=yy[:, j], scalar=rms[:, j:j + 1], in1=norm_w[:, :],
                                             op0=ALU.mult, op1=ALU.mult).then_inc(s["norm_ready"], 1)
                need(dve, s["x2_psum"], t, 1, 0)
                dve.tensor_tensor(x2[:, :, :], rows_of(ps_t)[:, :, 0:C], xm[:, :, :], ALU.add)
                dve.drain()
                ln_stats(dve, x2, stats, mv, var_eps, 1e-5).then_inc(s["var_ready"], 1)
                need(dve, s["rstd_ready"], t, 3, 2)
                ln_apply(dve, y2, x2, mv, rstd)
                affine(y2[:, :, :], 1).then_inc(s["y_ready"], 1)
                for m in range(KD):
                    if not last_turn:
                        if m == 0:
                            norm_1(t, 1)
                        elif m == 1:
                            norm_2(t, 1)
                        else:
                            affine(y[:, :, :], 0).then_inc(s["y_ready"], 1)
                    need(dve, s["a_psum"], t, KD, m)
                    need(dve, s["g_ready"], t, KD, m)
                    dve.tensor_tensor(f[:, m, :], ps_m[:, 1, :], gate[:, :], ALU.mult).then_inc(s["f_ready"], 1)
                need(dve, s["o_psum"], t, 1, 0)
                dve.tensor_tensor(x2[:, :, :], x2[:, :, :], rows_of(ps_t)[:, :, 0:C], ALU.add).then_inc(s["o_read"], 1)
                dve.drain()
                dve.tensor_tensor(kit.h[:, blocks, :], kit.h[:, blocks, :], x2[:, :, :], ALU.add)

            norm_1(0, 0)
            norm_2(0, 0)
            affine(y[:, :, :], 0).then_inc(s["y_ready"], 1)
            with dve.Fori(0, B - 1) as t:
                turn(t)
            turn(B - 1, last_turn=True)

        @block.tensor
        def _(pe):
            pe.wait_ge(loaded, 16 * LOADS)
            pe.wait_ge(consts, 2)

            def turn_rows(y):
                for j in range(J):
                    for c in range(2):
                        last = pe.transpose(ps_t[0:CH, c, j * P:(j + 1) * P], y[:, j, c * CH:(c + 1) * CH],
                                            kit.ident[:, :])
                last.then_inc(s["yT_psum"], 1)

            with pe.Fori(0, B) as t:
                need(pe, s["y_ready"], t, 2, 0)
                need(pe, s["o_read"], t, 1, 0, ago=1)
                turn_rows(y)
                need(pe, s["yT_ready"], t, 2, 0)
                for j in range(J):
                    if j < 2:
                        need(pe, s["f_ready"], t, KD, 0, ago=1)
                    else:
                        need(pe, s["z_read"], t, J, j, ago=2)
                    for c in range(2):
                        last = pe.matmul(ps_m[:, j % 2, 0:ZW], yT[:, c, j * P:(j + 1) * P], wz[:, c, :],
                                         start=c == 0, stop=c == 1)
                    last.then_inc(s["z_psum"], 1)
                for m in range(4):
                    if m < 2:
                        need(pe, s["z_read"], t, J, J - 2 + m)
                    else:
                        need(pe, s["x_read"], t, 4, m, ago=2)
                    for c in range(2):
                        last = pe.matmul(ps_m[:, m % 2, :], wx[:, c, m * P:(m + 1) * P], yT[:, c, :],
                                         start=c == 0, stop=c == 1)
                    last.then_inc(s["x_psum"], 1)
                need(pe, s["log_ready"], t, 1, 0)
                flat = log_a[:, :, :].rearrange("p j h -> p (j h)")
                pe.matmul(ps_s[:, DI:DI + J * NH], upto[:, :], flat, start=True, stop=True)
                pe.matmul(ps_s[:, DI + J * NH:DI + 2 * J * NH], ones[:, :], flat, start=True, stop=True)\
                  .then_inc(s["sums_psum"], 1)
                for n in range(2 * J):
                    j, half = n // 2, n % 2
                    if n >= 2:
                        need(pe, s["seg_ready"], t, 2 * J, n, ago=2)
                    for i in range(3):
                        dst = ps_t[:, half, i * P:(i + 1) * P]
                        pe.matmul(dst, log_a[:, j, 3 * half + i:3 * half + i + 1].broadcast_to([P, P]), upto[:, :],
                                  start=True, stop=False)
                        last = pe.matmul(dst, kit.ident16[:, :], after16[:, :], start=False, stop=True)
                    last.then_inc(s["row_psum"], 1)
                for j in range(J):
                    if j == 0:
                        need(pe, s["silu_ready"], t, 4, 3)
                    if j < 2:
                        need(pe, s["x_read"], t, 4, 2 + j)
                    else:
                        need(pe, s["xtm_ready"], t, J, j, ago=2)
                    for m in range(4):
                        last = pe.transpose(ps_m[:, j % 2, m * P:(m + 1) * P], conv[:, m, j * P:(j + 1) * P],
                                            kit.ident[:, :])
                    last.then_inc(s["xtm_psum"], 1)
                pe.wait_ge(c_moved, t * 16 + 16)
                for j in range(J):
                    last = pe.matmul(ps_cb[:, j, :], conv[0:DS, 3, j * P:(j + 1) * P], c_low[:, j * P:(j + 1) * P],
                                     start=True, stop=True)
                last.then_inc(s["cb_psum"], 1)
                for j in range(J):
                    need(pe, s["dtx_ready"], t, J, j)
                    if j < J - 1:
                        if j > 0:
                            need(pe, s["state_ready"], t, J - 1, j - 1)
                        pe.matmul(ps_s[0:DS, 0:DI], x_tm[:, j, DI:DI + DS], dtx_rest[:, j, :], start=True, stop=True)\
                          .then_inc(s["new_psum"], 1)
                    need(pe, s["mt_ready"], t, J, j)
                    if j > 0:
                        need(pe, s["chunk_ready"], t, J, j - 1)
                    for h in range(NH):
                        last = pe.matmul(ps_y[:, h * HP:(h + 1) * HP], seg[:, j, h, :], dtx[:, j, h * HP:(h + 1) * HP],
                                         start=True, stop=True)
                    last.then_inc(s["diag_psum"], 1)
                    if j > 0:
                        need(pe, s["state_ready"], t, J - 1, j - 1)
                        pe.matmul(ps_z[:, 0:DI], c_low[:, j * P:(j + 1) * P], state[:, :], start=True, stop=True)\
                          .then_inc(s["off_psum"], 1)
                for j in range(J):
                    need(pe, s["norm_ready"], t, J, j)
                    if j >= 2:
                        need(pe, s["yyT_ready"], t, J, j, ago=2)
                    for m in range(KD):
                        last = pe.transpose(ps_m[:, j % 2, m * P:(m + 1) * P], yy[:, j, m * P:(m + 1) * P],
                                            kit.ident[:, :])
                    last.then_inc(s["yyT_psum"], 1)
                need(pe, s["yyT_ready"], t, J, J - 1)
                for j in range(J):
                    for m in range(KD):
                        last = pe.matmul(rows_of(ps_t)[:, j, 0:C], yyT[:, m, j * P:(j + 1) * P], w_out[:, m, :],
                                         start=m == 0, stop=m == KD - 1)
                last.then_inc(s["x2_psum"], 1)
                need(pe, s["y_ready"], t, 2, 1)
                turn_rows(y2)
                need(pe, s["yT_ready"], t, 2, 1)
                for m in range(KD):
                    if m == 0:
                        need(pe, s["yyT_ready"], t, J, J - 1)
                    else:
                        need(pe, s["g_ready"], t, KD, m - 1)
                    for c in range(2):
                        last = pe.matmul(ps_m[:, 0, :], wf1[:, c, (KD + m) * P:(KD + m + 1) * P], yT[:, c, :],
                                         start=c == 0, stop=c == 1)
                    last.then_inc(s["g_psum"], 1)
                    if m > 0:
                        need(pe, s["f_ready"], t, KD, m - 1)
                    for c in range(2):
                        last = pe.matmul(ps_m[:, 1, :], wf1[:, c, m * P:(m + 1) * P], yT[:, c, :],
                                         start=c == 0, stop=c == 1)
                    last.then_inc(s["a_psum"], 1)
                need(pe, s["f_ready"], t, KD, KD - 1)
                for j in range(J):
                    for m in range(KD):
                        last = pe.matmul(rows_of(ps_t)[:, j, 0:C], f[:, m, j * P:(j + 1) * P], wf2[:, m, :],
                                         start=m == 0, stop=m == KD - 1)
                last.then_inc(s["o_psum"], 1)

        @block.scalar
        def _(act):
            act.wait_ge(loaded, 16 * LOADS)
            act.activation(neg_a[:, :], neg_a[:, :], ACT.Exp).then_inc(a_exp, 1)

            with act.Fori(0, B) as t:
                need(act, s["yT_psum"], t, 2, 0)
                act.activation(yT[:, :, :], ps_t[0:CH, :, :], ACT.Copy).then_inc(s["yT_ready"], 1)
                for j in range(J):
                    need(act, s["z_psum"], t, J, j)
                    if j == 0:
                        need(act, s["dt_read"], t, 1, 0, ago=1)
                    act.activation(dt_raw[:, j], ps_m[:, j % 2, DI:ZW], ACT.Copy)
                    act.activation(silu_z[:, j], ps_m[:, j % 2, 0:DI], ACT.Silu).then_inc(s["z_read"], 1)
                for m in range(4):
                    if m == 2:
                        need(act, s["abs_ready"], t, 1, 0)
                        act.activation(dt_e[:, :, :], dt_e[:, :, :], ACT.Exp).then_inc(s["e_ready"], 1)
                    need(act, s["x_psum"], t, 4, m)
                    act.activation(xin[:, m, TAPS - 1:], ps_m[:, m % 2, :], ACT.Copy).then_inc(s["x_read"], 1)
                need(act, s["u_ready"], t, 1, 0)
                act.activation(dt_l[:, :, :], dt_u[:, :, :], ACT.Ln).then_inc(s["l_ready"], 1)
                need(act, s["sums_ready"], t, 1, 0)
                act.activation(decays[:, :, :, :], sums[:, :, :, :], ACT.Exp).then_inc(s["decays_ready"], 1)
                for n in range(2 * J):
                    j, half = n // 2, n % 2
                    need(act, s["row_psum"], t, 2 * J, n)
                    for i in range(3):
                        h = 3 * half + i
                        last = act.activation(seg[:, j, h, :], ps_t[:, half, i * P:(i + 1) * P], ACT.Exp,
                                              bias=neg_cs[:, j, h:h + 1])
                    last.then_inc(s["seg_ready"], 1)
                for m in range(4):
                    need(act, s["conv_ready"], t, 4, m)
                    act.activation(conv[:, m, :], conv[:, m, :], ACT.Silu).then_inc(s["silu_ready"], 1)
                for j in range(J):
                    need(act, s["xtm_psum"], t, J, j)
                    act.activation(x_tm[:, j, :], ps_m[:, j % 2, :], ACT.Copy).then_inc(s["xtm_ready"], 1)
                for j in range(J):
                    act.drain()
                    need(act, s["chunk_ready"], t, J, j)
                    act.activation(square[:, :], yy[:, j], ACT.Square, accum_out=ms[:, j:j + 1])\
                       .then_inc(s["square_ready"], 1)
                for j in range(J):
                    need(act, s["yyT_psum"], t, J, j)
                    act.activation(yyT[:, :, j * P:(j + 1) * P], ps_m[:, j % 2, 0:DI].rearrange(
                        "p (m n) -> p m n", m=KD), ACT.Copy).then_inc(s["yyT_ready"], 1)
                need(act, s["yT_psum"], t, 2, 1)
                act.activation(yT[:, :, :], ps_t[0:CH, :, :], ACT.Copy).then_inc(s["yT_ready"], 1)
                for m in range(KD):
                    need(act, s["g_psum"], t, KD, m)
                    if m > 0:
                        need(act, s["f_ready"], t, KD, m - 1)
                    act.activation(gate[:, :], ps_m[:, 0, :], ACT.Silu).then_inc(s["g_ready"], 1)


E8 = 8
INNER = 4 * C
IT = INNER // P
CAP = 1280
SLOTS = E8 * CAP
NOWHERE = float(1 << 20)
LO = P // E8


class SharedExpert:

    def __init__(self, kit, a, x1, ctx, batch0):
        sb, ps = tile_maker(kit.nc, ctx), psum_maker(kit.nc, ctx)
        n = f"e{batch0}_"
        self.kit, self.a, self.x1, self.batch0, self.turns = kit, a, x1, batch0, B // 2
        self.s1 = sb(n + "s1", [CH, 2, INNER])
        self.s3 = sb(n + "s3", [CH, 2, INNER])
        self.s2 = sb(n + "s2", [P, IT, C])
        self.x = sb(n + "x", [P, J, C])
        self.xT = sb(n + "xT", [CH, 2, T])
        self.gate = sb(n + "gate", [P, 2, T])
        self.f = sb(n + "f", [P, IT, T])
        self.ps_t = ps(n + "ps_t", [P, 2, T])
        self.ps_g = ps(n + "ps_g", [P, 2, T])
        self.ps_u = ps(n + "ps_u", [P, 2, T])
        self.ps_o = ps(n + "ps_o", [P, 2, T])
        self.loaded = kit.sem(n + "loaded")
        self.counted = (self.x_ready, self.xT_psum, self.xT_ready, self.g_psum, self.g_ready, self.u_psum,
                        self.f_ready, self.o_psum, self.h_done) = [
            kit.sem(n + m) for m in "x_ready xT_psum xT_ready g_psum g_ready u_psum f_ready o_psum h_done".split()]

    def sync(self, sp):
        for x in self.counted:
            sp.sem_inc(x, U)
        for dst, src in ((self.s1[:, :, :], self.a["s1"]), (self.s3[:, :, :], self.a["s3"]),
                         (self.s2[:, :, :], self.a["s2"])):
            sp.dma_start(dst, src).then_inc(self.loaded, 16)

    def add_to_h(self, dve, t, back):
        need(dve, self.o_psum, t, 1, -back)
        blocks = bass.ds((t + (self.batch0 - back)) * J, J)
        dve.tensor_tensor(self.kit.h[:, blocks, :], self.kit.h[:, blocks, :], rows_of(self.ps_o)[:, :, 0:C],
                          ALU.add).then_inc(self.h_done, 1)

    def vector(self, dve, t, first=False):
        if not first:
            self.add_to_h(dve, t, 1)
        for m in range(IT):
            need(dve, self.g_ready, t, IT, m)
            need(dve, self.u_psum, t, IT, m)
            dve.tensor_tensor(self.f[:, m, :], self.ps_u[:, m % 2, :], self.gate[:, m % 2, :], ALU.mult)\
               .then_inc(self.f_ready, 1)

    def vector_end(self, dve):
        self.add_to_h(dve, self.turns - 1, 0)
        dve.drain()

    def tensor(self, pe):
        def outputs(t, back):
            need(pe, self.f_ready, t, IT, IT - 1 - back * IT)
            need(pe, self.h_done, t, 1, -back, ago=1)
            for j in range(J):
                for m in range(IT):
                    last = pe.matmul(rows_of(self.ps_o)[:, j, 0:C], self.f[:, m, j * P:(j + 1) * P], self.s2[:, m, :],
                                     start=m == 0, stop=m == IT - 1)
            last.then_inc(self.o_psum, 1)

        def turn(t, first=False):
            need(pe, self.x_ready, t, 1, 0)
            need(pe, self.xT_ready, t, 1, 0, ago=1)
            for j in range(J):
                for c in range(2):
                    last = pe.transpose(self.ps_t[0:CH, c, j * P:(j + 1) * P], self.x[:, j, c * CH:(c + 1) * CH],
                                        self.kit.ident[:, :])
            last.then_inc(self.xT_psum, 1)
            if not first:
                outputs(t, 1)
            need(pe, self.xT_ready, t, 1, 0)
            for m in range(IT):
                need(pe, self.g_ready, t, IT, m, ago=2)
                for c in range(2):
                    last = pe.matmul(self.ps_g[:, m % 2, :], self.s1[:, c, m * P:(m + 1) * P], self.xT[:, c, :],
                                     start=c == 0, stop=c == 1)
                last.then_inc(self.g_psum, 1)
                need(pe, self.f_ready, t, IT, m, ago=2)
                for c in range(2):
                    last = pe.matmul(self.ps_u[:, m % 2, :], self.s3[:, c, m * P:(m + 1) * P], self.xT[:, c, :],
                                     start=c == 0, stop=c == 1)
                last.then_inc(self.u_psum, 1)

        pe.wait_ge(self.loaded, 48)
        turn(0, first=True)
        with pe.Fori(1, self.turns) as t:
            turn(t)
        outputs(self.turns - 1, 0)

    def scalar(self, act):
        with act.Fori(0, self.turns) as t:
            need(act, self.xT_psum, t, 1, 0, ago=1)
            act.activation(self.x[:, :, :], self.x1[:, bass.ds((t + self.batch0) * J, J), :], ACT.Copy)\
               .then_inc(self.x_ready, 1)
            need(act, self.xT_psum, t, 1, 0)
            need(act, self.u_psum, t, IT, 0, ago=1)
            act.activation(self.xT[:, :, :], self.ps_t[0:CH, :, :], ACT.Copy).then_inc(self.xT_ready, 1)
            for m in range(IT):
                need(act, self.g_psum, t, IT, m)
                need(act, self.f_ready, t, IT, m, ago=2)
                act.activation(self.gate[:, m % 2, :], self.ps_g[:, m % 2, :], ACT.Silu).then_inc(self.g_ready, 1)


def norm_and_router(kit, a, x1, logits):
    nc = kit.nc
    with kit.phase() as ctx:
        sb, ps = tile_maker(nc, ctx), psum_maker(nc, ctx)
        wr = sb("wr", [CH, 2, E8])
        stats = sb("e_stats", [P, U, J, 6])
        mv = sb("e_mv", [P, U, J, 2])
        var_eps = sb("e_var_eps", [P, U, J])
        rstd = sb("e_rstd", [P, U, J])
        xn = sb("e_xn", [P, U, J, C])
        xT = sb("e_xT", [CH, U, 2, T])
        ps_t = ps("e_ps_t", [P, U, 2, T])
        ps_l = ps("e_ps_l", [P, U, T])
        names = "var_ready rstd_ready xn_ready x1_kept xT_psum xT_ready logit_psum logit_read"
        s = {n: kit.sem("e_" + n) for n in names.split()}
        loaded = kit.sem("e_loaded")
        block = ctx.enter_context(nc.Block())

        @block.sync
        def _(sp):
            for x in s.values():
                sp.sem_inc(x, U)
            sp.dma_start(wr[:, :, :], a["wr"]).then_inc(loaded, 16)

        @block.gpsimd
        def _(pool):
            with pool.Fori(0, TURNS) as t:
                for u in range(U):
                    need(pool, s["var_ready"], t, U, u)
                    ln_rstd(kit, pool, rstd[:, u, :], var_eps[:, u, :]).then_inc(s["rstd_ready"], 1)
                for u in range(U):
                    need(pool, s["xn_ready"], t, U, u)
                    kit.apart(pool)
                    pool.tensor_copy(x1[:, bass.ds(t * (U * J) + u * J, J), :], xn[:, u]).then_inc(s["x1_kept"], 1)

        @block.vector
        def _(dve):
            with dve.Fori(0, TURNS) as t:
                for u in range(U):
                    dve.drain()
                    ln_stats(dve, kit.h[:, bass.ds(t * (U * J) + u * J, J), :], stats[:, u], mv[:, u],
                             var_eps[:, u], 1e-5).then_inc(s["var_ready"], 1)
                for u in range(U):
                    need(dve, s["rstd_ready"], t, U, u)
                    need(dve, s["xT_psum"], t, U, u, ago=U)
                    need(dve, s["x1_kept"], t, U, u, ago=U)
                    ln_apply(dve, xn[:, u], kit.h[:, bass.ds(t * (U * J) + u * J, J), :], mv[:, u],
                             rstd[:, u]).then_inc(s["xn_ready"], 1)
                for u in range(U):
                    need(dve, s["logit_psum"], t, U, u)
                    dve.tensor_copy(logits[:, bass.ds(t * (U * J) + u * J, J), :],
                                    ps_l[:, u, 0:J * E8].rearrange("p (j e) -> p j e", j=J)).then_inc(s["logit_read"], 1)

        @block.tensor
        def _(pe):
            pe.wait_ge(loaded, 16)
            with pe.Fori(0, TURNS) as t:
                for u in range(U):
                    need(pe, s["xn_ready"], t, U, u)
                    need(pe, s["xT_ready"], t, U, u, ago=U)
                    for j in range(J):
                        for c in range(2):
                            last = pe.transpose(ps_t[0:CH, u, c, j * P:(j + 1) * P], xn[:, u, j, c * CH:(c + 1) * CH],
                                                kit.ident[:, :])
                    last.then_inc(s["xT_psum"], 1)
                for u in range(U):
                    need(pe, s["xT_ready"], t, U, u)
                    need(pe, s["logit_read"], t, U, u, ago=U)
                    for j in range(J):
                        for c in range(2):
                            last = pe.matmul(ps_l[:, u, j * E8:(j + 1) * E8], xT[:, u, c, j * P:(j + 1) * P],
                                             wr[:, c, :], start=c == 0, stop=c == 1)
                    last.then_inc(s["logit_psum"], 1)

        @block.scalar
        def _(act):
            with act.Fori(0, TURNS) as t:
                for u in range(U):
                    need(act, s["xT_psum"], t, U, u)
                    need(act, s["logit_psum"], t, U, u, ago=U)
                    act.activation(xT[:, u], ps_t[0:CH, u, :, :], ACT.Copy).then_inc(s["xT_ready"], 1)


def choose_slots(kit, logits, weight, slot):
    nc = kit.nc
    with kit.phase() as ctx:
        sb, ps = tile_maker(nc, ctx), psum_maker(nc, ctx)
        V = [P, NB, E8]
        probs, probs2, mark8, rank8 = sb("r_probs", V), sb("r_probs2", V), sb("r_mark8", V), sb("r_rank8", V)
        hot = [sb("r_hot0", V), sb("r_hot1", V)]
        score = sb("r_score", V)
        order = sb("order", [P, E8])
        peak = sb("r_peak", [P, 2, NB])
        mass = sb("r_mass", [P, NB])
        slot_f = sb("slot_f", [P, 2, NB])
        rows = sb("r_rows", [P, 2, P])
        mark = sb("r_mark", [P, 2, P])
        tie = sb("r_tie", [P, 2, P])
        rank = sb("r_rank", [P, 2, P])
        ones = sb("r_ones", [P, P])
        same = sb("same", [P, P])
        before = sb("before", [P, P])
        hotT = sb("hotT", [E8, P])
        first_i = sb("first_i", [E8, 1], I32)
        first_f = sb("first_f", [E8, 1])
        first_slot = sb("first_slot", [P, 1])
        bits = sb("r_bits", [P, 1], I32)
        cand = sb("r_cand", [P, 1], I32)
        bit = sb("r_bit", [P, 1], I32)
        keep = sb("r_keep", [P, 1], I32)
        count = sb("r_count", [P, 1])
        room = sb("r_room", [P, 1])
        offset = sb("r_offset", [P, 2])
        ps_c = ps("r_ps_c", [P, 512])
        ps_r = ps("r_ps_r", [P, 2, P])
        ps_k = ps("r_ps_k", [P, 512])
        made, made_f, same_psum, same_ready, before_ready, shifted, exp_ready = kit.sems(
            "r_made r_made_f r_same_psum r_same_ready r_before_ready r_shifted r_exp_ready")
        score_ready, rows_psum, counted, total_ready, more_counted, more_total, slots_ready, slots_psum = kit.sems(
            "r_score_ready r_rows_psum r_counted r_total_ready r_more_counted r_more_total r_slots_ready r_slots_psum")
        block = ctx.enter_context(nc.Block())

        @block.gpsimd
        def _(pool):
            for e in range(E8):
                pool.memset(order[:, e:e + 1], float(E8 - e))
            pool.memset(ones[:, :], 1.0)
            pool.memset(hotT[:, :], 0.0).then_inc(made, 1)
            pool.wait_ge(made, 1)
            pool.affine_select(out=hotT[:, :].rearrange("e (b f) -> e b f", f=E8),
                               in_=hotT[:, :].rearrange("e (b f) -> e b f", f=E8), compare_op=ALU.not_equal,
                               fill=1.0, base=0, pattern=[[0, LO], [-1, E8]], channel_multiplier=1)
            pool.iota(first_i[:, :], pattern=[[0, 1]], base=-1, channel_multiplier=CAP).then_inc(made, 1)
            pool.wait_ge(same_ready, 1)
            pool.affine_select(out=before[:, :], in_=same[:, :], compare_op=ALU.is_gt, fill=0.0, base=0,
                               pattern=[[1, P]], channel_multiplier=-1).then_inc(before_ready, 1)

        @block.vector
        def _(dve):
            dve.wait_ge(made, 2)
            dve.tensor_copy(first_f[:, :], first_i[:, :]).then_inc(made_f, 1)
            dve.wait_ge(same_psum, 1)
            dve.tensor_copy(same[:, :], ps_c[:, 0:P])
            dve.tensor_copy(first_slot[:, :], ps_c[:, P:P + 1]).then_inc(same_ready, 1)
            dve.tensor_reduce(peak[:, 0, :], logits[:, :, :], AX_X, ALU.max)
            dve.drain()
            dve.tensor_tensor(probs[:, :, :], logits[:, :, :], bc(peak[:, 0, :], E8), ALU.subtract).then_inc(shifted, 1)
            dve.wait_ge(exp_ready, 1)
            dve.tensor_reduce(mass[:, :], probs[:, :, :], AX_X, ALU.add)
            dve.drain()
            dve.reciprocal(mass[:, :], mass[:, :])
            dve.drain()
            dve.tensor_tensor(probs[:, :, :], probs[:, :, :], bc(mass[:, :], E8), ALU.mult)
            dve.drain()
            for k, p in enumerate((probs, probs2)):
                dve.tensor_reduce(peak[:, k, :], p[:, :, :], AX_X, ALU.max)
                dve.drain()
                dve.tensor_tensor(mark8[:, :, :], p[:, :, :], bc(peak[:, k, :], E8), ALU.is_equal)
                dve.drain()
                dve.tensor_tensor(mark8[:, :, :], mark8[:, :, :], order[:, :].unsqueeze(1).broadcast_to(V), ALU.mult)
                dve.drain()
                dve.tensor_reduce(mass[:, :], mark8[:, :, :], AX_X, ALU.max)
                dve.drain()
                dve.tensor_tensor(hot[k][:, :, :], mark8[:, :, :], bc(mass[:, :], E8), ALU.is_equal)
                dve.drain()
                if k == 0:
                    dve.scalar_tensor_tensor(out=probs2[:, :, :], in0=hot[0][:, :, :], scalar=-4.0, in1=probs[:, :, :],
                                             op0=ALU.mult, op1=ALU.add)
                    dve.drain()
            dve.tensor_tensor(mass[:, :], peak[:, 0, :], peak[:, 1, :], ALU.add)
            dve.drain()
            dve.tensor_scalar(mass[:, :], mass[:, :], 1e-9, None, ALU.max)
            dve.drain()
            dve.reciprocal(mass[:, :], mass[:, :])
            dve.drain()
            dve.tensor_tensor(weight[:, :, :], peak[:, :, :], mass[:, :].unsqueeze(1).broadcast_to([P, 2, NB]), ALU.mult)
            dve.drain()
            dve.tensor_tensor(score[:, :, :], hot[0][:, :, :], bc(weight[:, 0, :], E8), ALU.mult)
            dve.tensor_tensor(mark8[:, :, :], hot[1][:, :, :], bc(weight[:, 1, :], E8), ALU.mult)
            dve.tensor_tensor(rank8[:, :, :], hot[0][:, :, :], hot[1][:, :, :], ALU.add)
            dve.drain()
            dve.tensor_tensor(score[:, :, :], score[:, :, :], mark8[:, :, :], ALU.add)
            dve.drain()
            dve.scalar_tensor_tensor(out=score[:, :, :], in0=rank8[:, :, :], scalar=-1.0, in1=score[:, :, :],
                                     op0=ALU.add, op1=ALU.add).then_inc(score_ready, 1)
            dve.wait_ge(rows_psum, 1)
            dve.tensor_copy(rows[:, :, :], ps_r[:, :, :])
            dve.drain()

            def total(dve, step, last):
                last.then_inc(counted, 1)
                dve.wait_ge(total_ready, step + 1)
                return ps_k[:, 0:1]

            flat = rows[:, :, :].rearrange("p a b -> p (a b)")
            mark_flat = mark[:, :, :].rearrange("p a b -> p (a b)")
            kth_largest(dve, P, flat, bits, cand, bit, count, keep, mark_flat, CAP, total)
            kth = bits[:, :].bitcast(F32)
            dve.tensor_scalar(mark_flat, flat, kth, 0.0, ALU.is_gt, ALU.add, accum_out=count[:, :])\
               .then_inc(more_counted, 1)
            dve.tensor_scalar(tie[:, :, :], rows[:, :, :], kth, None, ALU.is_equal)
            dve.wait_ge(more_total, 1)
            dve.tensor_scalar(room[:, :], ps_k[:, 1:2], -1.0, float(CAP), ALU.mult, ALU.add)

            def ranks(src, n):
                dve.drain()
                for hi in range(2):
                    last = dve.tensor_tensor_scan(rank[:, hi, :], ones[:, :], src[:, hi, :], 0.0, ALU.mult, ALU.add)
                last.then_inc(more_counted, 1)
                dve.wait_ge(more_total, n)
                dve.tensor_copy(offset[:, :], ps_k[:, 2:4])
                dve.drain()
                for hi in range(2):
                    dve.tensor_scalar(rank[:, hi, :], rank[:, hi, :], offset[:, hi:hi + 1], None, ALU.add)
                dve.drain()

            ranks(tie, 2)
            dve.scalar_tensor_tensor(out=tie[:, :, :], in0=rank[:, :, :], scalar=room[:, :], in1=tie[:, :, :],
                                     op0=ALU.is_le, op1=ALU.mult)
            dve.drain()
            dve.tensor_tensor(mark[:, :, :], mark[:, :, :], tie[:, :, :], ALU.add)
            ranks(mark, 3)
            dve.tensor_scalar(rank[:, :, :], rank[:, :, :], first_slot[:, :], -NOWHERE, ALU.add, ALU.add)
            dve.drain()
            dve.tensor_tensor(rank[:, :, :], rank[:, :, :], mark[:, :, :], ALU.mult)
            dve.drain()
            dve.tensor_scalar(rank[:, :, :], rank[:, :, :], NOWHERE, None, ALU.add).then_inc(slots_ready, 1)
            dve.wait_ge(slots_psum, 1)
            dve.tensor_copy(rank8[:, :, :], ps_r[:, :, :].rearrange("p a (b e) -> p (a b) e", e=E8))
            dve.drain()
            for k in range(2):
                dve.tensor_tensor(mark8[:, :, :], hot[k][:, :, :], rank8[:, :, :], ALU.mult)
                dve.drain()
                dve.tensor_reduce(slot_f[:, k, :], mark8[:, :, :], AX_X, ALU.add)
                dve.drain()
            dve.tensor_copy(slot[:, :, :], slot_f[:, :, :])
            dve.scalar_tensor_tensor(out=weight[:, :, :], in0=slot_f[:, :, :], scalar=float(SLOTS), in1=weight[:, :, :],
                                     op0=ALU.is_lt, op1=ALU.mult)

        @block.tensor
        def _(pe):
            pe.wait_ge(made_f, 1)
            pe.matmul(ps_c[:, 0:P], hotT[:, :], hotT[:, :], start=True, stop=True)
            pe.matmul(ps_c[:, P:P + 1], hotT[:, :], first_f[:, :], start=True, stop=True).then_inc(same_psum, 1)
            pe.wait_ge(score_ready, 1)
            for hi in range(2):
                last = pe.transpose(ps_r[:, hi, :], score[:, hi * LO:(hi + 1) * LO, :].rearrange("p b e -> p (b e)"),
                                    kit.ident[:, :])
            last.then_inc(rows_psum, 1)
            pe.wait_ge(before_ready, 1)
            with pe.Fori(0, TOP_BIT + 1) as step:
                pe.wait_ge(counted, step + 1)
                pe.matmul(ps_k[:, 0:1], same[:, :], count[:, :], start=True, stop=True).then_inc(total_ready, 1)
            pe.wait_ge(more_counted, 1)
            pe.matmul(ps_k[:, 1:2], same[:, :], count[:, :], start=True, stop=True).then_inc(more_total, 1)
            for n in (2, 3):
                pe.wait_ge(more_counted, n)
                pe.matmul(ps_k[:, 2:3], before[:, :], rank[:, 0, P - 1:P], start=True, stop=True)
                pe.matmul(ps_k[:, 3:4], before[:, :], rank[:, 1, P - 1:P], start=True, stop=False)
                pe.matmul(ps_k[:, 3:4], same[:, :], rank[:, 0, P - 1:P], start=False, stop=True)\
                  .then_inc(more_total, 1)
            pe.wait_ge(slots_ready, 1)
            for hi in range(2):
                last = pe.transpose(ps_r[:, hi, :], rank[:, hi, :], kit.ident[:, :])
            last.then_inc(slots_psum, 1)

        @block.scalar
        def _(act):
            act.wait_ge(shifted, 1)
            act.activation(probs[:, :, :], probs[:, :, :], ACT.Exp).then_inc(exp_ready, 1)


def deal_out(kit, a, x1, slot, dealt):
    nc = kit.nc
    ZC = SLOTS // E8 * C // P
    with kit.phase() as ctx:
        sb = tile_maker(nc, ctx)
        zeros = sb("zeros", [P, ZC])
        rows = sb("s_rows", [P, U, J, C])
        where = sb("s_where", [P, U, 2, J], I32)
        zeroed, cleared, rows_ready, where_ready = kit.sems("s_zeroed s_cleared s_rows_ready s_where_ready")
        scattered = [kit.pool_dma_sem(f"s_scattered{u}") for u in range(U)]
        shared = SharedExpert(kit, a, x1, ctx, 0)
        block = ctx.enter_context(nc.Block())

        @block.sync
        def _(sp):
            shared.sync(sp)
            sp.wait_ge(zeroed, 1)
            for e in range(E8):
                sp.dma_start(dealt[e * CAP:(e + 1) * CAP, :].rearrange("(p r) c -> p (r c)", p=P), zeros[:, :])\
                  .then_inc(cleared, 16)

        @block.vector
        def _(dve):
            dve.memset(zeros[:, :], 0.0).then_inc(zeroed, 1)
            shared.vector(dve, 0, first=True)
            with dve.Fori(1, TURNS) as t:
                shared.vector(dve, t)
            shared.vector_end(dve)

        @block.tensor
        def _(pe):
            shared.tensor(pe)

        @block.scalar
        def _(act):
            shared.scalar(act)

        @block.gpsimd
        def _(pool):
            pool.wait_ge(cleared, 16 * E8)
            with pool.Fori(0, TURNS) as t:
                for u in range(U):
                    pool.tensor_copy(where[:, u], slot[:, :, bass.ds(t * (U * J) + u * J, J)]).then_inc(where_ready, 1)
                    pool.tensor_copy(rows[:, u], x1[:, bass.ds(t * (U * J) + u * J, J), :]).then_inc(rows_ready, 1)
                for u in range(U):
                    pool.wait_ge(where_ready, t * U + (u + 1))
                    pool.wait_ge(rows_ready, t * U + (u + 1))
                    kit.apart(pool)
                    for k in range(2):
                        for j in range(J):
                            pool.indirect_dma_start(
                                out=dealt, out_offset=bass.IndirectOffsetOnAxis(ap=where[:, u, k, j:j + 1], axis=0),
                                in_=rows[:, u, j, :], in_offset=None, bounds_check=SLOTS - 1, oob_is_err=False
                            ).then_inc(scattered[u], 16)
                for u in range(U):
                    pool.wait_ge(scattered[u], t * (2 * J * 16) + 2 * J * 16)
            for u in range(U):
                pool.wait_ge(scattered[u], TURNS * 2 * J * 16)


CB = 2
CHUNKS = CAP // (CB * P)
CT = CB * P


def routed_experts(kit, a, dealt, done):
    nc = kit.nc
    NC = U * CHUNKS
    with kit.phase() as ctx:
        sb, ps = tile_maker(nc, ctx), psum_maker(nc, ctx)
        w1 = sb("m_w1", [CH, U, 2, INNER])
        w3 = sb("m_w3", [CH, U, 2, INNER])
        w2 = sb("m_w2", [P, U, IT, C])
        x = sb("m_x", [P, 2, CB, C])
        xT = sb("m_xT", [CH, 2, 2, CT])
        gate = sb("m_gate", [P, 2, 2, CT])
        f = sb("m_f", [P, 2, IT, CT])
        o = sb("m_o", [P, 2, CB, C])
        ps_t = ps("m_ps_t", [CH, 2, 2, CT])
        ps_g = ps("m_ps_g", [P, 2, 2, CT])
        ps_u = ps("m_ps_u", [P, 2, 2, CT])
        ps_o = ps("m_ps_o", [P, 2, CB, 256])
        names = "xT_psum xT_ready g_psum g_ready u_psum f_ready o_psum o_ready o_free"
        s = {n: kit.sem("m_" + n) for n in names.split()}
        w_in = [kit.sem(f"m_w_in{u}") for u in range(U)]
        x_in = [kit.sem(f"m_x_in{k}") for k in range(2)]
        stored = [kit.pool_dma_sem(f"m_stored{k}") for k in range(2)]
        block = ctx.enter_context(nc.Block())
        IP = IT // 2

        @block.sync
        def _(sp):
            for v in s.values():
                sp.sem_inc(v, U)
            def load_expert(e, u):
                for dst, src in ((w1, a["w1e"]), (w3, a["w3e"]), (w2, a["w2e"])):
                    sp.dma_start(dst[:, u], src[bass.ds(e, 1)].rearrange("e p k n -> p (e k) n")).then_inc(w_in[u], 16)

            def turn(t, last=False):
                for n in range(NC):
                    u, k = n // CHUNKS, n % CHUNKS
                    if k == 1 and not (last and u == U - 1):
                        need(sp, s["o_psum"], t, NC, n, ago=2)
                        load_expert(t * U + (u + 1), (u + 1) % U)
                    need(sp, s["xT_psum"], t, NC, n, ago=2)
                    sp.dma_start(x[:, n % 2], dealt[bass.ds((t * U + u) * CAP + k * CT, CT), :].rearrange(
                        "(b p) c -> p b c", p=P)).then_inc(x_in[n % 2], 16)

            load_expert(0, 0)
            with sp.Fori(0, TURNS - 1) as t:
                turn(t)
            turn(TURNS - 1, last=True)

        @block.gpsimd
        def _(pool):
            with pool.Fori(0, TURNS) as t:
                for n in range(NC):
                    u, k = n // CHUNKS, n % CHUNKS
                    need(pool, s["o_ready"], t, NC, n)
                    pool.dma_start(done[bass.ds((t * U + u) * CAP + k * CT, CT), :].rearrange("(b p) c -> p b c", p=P),
                                   o[:, n % 2]).then_inc(stored[n % 2], 16)
                    pool.wait_ge(stored[n % 2], t * (NC // 2 * 16) + (n // 2 + 1) * 16)
                    pool.sem_inc(s["o_free"], 1)
            for k in range(2):
                pool.wait_ge(stored[k], TURNS * NC // 2 * 16)

        @block.tensor
        def _(pe):
            def transposes(t, n):
                b = n % 2
                pe.wait_ge(x_in[b], t * (NC // 2 * 16) + (n // 2 + 1) * 16)
                need(pe, s["xT_ready"], t, NC, n, ago=2)
                for r in range(CB):
                    for c in range(2):
                        last = pe.transpose(ps_t[:, b, c, r * P:(r + 1) * P], x[:, b, r, c * CH:(c + 1) * CH],
                                            kit.ident[:, :])
                last.then_inc(s["xT_psum"], 1)

            def inner(t, n):
                u, k, b = n // CHUNKS, n % CHUNKS, n % 2
                if k == 0:
                    pe.wait_ge(w_in[u], t * 48 + 48)
                need(pe, s["xT_ready"], t, NC, n)
                for i in range(IP):
                    q = n * IP + i
                    need(pe, s["g_ready"], t, NC * IP, q, ago=2)
                    for m in (2 * i, 2 * i + 1):
                        for c in range(2):
                            last = pe.matmul(ps_g[:, q % 2, m % 2, :], w1[:, u, c, m * P:(m + 1) * P],
                                             xT[:, b, c, :], start=c == 0, stop=c == 1)
                    last.then_inc(s["g_psum"], 1)
                    need(pe, s["f_ready"], t, NC * IP, q, ago=2)
                    for m in (2 * i, 2 * i + 1):
                        for c in range(2):
                            last = pe.matmul(ps_u[:, q % 2, m % 2, :], w3[:, u, c, m * P:(m + 1) * P],
                                             xT[:, b, c, :], start=c == 0, stop=c == 1)
                    last.then_inc(s["u_psum"], 1)

            def outputs(t, n):
                u, b = n // CHUNKS, n % 2
                need(pe, s["f_ready"], t, NC * IP, n * IP + IP - 1)
                need(pe, s["o_ready"], t, NC, n, ago=2)
                for r in range(CB):
                    for m in range(IT):
                        last = pe.matmul(ps_o[:, b, r, 0:C], f[:, b, m, r * P:(r + 1) * P], w2[:, u, m, :],
                                         start=m == 0, stop=m == IT - 1)
                last.then_inc(s["o_psum"], 1)

            with pe.Fori(0, TURNS) as t:
                for n in range(NC):
                    transposes(t, n)
                    if n >= 1:
                        outputs(t, n - 1)
                    inner(t, n)
                outputs(t, NC - 1)

        @block.scalar
        def _(act):
            with act.Fori(0, TURNS) as t:
                for n in range(NC):
                    b = n % 2
                    need(act, s["xT_psum"], t, NC, n)
                    need(act, s["o_psum"], t, NC, n, ago=2)
                    act.activation(xT[:, b], ps_t[:, b], ACT.Copy).then_inc(s["xT_ready"], 1)
                    for i in range(IP):
                        q = n * IP + i
                        need(act, s["g_psum"], t, NC * IP, q)
                        need(act, s["f_ready"], t, NC * IP, q, ago=2)
                        act.activation(gate[:, q % 2], ps_g[:, q % 2], ACT.Silu).then_inc(s["g_ready"], 1)

        @block.vector
        def _(dve):
            with dve.Fori(0, TURNS) as t:
                for n in range(NC):
                    b = n % 2
                    need(dve, s["o_psum"], t, NC, n, ago=2)
                    for i in range(IP):
                        q = n * IP + i
                        need(dve, s["g_ready"], t, NC * IP, q)
                        need(dve, s["u_psum"], t, NC * IP, q)
                        dve.tensor_tensor(f[:, b, 2 * i:2 * i + 2, :], ps_u[:, q % 2], gate[:, q % 2], ALU.mult)\
                           .then_inc(s["f_ready"], 1)
                    need(dve, s["o_psum"], t, NC, n)
                    need(dve, s["o_free"], t, NC, n, ago=2)
                    dve.tensor_copy(o[:, b], ps_o[:, b, :, 0:C]).then_inc(s["o_ready"], 1)


def gather_and_store(kit, a, x1, weight, slot, done, out):
    nc = kit.nc
    with kit.phase() as ctx:
        sb = tile_maker(nc, ctx)
        where = sb("g_where", [P, U, 2, J], I32)
        got = sb("got", [P, U, 2, J, C])
        res = sb("res", [P, U, J, C])
        where_ready, summed = kit.sems("g_where_ready g_summed")
        gathered = [kit.pool_dma_sem(f"g_gathered{u}") for u in range(U)]
        stored = [kit.sem(f"g_stored{u}") for u in range(U)]
        shared = SharedExpert(kit, a, x1, ctx, B // 2)
        block = ctx.enter_context(nc.Block())

        @block.gpsimd
        def _(pool):
            with pool.Fori(0, TURNS) as t:
                for u in range(U):
                    need(pool, summed, t, U, u, ago=U)
                    kit.apart(pool)
                    pool.tensor_copy(where[:, u], slot[:, :, bass.ds(t * (U * J) + u * J, J)])
                    pool.memset(got[:, u], 0.0).then_inc(where_ready, 1)
                for u in range(U):
                    pool.wait_ge(where_ready, t * U + (u + 1))
                    kit.apart(pool)
                    for k in range(2):
                        for j in range(J):
                            pool.indirect_dma_start(
                                out=got[:, u, k, j, :], out_offset=None, in_=done,
                                in_offset=bass.IndirectOffsetOnAxis(ap=where[:, u, k, j:j + 1], axis=0),
                                bounds_check=SLOTS - 1, oob_is_err=False).then_inc(gathered[u], 16)

        @block.vector
        def _(dve):
            def sum_up(t, back=0):
                for u in range(U):
                    blocks = bass.ds((t - back) * (U * J) + u * J, J)
                    dve.wait_ge(gathered[u], t * (2 * J * 16) + (1 - back) * (2 * J * 16))
                    for k in range(2):
                        dve.tensor_tensor(got[:, u, k], got[:, u, k], bc(weight[:, k, blocks], C), ALU.mult)
                    dve.drain()
                    dve.tensor_tensor(got[:, u, 0], got[:, u, 0], got[:, u, 1], ALU.add)
                    dve.drain()
                    dve.wait_ge(stored[u], t * 16 + (DMA - back * 16))
                    dve.tensor_tensor(res[:, u], got[:, u, 0], kit.h[:, blocks, :], ALU.add).then_inc(summed, 1)

            dve.sem_inc(summed, U)
            shared.vector(dve, 0, first=True)
            with dve.Fori(1, TURNS) as t:
                shared.vector(dve, t)
                sum_up(t, back=1)
            shared.vector_end(dve)
            sum_up(TURNS - 1)

        @block.tensor
        def _(pe):
            shared.tensor(pe)

        @block.scalar
        def _(act):
            shared.scalar(act)

        @block.sync
        def _(sp):
            for u in range(U):
                sp.sem_inc(stored[u], DMA)
            shared.sync(sp)
            with sp.Fori(0, TURNS) as t:
                for u in range(U):
                    need(sp, summed, t, U, u)
                    sp.dma_start(out[:, bass.ds(t * (U * J) + u * J, J), :], res[:, u]).then_inc(stored[u], 16)
            for u in range(U):
                sp.wait_ge(stored[u], TURNS * 16 + DMA)


def store_output(kit, out):
    nc = kit.nc
    stored = kit.sem("stored")
    with nc.Block() as block:
        @block.sync
        def _(sp):
            sp.dma_start(out, kit.h[:, :, :]).then_inc(stored, 16)
            sp.wait_ge(stored, 16)


PHASES = 4


def lm_tower(nc, a, out):
    with ExitStack() as ctx:
        kit = Kit(nc, ctx)
        setup_constants(kit)
        embed_and_time_mix(kit, a)
        if PHASES > 1:
            with ExitStack() as layer:
                sb = tile_maker(nc, layer)
                x1 = sb("x1", [P, NB, C])
                bands = sb("bands", [P, 2, NB, EXPERTS0])
                route_tokens(kit, a, x1, bands)
                moe_attention_ffn(kit, a, x1, bands)
        if PHASES > 2:
            state_space_block(kit, a)
        if PHASES > 3:
            dealt = nc.dram_tensor("dealt", (SLOTS, C), F32, kind="Internal").ap()
            done = nc.dram_tensor("done", (SLOTS, C), F32, kind="Internal").ap()
            sb = tile_maker(nc, ctx)
            weight = sb("weight", [P, 2, NB])
            slot = sb("slot", [P, 2, NB], I32)
            x1 = sb("e_x1", [P, NB, C])
            with ExitStack() as layer:
                logits = tile_maker(nc, layer)("logits", [P, NB, E8])
                norm_and_router(kit, a, x1, logits)
                choose_slots(kit, logits, weight, slot)
            deal_out(kit, a, x1, slot, dealt)
            routed_experts(kit, a, dealt, done)
            gather_and_store(kit, a, x1, weight, slot, done, out)
        else:
            store_output(kit, out)


def lay_out(i):
    import numpy as np

    def col(v):
        return np.ascontiguousarray(np.asarray(v).reshape(2, CH).T)

    def rows(w):
        w = np.asarray(w)
        return np.ascontiguousarray(w.reshape(2, CH, w.shape[1]).transpose(1, 0, 2))

    w1 = np.zeros((CH + 1, 2, MLP + 3 * C), np.float32)
    w1[0:CH] = rows(np.asarray(i["L0_ffn_w1"]).T)
    w1[CH, 1] = np.asarray(i["L0_ffn_b1"])
    w2 = np.asarray(i["L0_ffn_w2"]).T
    in_proj = np.asarray(i["L1_attn_in_proj_w"]).T

    return {
        "x": np.ascontiguousarray(np.asarray(i["x"]).reshape(NB, P).T),
        "emb": np.asarray(i["L0_tok_W"]),
        "decay": col(i["L0_attn_time_decay"]),
        "first": col(i["L0_attn_time_first"]),
        "mix": np.stack([col(np.asarray(i[f"L0_attn_time_mix_{n}"]).reshape(-1)) for n in "kvr"], axis=1),
        "wkvr": np.stack([rows(np.asarray(i[f"L0_attn_W{n}"]).T) for n in "kvr"], axis=1),
        "wo": rows(np.asarray(i["L0_attn_Wo"]).T),
        "w_router": rows(np.asarray(i["L0_ffn_w_router"]).T),
        "gamma1": np.asarray(i["L0_ffn_gamma1"])[None],
        "beta1": np.asarray(i["L0_ffn_beta1"])[None],
        "w1": w1,
        "w2_mlp": w2[0:MLP].reshape(FC1_TILES, P, 2, C).transpose(1, 0, 2, 3),
        "w2_att": w2[MLP:].reshape(2, CH, 2, C).transpose(1, 0, 2, 3),
        "b2": np.asarray(i["L0_ffn_b2"]).reshape(1, 2, C),
        "ln12": np.stack([np.asarray(i[f"L1_attn_{n}"]) for n in ("ln1_w", "ln1_b", "ln2_w", "ln2_b")])[None],
        "wz": rows(np.concatenate([in_proj[:, 0:DI], in_proj[:, DI + 4 * P:]], axis=1)),
        "wx": rows(in_proj[:, DI:DI + 4 * P]),
        "conv_w": np.asarray(i["L1_attn_conv_w"]).reshape(4, P, TAPS).transpose(1, 0, 2),
        "conv_b": np.asarray(i["L1_attn_conv_b"]).reshape(4, P).T,
        "dt_bias": np.asarray(i["L1_attn_dt_bias"])[None],
        "a_log": np.asarray(i["L1_attn_A_log"])[None],
        "d_skip": np.asarray(i["L1_attn_D_skip"])[None],
        "norm_w": np.asarray(i["L1_attn_ssm_norm_w"])[None],
        "w_out": np.asarray(i["L1_attn_out_proj_w"]).T.reshape(KD, P, C).transpose(1, 0, 2),
        "wf1": rows(np.asarray(i["L1_attn_fc1_w"]).T),
        "wr": rows(np.asarray(i["L1_ffn_Wr"])),
        "s1": rows(np.asarray(i["L1_ffn_s1"])),
        "s3": rows(np.asarray(i["L1_ffn_s3"])),
        "s2": np.asarray(i["L1_ffn_s2"]).reshape(IT, P, C).transpose(1, 0, 2),
        "w1e": np.asarray(i["L1_ffn_w1"]).reshape(E8, 2, CH, INNER).transpose(0, 2, 1, 3),
        "w3e": np.asarray(i["L1_ffn_w3"]).reshape(E8, 2, CH, INNER).transpose(0, 2, 1, 3),
        "w2e": np.asarray(i["L1_ffn_w2"]).reshape(E8, IT, P, C).transpose(0, 2, 1, 3),
        "wf2": np.asarray(i["L1_attn_fc2_w"]).T.reshape(KD, P, C).transpose(1, 0, 2),
    }


def kernel(**inputs):
    import numpy as np
    import concourse.bacc as bacc
    from concourse.bass_utils import run_bass_kernel_spmd

    nc = bacc.Bacc("TRN2", target_bir_lowering=False, num_devices=1)
    arrays = {f"in_{n}": np.ascontiguousarray(v) for n, v in lay_out(inputs).items()}
    aps = {n[3:]: nc.dram_tensor(n, v.shape, mybir.dt.from_np(v.dtype), kind="ExternalInput").ap()
           for n, v in arrays.items()}
    out = nc.dram_tensor("out", (N, C), F32, kind="ExternalOutput").ap()
    lm_tower(nc, aps, out.rearrange("(b p) c -> p b c", p=P))
    got = run_bass_kernel_spmd(nc, [arrays], core_ids=[0]).results[0]["out"]
    return got.reshape(B, T, C)
```
